# Optimizing a Trainium2 kernel written in Bass

```python
import numpy as np
import jax
import jax.numpy as jnp

def _softmax(x, axis=-1):
    return jax.nn.softmax(x, axis=axis)

def _gelu(x):
    return jax.nn.gelu(x, approximate=True)

def _silu(x):
    return jax.nn.silu(x)

def _sigmoid(x):
    return jax.nn.sigmoid(x)

def _layernorm(x, axis=-1, eps=1e-05):
    m = jnp.mean(x, axis=axis, keepdims=True)
    v = jnp.var(x, axis=axis, keepdims=True)
    return (x - m) / jnp.sqrt(v + eps)

def _scatter_add(tgt, idx, src, axis=0):
    return tgt.at[idx].add(src)

def _segment_sum(src, seg, n):
    return jax.ops.segment_sum(src, seg, n)
kernel_name = 'mk_gnn_resnorm_d2_gnn_r8_834581'

def setup_inputs(seed: int=0):
    np.random.seed(seed)
    _w = jnp.asarray

    def _rec_inputs():
        import jax
        import jax.numpy as jnp
        _gk = jax.random.key(seed)
        x = -0.0001006 + 1 * jax.random.normal(jax.random.fold_in(_gk, 1), (12500, 96), jnp.float32)
        src = jax.random.randint(jax.random.fold_in(_gk, 2), (400000,), 0, 12500, jnp.int32)
        dst = jax.random.randint(jax.random.fold_in(_gk, 3), (400000,), 0, 12500, jnp.int32)
        _o = jnp.argsort(dst, stable=True)
        src = src[_o]
        dst = dst[_o]
        edge_attr_4 = 0.000714719 + 1.00021 * jax.random.normal(jax.random.fold_in(_gk, 12), (400000, 4), jnp.float32)
        edge_attr_96 = jax.random.uniform(jax.random.fold_in(_gk, 13), (400000, 96), jnp.float32, 0.0, 1.11111)
        return (x, src, dst, edge_attr_4, edge_attr_96)
    x, src, dst, edge_attr_4, edge_attr_96 = _rec_inputs()

    def _L0_gnn_setup():
        import jax, jax.numpy as jnp
        import numpy as np
        EPS = 1e-05

        def _mlp(h, W, b, gamma, beta):
            h = jax.nn.relu(h @ W + b)
            mu = jnp.mean(h, axis=0)
            var = jnp.mean(jnp.square(h - mu), axis=0)
            return gamma * (h - mu) * jax.lax.rsqrt(var + EPS) + beta
        key = jax.random.key(seed)
        ks = jax.random.split(key, 10)
        N, E, C_in, C_out, E_dim = (6250, 100000, 96, 96, 4)
        x = jax.random.normal(ks[0], (N, C_in), dtype=jnp.float32)
        edge_index = jax.random.randint(ks[1], (2, E), 0, N, dtype=jnp.int64)
        edge_attr = jax.random.normal(ks[2], (E, E_dim), dtype=jnp.float32)
        s = lambda fan_in: 1.0 / np.sqrt(fan_in)
        W_node = jax.random.uniform(ks[3], (C_in, C_out), jnp.float32, -s(C_in), s(C_in))
        b_node = jnp.zeros((C_out,), jnp.float32)
        g_node = jnp.ones((C_out,), jnp.float32)
        beta_node = jnp.zeros((C_out,), jnp.float32)
        W_edge = jax.random.uniform(ks[4], (E_dim, C_out), jnp.float32, -s(E_dim), s(E_dim))
        b_edge = jnp.zeros((C_out,), jnp.float32)
        g_edge = jnp.ones((C_out,), jnp.float32)
        beta_edge = jnp.zeros((C_out,), jnp.float32)
        M_in = 2 * C_in + C_out
        W_msg = jax.random.uniform(ks[5], (M_in, C_out), jnp.float32, -s(M_in), s(M_in))
        b_msg = jnp.zeros((C_out,), jnp.float32)
        g_msg = jnp.ones((C_out,), jnp.float32)
        beta_msg = jnp.zeros((C_out,), jnp.float32)
        return dict(x=x, edge_index=edge_index, edge_attr=edge_attr, W_node=W_node, b_node=b_node, g_node=g_node, beta_node=beta_node, W_edge=W_edge, b_edge=b_edge, g_edge=g_edge, beta_edge=beta_edge, W_msg=W_msg, b_msg=b_msg, g_msg=g_msg, beta_msg=beta_msg)
    _L0_gnn_all = _L0_gnn_setup()
    _L0_gnn_in = {k: v for k, v in _L0_gnn_all.items() if k in ('W_node', 'b_node', 'g_node', 'beta_node', 'W_edge', 'b_edge', 'g_edge', 'beta_edge', 'W_msg', 'b_msg', 'g_msg', 'beta_msg')}
    del _L0_gnn_all

    def _L1_gnn_setup():
        import jax, jax.numpy as jnp
        import numpy as np
        N_NODES = 6250
        N_EDGES = 100000
        D = 96
        EDGE_DROP = 0.1
        key = jax.random.key(seed)
        ks = jax.random.split(key, 12)
        d2 = 2 * D
        s1 = 1.0 / np.sqrt(d2)
        s2 = 1.0 / np.sqrt(D)
        h = jax.random.normal(ks[0], (N_NODES, D), dtype=jnp.float32)
        src = jax.random.randint(ks[1], (N_EDGES,), 0, N_NODES, dtype=jnp.int32)
        dst = jax.random.randint(ks[2], (N_EDGES,), 0, N_NODES, dtype=jnp.int32)
        Wm1 = jax.random.uniform(ks[3], (d2, D), jnp.float32, -s1, s1)
        bm1 = jnp.zeros((D,), jnp.float32)
        Wm2 = jax.random.uniform(ks[4], (D, D), jnp.float32, -s2, s2)
        bm2 = jnp.zeros((D,), jnp.float32)
        Wu1 = jax.random.uniform(ks[5], (d2, D), jnp.float32, -s1, s1)
        bu1 = jnp.zeros((D,), jnp.float32)
        Wu2 = jax.random.uniform(ks[6], (D, D), jnp.float32, -s2, s2)
        bu2 = jnp.zeros((D,), jnp.float32)
        keep = 1.0 - EDGE_DROP
        drop_mask = (jax.random.uniform(ks[7], (N_EDGES, D)) < keep).astype(jnp.float32) / keep
        return {'h': h, 'Wm1': Wm1, 'bm1': bm1, 'Wm2': Wm2, 'bm2': bm2, 'Wu1': Wu1, 'bu1': bu1, 'Wu2': Wu2, 'bu2': bu2, 'drop_mask': drop_mask, 'src': src, 'dst': dst}
    _L1_gnn_all = _L1_gnn_setup()
    _L1_gnn_in = {k: v for k, v in _L1_gnn_all.items() if k in ('Wm1', 'bm1', 'Wm2', 'bm2', 'Wu1', 'bu1', 'Wu2', 'bu2')}
    del _L1_gnn_all
    return {'x': x, 'src': src, 'dst': dst, 'edge_attr_4': edge_attr_4, 'edge_attr_96': edge_attr_96, 'L0_gnn_W_node': _L0_gnn_in['W_node'], 'L0_gnn_b_node': _L0_gnn_in['b_node'], 'L0_gnn_g_node': _L0_gnn_in['g_node'], 'L0_gnn_beta_node': _L0_gnn_in['beta_node'], 'L0_gnn_W_edge': _L0_gnn_in['W_edge'], 'L0_gnn_b_edge': _L0_gnn_in['b_edge'], 'L0_gnn_g_edge': _L0_gnn_in['g_edge'], 'L0_gnn_beta_edge': _L0_gnn_in['beta_edge'], 'L0_gnn_W_msg': _L0_gnn_in['W_msg'], 'L0_gnn_b_msg': _L0_gnn_in['b_msg'], 'L0_gnn_g_msg': _L0_gnn_in['g_msg'], 'L0_gnn_beta_msg': _L0_gnn_in['beta_msg'], 'L1_gnn_Wm1': _L1_gnn_in['Wm1'], 'L1_gnn_bm1': _L1_gnn_in['bm1'], 'L1_gnn_Wm2': _L1_gnn_in['Wm2'], 'L1_gnn_bm2': _L1_gnn_in['bm2'], 'L1_gnn_Wu1': _L1_gnn_in['Wu1'], 'L1_gnn_bu1': _L1_gnn_in['bu1'], 'L1_gnn_Wu2': _L1_gnn_in['Wu2'], 'L1_gnn_bu2': _L1_gnn_in['bu2']}

def reference(x, src, dst, edge_attr_4, edge_attr_96, L0_gnn_W_node, L0_gnn_b_node, L0_gnn_g_node, L0_gnn_beta_node, L0_gnn_W_edge, L0_gnn_b_edge, L0_gnn_g_edge, L0_gnn_beta_edge, L0_gnn_W_msg, L0_gnn_b_msg, L0_gnn_g_msg, L0_gnn_beta_msg, L1_gnn_Wm1, L1_gnn_bm1, L1_gnn_Wm2, L1_gnn_bm2, L1_gnn_Wu1, L1_gnn_bu1, L1_gnn_Wu2, L1_gnn_bu2):
    import jax
    import jax.numpy as jnp

    def _L0_gnn_ref(x, edge_index, edge_attr, W_node, b_node, g_node, beta_node, W_edge, b_edge, g_edge, beta_edge, W_msg, b_msg, g_msg, beta_msg):
        import jax, jax.numpy as jnp
        import numpy as np
        EPS = 1e-05

        def _mlp(h, W, b, gamma, beta):
            h = jax.nn.relu(h @ W + b)
            mu = jnp.mean(h, axis=0)
            var = jnp.mean(jnp.square(h - mu), axis=0)
            return gamma * (h - mu) * jax.lax.rsqrt(var + EPS) + beta
        node_feat = _mlp(x, W_node, b_node, g_node, beta_node)
        edge_feat = _mlp(edge_attr, W_edge, b_edge, g_edge, beta_edge)
        row, col = (edge_index[0], edge_index[1])
        message = jnp.concatenate([x[row], x[col], edge_feat], axis=1)
        message = _mlp(message, W_msg, b_msg, g_msg, beta_msg)
        agg = jax.ops.segment_sum(message, col, num_segments=node_feat.shape[0])
        return agg + node_feat

    def _L1_gnn_ref(h, Wm1, bm1, Wm2, bm2, Wu1, bu1, Wu2, bu2, drop_mask, src, dst):
        import jax, jax.numpy as jnp
        import numpy as np
        N_NODES = 6250
        N_EDGES = 100000
        D = 96
        EDGE_DROP = 0.1
        n = h.shape[0]
        e = jnp.concatenate([h[src], h[dst]], axis=-1)
        e = jax.nn.relu(e @ Wm1 + bm1) @ Wm2 + bm2
        e = e * drop_mask
        m = jax.ops.segment_sum(e, dst, num_segments=n)
        z = jnp.concatenate([h, m], axis=-1)
        h_new = jax.nn.relu(z @ Wu1 + bu1) @ Wu2 + bu2
        return h_new
    edge_index = jnp.stack([src, dst])
    x = _layernorm(x + _L0_gnn_ref(x, edge_index, edge_attr_4, L0_gnn_W_node, L0_gnn_b_node, L0_gnn_g_node, L0_gnn_beta_node, L0_gnn_W_edge, L0_gnn_b_edge, L0_gnn_g_edge, L0_gnn_beta_edge, L0_gnn_W_msg, L0_gnn_b_msg, L0_gnn_g_msg, L0_gnn_beta_msg), axis=-1)
    x = _layernorm(x + _L1_gnn_ref(x, L1_gnn_Wm1, L1_gnn_bm1, L1_gnn_Wm2, L1_gnn_bm2, L1_gnn_Wu1, L1_gnn_bu1, L1_gnn_Wu2, L1_gnn_bu2, edge_attr_96, src, dst), axis=-1)
    return x

_drawn_inputs = setup_inputs


def setup_inputs(seed=0):
    import zlib

    import numpy as np

    out = dict(_drawn_inputs(seed))
    spreads = {'L0_gnn_b_node': (0.0, 0.8),
     'L0_gnn_g_node': (1.0, 0.6),
     'L0_gnn_beta_node': (0.0, 0.8),
     'L0_gnn_b_edge': (0.0, 0.1),
     'L0_gnn_g_edge': (1.0, 0.2),
     'L0_gnn_beta_edge': (0.0, 0.444),
     'L0_gnn_b_msg': (0.0, 0.1),
     'L0_gnn_g_msg': (1.0, 0.2),
     'L0_gnn_beta_msg': (0.0, 0.1),
     'L1_gnn_bm1': (0.0, 0.1),
     'L1_gnn_bm2': (0.0, 0.1),
     'L1_gnn_bu1': (0.0, 0.1),
     'L1_gnn_bu2': (0.0, 0.1)}
    factors = {}
    for name, (base, spread) in spreads.items():
        noise = np.random.default_rng([zlib.crc32(name.encode()), seed]).standard_normal(out[name].shape)
        drawn = base * np.exp(spread * noise) if base else spread * noise
        out[name] = jnp.asarray(drawn.astype(out[name].dtype))
    for name, factor in factors.items():
        out[name] = (out[name] * factor).astype(out[name].dtype)
    return out
```

```python
import concourse.bass as bass
from concourse import mybir
from contextlib import ExitStack

F32 = mybir.dt.float32
BF16 = mybir.dt.bfloat16
I32 = mybir.dt.int32
ALU = mybir.AluOpType
ACT = mybir.ActivationFunctionType
AX = mybir.AxisListType

P = 128
EPS = 1e-5


def build_gnn(nc, x, src, dst, edge4, mask, W_node, b_node, g_node, beta_node, W_edge, b_edge, g_edge,
              beta_edge, W_msg, b_msg, g_msg, beta_msg, Wm1, bm1, Wm2, bm2, Wu1, bu1, Wu2, bu2, out):
    N, C = x.shape
    E, KE = edge4.shape
    STEPS, ST = 5, 5
    TG = STEPS * ST
    GE = TG * P
    G = E // GE
    NT = 100
    NP = N // NT
    CH = 5
    NCH = NT // CH
    assert G * GE == E and NP * NT == N and NP <= P and NCH % 2 == 0
    C1 = C + 1
    STC = ST * C
    CHC = CH * C
    NR = N + P

    src_v = src.rearrange("(g p t) -> g p t", p=P, t=TG)
    dst_v = dst.rearrange("(g p t) -> p g t", p=P, t=TG)
    edge4_v = edge4.rearrange("(g p t) k -> g p (t k)", p=P, t=TG)
    mask_v = mask.rearrange("(g p t) c -> g p (t c)", p=P, t=TG)
    x_v = x.rearrange("(p j) c -> p (j c)", j=NT)
    out_v = out.rearrange("(p j) c -> p (j c)", j=NT)

    srows = [nc.dram_tensor(f"source_rows{k}", (N, C), F32, kind="Internal").ap() for k in range(2)]
    drows = [nc.dram_tensor(f"dest_rows{k}", (NR, 3 * C), BF16, kind="Internal").ap() for k in range(2)]
    sums0 = nc.dram_tensor("sums0", (NR, C1), F32, kind="Internal").ap()
    sums1 = nc.dram_tensor("sums1", (NR, C), F32, kind="Internal").ap()
    h1_dram = nc.dram_tensor("h1_rows", (N, C), F32, kind="Internal").ap()
    srows_v = [t.rearrange("(p j) c -> p (j c)", j=NT) for t in srows]
    drows_v = [t[0:N, :].rearrange("(p j) c -> p (j c)", j=NT) for t in drows]
    h1_v = h1_dram.rearrange("(p j) c -> p (j c)", j=NT)

    ctx = ExitStack()
    with ctx:
        def sb(name, shape, dt=F32):
            return ctx.enter_context(nc.sbuf_tensor(name, shape, dt))

        def sem(name):
            return ctx.enter_context(nc.semaphore(name))

        ident = sb("ident", [P, P])
        ones = sb("ones", [P, P])
        iota_i = sb("iota_i", [P, P], I32)
        iota = sb("iota", [P, P])
        zeros = sb("zeros", [P, 512])
        rel = sb("rel", [P, (G + 1) * TG])
        base_i = sb("base_i", [1, G], I32)
        base_f = sb("base_f", [1, G])
        blockmask = sb("blockmask", [TG * KE, TG])
        we_rep = sb("we_rep", [TG * KE, C])
        we_blk = sb("we_blk", [TG * KE, TG, C])
        proj_w = [sb(f"proj_w{k}", [C1, 3 * C]) for k in range(2)]
        wc = sb("wc", [C, C])
        wc1 = sb("wc1", [C1, C])
        bmsg_row = sb("bmsg_row", [C1, C])
        wm2 = sb("wm2", [C1, C])
        wu1b = sb("wu1b", [C, C])
        wu2 = sb("wu2", [C1, C])
        cols = sb("cols", [C, 8])
        stat = sb("stat", [C, 48])
        ce_lhs = sb("ce_lhs", [C, C1])
        diag = sb("diag", [C, 2, C])
        rows = sb("rows", [NP, 2, C])
        bn_edge = sb("bn_edge", [C, 2 * STEPS, 6])
        mv_group = sb("mv_group", [C, 2])
        mv_edge = sb("mv_edge", [C, G, 2])
        gram_n = sb("gram_n", [C, C1])
        gram_m = sb("gram_m", [C, C1])

        x_all = sb("x_all", [NP, NT * C])
        h_all = sb("h_all", [NP, NT * C])
        xs = [sb(f"xs{k}", [NP, CHC]) for k in range(2)]
        xT = [sb(f"xT{k}", [C1, CH * NP]) for k in range(2)]
        u_st = [sb(f"u_st{k}", [NP, CHC]) for k in range(2)]
        v_st = [sb(f"v_st{k}", [NP, CH, 3, C], BF16) for k in range(2)]
        v_r1 = [sb(f"v_r1{k}", [NP, CHC]) for k in range(2)]
        h_st = [sb(f"h_st{k}", [NP, CH, C1]) for k in range(2)]
        s_ch = [sb(f"s_ch{k}", [NP, CH, C1]) for k in range(2)]
        y_ch = [sb(f"y_ch{k}", [NP, CHC]) for k in range(2)]
        ln_bn = [sb(f"ln_bn{k}", [NP, CH, 6]) for k in range(2)]
        ln_mv = [sb(f"ln_mv{k}", [NP, CH, 2]) for k in range(2)]
        ln_rs = [sb(f"ln_rs{k}", [NP, CH]) for k in range(2)]
        ln_nb = [sb(f"ln_nb{k}", [NP, CH]) for k in range(2)]

        idx = sb("idx", [P, STEPS, ST], I32)
        grows = sb("grows", [P, STEPS, STC])
        onehot = sb("onehot", [P, STEPS, ST * P])
        relraw = onehot[:, :, :].rearrange("p s n -> p (s n)")[:, 0:G * TG].bitcast(I32)
        onehotT = sb("onehotT", [P, STEPS, ST * P], BF16)
        eas = sb("eas", [P, TG * KE])
        eaT = sb("eaT", [TG * KE, P])
        heT = sb("heT", [C1, STEPS, ST * P])
        pre = sb("pre", [P, STEPS, STC])
        hm = sb("hm", [P, STEPS, ST, C1])
        mtile = pre
        win_ld = sb("win_ld", [P, 3 * C], BF16)
        win = sb("win", [P, 3 * C], BF16)
        seg_sb = sb("seg_sb", [P, C1])

        ps = ctx.enter_context(nc.psum_tensor("ps", [P, 8, 512], F32))
        flat = ps[:, :, :].rearrange("p b n -> p (b n)")

        link_v = sem("link_v")
        const_ready = sem("const_ready")
        bias_rows = sem("bias_rows")
        zero_w = sem("zero_w")
        zero_in = sem("zero_in")
        param_in = sem("param_in")
        dst_in = sem("dst_in")
        xall_in = sem("xall_in")
        base_bc = sem("base_bc")
        base_cast = sem("base_cast")
        rel_ready = sem("rel_ready")
        we_ready = sem("we_ready")
        xs_in = [[sem(f"xs_in{k}{b}") for b in range(2)] for k in range(2)]
        xs_T = [sem(f"xs_T{k}") for k in range(2)]
        xT_ready = [sem(f"xT_ready{k}") for k in range(2)]
        proj_done = [sem(f"proj_done{k}") for k in range(2)]
        uhm_ready = [sem(f"uhm_ready{k}") for k in range(2)]
        r1_ready = [sem(f"r1_ready{k}") for k in range(2)]
        mid_ready = [sem(f"mid_ready{k}") for k in range(2)]
        low_ready = [sem(f"low_ready{k}") for k in range(2)]
        u_out = [[sem(f"u_out{k}{b}") for b in range(2)] for k in range(2)]
        v_out = [[sem(f"v_out{k}{b}") for b in range(2)] for k in range(2)]
        gram_step = sem("gram_step")
        nodegram_ready = sem("nodegram_ready")
        h_copied = sem("h_copied")
        root_wanted, root_ready = sem("root_wanted"), sem("root_ready")
        diag_ready, rows_spread, rows_ready = sem("diag_ready"), sem("rows_spread"), sem("rows_ready")
        ce_ready, ce_done, wc1_ready = sem("ce_ready"), sem("ce_done"), sem("wc1_ready")
        a_ea_in, a_eaT, a_eaT_sb, a_he, a_relu, a_bn = (sem("a_" + n) for n in
            ("ea_in", "eaT", "eaT_sb", "he", "relu", "bn"))
        a_mv, a_turn = sem("a_mv"), sem("a_turn")

        class EdgeSems:

            def __init__(self, k):
                self.rows_used = sem(f"rows_used{k}")
                self.onehot_ready = sem(f"onehot_ready{k}")
                self.onehot_used = sem(f"onehot_used{k}")
                self.T_done = sem(f"T_done{k}")
                self.T_copied = sem(f"T_copied{k}")
                self.H_relu = sem(f"H_relu{k}")
                self.P_done = sem(f"P_done{k}")
                self.win_in = sem(f"win_in{k}")
                self.win_ready = sem(f"win_ready{k}")
                self.seg_out = sem(f"seg_out{k}")
                self.added = sem(f"added{k}")
                self.turn = sem(f"turn{k}")
                if k == 0:
                    self.H_done = sem(f"H_done{k}")
                    self.h_ready = sem(f"h_ready{k}")
                    self.ld_in = sem(f"ld_in{k}")
                    self.eaT_done = sem(f"eaT_done{k}")
                    self.eaT_sb = sem(f"eaT_sb{k}")
                else:
                    self.P_out = sem(f"P_out{k}")
                    self.mask_in = [sem(f"mask_in{k}{i}") for i in range(STEPS)]
                self.idx_in = [sem(f"idx_in{k}{i}") for i in range(STEPS)]
                self.gathered = [sem(f"gathered{k}{i}") for i in range(STEPS)]

        L = (EdgeSems(0), EdgeSems(1))
        L0, L1 = L
        s_in = [sem(f"s_in{b}") for b in range(2)]
        y_scaled, y_added, z_summed = sem("y_scaled"), sem("y_added"), sem("z_summed")
        ln_own = [sem("ln_" + n) for n in ("bnd", "turn", "agg", "inv")]
        g_own = [sem("g_" + n) for n in ("bnd", "turn", "agg", "inv")]
        ln_y, ln_sq, ln_root, ln_c, ln_done = (sem("ln_" + n) for n in ("y", "sq", "root", "c", "done"))
        h1_out = [sem(f"h1_out{b}") for b in range(2)]
        f_in = [sem(f"f_in{b}") for b in range(2)]
        f_T, f_mT, f_z, f_zr, f_zT, f_zT_sb, f_o = (sem("f_" + n) for n in ("T", "mT", "z", "zr", "zT", "zT_sb", "o"))
        g_y, g_sq, g_root, g_c, g_done = (sem("g_" + n) for n in ("y", "sq", "root", "c", "done"))
        o_out = [sem(f"o_out{b}") for b in range(2)]

        VAR, ROOT, INV = 30, 31, 32
        CR = 2
        N_ZERO = 2 + sum(-(-w // 512) + 1 for w in (NT * C1, NT * C))
        N_CONST = 10
        PARAMS = []
        PARAMS += [(proj_w[0][0:C, 0:C], W_msg[0:C, :]), (proj_w[0][0:C, C:2 * C], W_msg[C:2 * C, :]),
                   (proj_w[0][0:C, 2 * C:3 * C], W_node), (proj_w[0][C:C1, 2 * C:3 * C], b_node.unsqueeze(0)),
                   (proj_w[1][0:C, 0:C], Wm1[0:C, :]), (proj_w[1][0:C, C:2 * C], Wm1[C:2 * C, :]),
                   (proj_w[1][0:C, 2 * C:3 * C], Wu1[0:C, :]), (proj_w[1][C:C1, C:2 * C], bm1.unsqueeze(0)),
                   (proj_w[1][C:C1, 2 * C:3 * C], bu1.unsqueeze(0)),
                   (wc[:, :], W_msg[2 * C:3 * C, :]), (bmsg_row[C:C1, :], b_msg.unsqueeze(0)),
                   (wm2[0:C, :], Wm2), (wm2[C:C1, :], bm2.unsqueeze(0)), (wu1b[:, :], Wu1[C:2 * C, :]),
                   (wu2[0:C, :], Wu2), (wu2[C:C1, :], bu2.unsqueeze(0))]
        PARAMS += [(cols[:, i:i + 1], v.unsqueeze(1)) for i, v in
                   enumerate((b_edge, g_edge, beta_edge, g_node, beta_node, g_msg, beta_msg))]
        BE, GEDGE, BEDGE, GN, BN, GM, BM = range(7)
        N_PARAMS = len(PARAMS) + TG

        block = ctx.enter_context(nc.Block())

        @block.sync
        def _(sp):
            with nc.allow_non_contiguous_dma(reason="columns of parameters and first destinations, once"):
                for to, of in PARAMS:
                    sp.dma_start(to, of).then_inc(param_in, 16)
                for t in range(TG):
                    sp.dma_start(we_rep[KE * t:KE * (t + 1), :], W_edge).then_inc(param_in, 16)
                first = dst.rearrange("(g e) -> g e", e=GE)[:, 0:1].rearrange("g a -> a g")
                sp.dma_start(base_i[:, :], first).then_inc(dst_in, 16)

            def store_chunk(k, i, b):
                c = 2 * i + b
                sp.wait_ge(uhm_ready[k], c + 1)
                sp.dma_start(srows_v[k][:, bass.ds(c * CHC, CHC)], u_st[b][:, :]).then_inc(u_out[k][b], 16)
                sp.wait_ge(low_ready[k], CR + c + 1)
                sp.dma_start(drows_v[k][:, bass.ds(c * 3 * CHC, 3 * CHC)],
                             v_st[b][:, :, :, :].rearrange("p a b c -> p (a b c)")).then_inc(v_out[k][b], 16)

            for b in range(2):
                sp.dma_start(xs[b][:, :], x_v[:, b * CHC:(b + 1) * CHC]).then_inc(xs_in[0][b], 16)
            sp.dma_start(relraw.rearrange("p (g t) -> p g t", t=TG), dst_v).then_inc(dst_in, 16)
            sp.dma_start(x_all[:, :], x_v).then_inc(xall_in, 16)
            sp.wait_ge(const_ready, 1)
            sp.dma_start(proj_w[0][C:C1, 0:2 * C], zeros[0:1, 0:2 * C]).then_inc(zero_w, 16)
            sp.dma_start(proj_w[1][C:C1, 0:C], zeros[0:1, 0:C]).then_inc(zero_w, 16)
            for k in range(2):
                sp.dma_start(drows[k][N:NR, :], zeros[:, 0:3 * C // 2].bitcast(BF16)).then_inc(zero_in, 16)
            for table, width in ((sums0, C1), (sums1, C)):
                whole = NT * width
                body = table[0:N, :].rearrange("(p j) c -> p (j c)", j=NT)
                for at in range(0, whole, 512):
                    n = min(512, whole - at)
                    sp.dma_start(body[:, at:at + n], zeros[0:NP, 0:n]).then_inc(zero_in, 16)
                sp.dma_start(table[N:NR, :], zeros[:, 0:width]).then_inc(zero_in, 16)
            with sp.Fori(0, NCH // 2 - 1) as i:
                for b in range(2):
                    sp.wait_ge(xs_T[0], 2 * i + b + 1)
                    sp.dma_start(xs[b][:, :], x_v[:, bass.ds((2 * i + 2 + b) * CHC, CHC)]).then_inc(xs_in[0][b], 16)
                    store_chunk(0, i, b)
            for b in range(2):
                store_chunk(0, NCH // 2 - 1, b)

            sp.dma_start(eas[:, :], edge4_v[0, :, :]).then_inc(a_ea_in, 16)
            with sp.Fori(1, G) as i:
                sp.wait_ge(a_eaT, i)
                sp.dma_start(eas[:, :], edge4_v[bass.ds(i, 1), :, :].rearrange("a p n -> (a p) n")).then_inc(a_ea_in, 16)

            def load_indices(s, i, j):
                sp.dma_start(idx[:, j, :], src_v[bass.ds(i, 1), :, j * ST:(j + 1) * ST].rearrange("a p t -> (a p) t"))\
                  .then_inc(s.idx_in[j], 16)

            def first_of(i):
                return sp.value_load(dst[bass.ds(i * GE, 1)].unsqueeze(0), min_val=0, max_val=N - 1)

            def load_window(s, k, first):
                sp.dma_start(win_ld[:, :], drows[k][bass.ds(first, P), :]).then_inc(s.win_in, 16)

            def load_attributes(i):
                sp.dma_start(eas[:, :], edge4_v[bass.ds(i, 1), :, :].rearrange("a p n -> (a p) n")).then_inc(L0.ld_in, 16)

            def load_factors(i, j):
                sp.dma_start(mtile[:, j, :], mask_v[bass.ds(i, 1), :, j * STC:(j + 1) * STC].rearrange("a p n -> (a p) n"))\
                  .then_inc(L1.mask_in[j], 16)

            def layer_loads(k):
                s = L[k]
                for j in range(STEPS):
                    load_indices(s, 0, j)
                    if k == 1:
                        load_factors(0, j)
                if k == 0:
                    sp.wait_ge(a_eaT, G)
                    load_attributes(0)
                first = first_of(0)
                for b in range(2):
                    sp.wait_ge(v_out[k][b], 16 * (NCH // 2))
                sp.wait_ge(zero_in, 16 * N_ZERO)
                load_window(s, k, first)
                with sp.Fori(1, G) as i:
                    first = first_of(i)
                    sp.wait_ge(s.win_ready, i)
                    load_window(s, k, first)
                    if k == 0:
                        sp.wait_ge(L0.eaT_done, i)
                        load_attributes(i)
                    for j in range(STEPS):
                        sp.wait_ge(s.rows_used, STEPS * (i - 1) + j + 1)
                        load_indices(s, i, j)
                        if k == 1:
                            sp.wait_ge(L1.P_out, STEPS * (i - 1) + j + 1)
                            load_factors(i, j)

            layer_loads(0)
            first = first_of(0)
            sp.wait_ge(L0.eaT_done, G)
            load_attributes(0)
            sp.wait_ge(L0.win_ready, G)
            load_window(L0, 0, first)

            sp.wait_ge(L0.added, 16 * G)
            s0v = sums0[0:N, :].rearrange("(p j) c -> p (j c)", j=NT)
            for b in range(2):
                sp.dma_start(s_ch[b][:, :, :].rearrange("p a b -> p (a b)"), s0v[:, b * CH * C1:(b + 1) * CH * C1]).then_inc(s_in[b], 16)

            def store_h1(i, b):
                c = 2 * i + b
                sp.wait_ge(ln_done, c + 1)
                sp.dma_start(h1_v[:, bass.ds(c * CHC, CHC)], xs[b][:, :]).then_inc(h1_out[b], 16)

            with sp.Fori(0, NCH // 2 - 1) as i:
                for b in range(2):
                    sp.wait_ge(ln_y, 2 * i + b + 1)
                    sp.dma_start(s_ch[b][:, :, :].rearrange("p a b -> p (a b)"),
                                 s0v[:, bass.ds((2 * i + 2 + b) * CH * C1, CH * C1)]).then_inc(s_in[b], 16)
                    store_h1(i, b)
                    store_chunk(1, i, b)
            for b in range(2):
                store_h1(NCH // 2 - 1, b)
                store_chunk(1, NCH // 2 - 1, b)

            layer_loads(1)
            first = first_of(0)
            sp.wait_ge(L1.win_ready, G)
            load_window(L1, 1, first)

            sp.wait_ge(L1.added, 16 * G)
            for b in range(2):
                sp.wait_ge(h1_out[b], 16 * (NCH // 2))
            s1v = sums1[0:N, :].rearrange("(p j) c -> p (j c)", j=NT)

            def load_final(c, b):
                sp.dma_start(xs[b][:, :], s1v[:, bass.ds(c * CHC, CHC)]).then_inc(f_in[b], 16)
                sp.dma_start(y_ch[b][:, :], h1_v[:, bass.ds(c * CHC, CHC)]).then_inc(f_in[b], 16)

            def store_final(c, b):
                sp.wait_ge(g_done, c + 1)
                sp.dma_start(out_v[:, bass.ds(c * CHC, CHC)], u_st[b][:, :]).then_inc(o_out[b], 16)

            for b in range(2):
                load_final(b, b)
            with sp.Fori(0, NCH // 2 - 1) as i:
                for b in range(2):
                    store_final(2 * i + b, b)
                    load_final(2 * i + 2 + b, b)
            for b in range(2):
                store_final(NCH - 2 + b, b)
            for b in range(2):
                sp.wait_ge(o_out[b], 16 * (NCH // 2))
                sp.wait_ge(u_out[0][b], 16 * (NCH // 2))
                sp.wait_ge(u_out[1][b], 16 * (NCH // 2))

        @block.gpsimd
        def _(pool):
            pool.memset(zeros[:, :], 0.0).then_inc(const_ready, 1)
            pool.memset(ones[:, :], 1.0).then_inc(const_ready, 1)
            pool.iota(iota_i[:, :], pattern=[[1, P]], base=0, channel_multiplier=0).then_inc(const_ready, 1)
            pool.memset(ident[:, :], 0.0).then_inc(const_ready, 1)
            pool.memset(blockmask[:, :], 1.0).then_inc(const_ready, 1)
            for b in range(2):
                pool.memset(h_st[b][:, :, C:C1], 1.0).then_inc(const_ready, 1)
            pool.memset(hm[:, :, :, C:C1], 1.0).then_inc(const_ready, 1)
            pool.memset(rel[:, G * TG:], 0.0).then_inc(const_ready, 1)
            pool.memset(ce_lhs[:, :], 0.0).then_inc(const_ready, 1)
            pool.wait_ge(const_ready, N_CONST)
            pool.affine_select(out=ident[:, :], in_=ident[:, :], compare_op=ALU.not_equal, fill=1.0, base=0,
                               pattern=[[-1, P]], channel_multiplier=1).then_inc(const_ready, 1)
            pool.affine_select(out=blockmask[:, :], in_=blockmask[:, :], compare_op=ALU.is_ge, fill=0.0, base=0,
                               pattern=[[-KE, TG]], channel_multiplier=1).then_inc(const_ready, 1)
            pool.wait_ge(const_ready, N_CONST + 2)
            pool.affine_select(out=blockmask[:, :], in_=blockmask[:, :], compare_op=ALU.is_ge, fill=0.0, base=KE - 1,
                               pattern=[[KE, TG]], channel_multiplier=-1).then_inc(const_ready, 1)

            def add_sums(k, i):
                s = L[k]
                table, width = ((sums0, C1), (sums1, C))[k]
                first = pool.value_load(dst[bass.ds(i * GE, 1)].unsqueeze(0), min_val=0, max_val=N - 1)
                pool.wait_ge(s.added, 16 * i)
                pool.wait_ge(s.seg_out, i + 1)
                pool.wait_ge(zero_in, 16 * N_ZERO)
                pool.dma_start(table[bass.ds(first, P), :], seg_sb[:, 0:width], accum_op=ALU.add).then_inc(s.added, 16)

            def gathers(k, i):
                s = L[k]
                pool.wait_ge(s.idx_in[0], 16 * i + 16)
                pool.sem_inc(s.turn, 1)
                for j in range(STEPS):
                    if j:
                        pool.wait_ge(u_out[k][1], 16 * (NCH // 2))
                        pool.wait_ge(s.idx_in[j], 16 * i + 16)
                    for t in range(ST):
                        pool.indirect_dma_start(
                            out=grows[:, j, t * C:(t + 1) * C], out_offset=None, in_=srows[k],
                            in_offset=bass.IndirectOffsetOnAxis(ap=idx[:, j, t:t + 1], axis=0)).then_inc(s.gathered[j], 16)

            for k in range(2):
                for b in range(2):
                    pool.wait_ge(u_out[k][b], 16 * (NCH // 2))
                gathers(k, 0)
                with pool.Fori(1, G) as i:
                    gathers(k, i)
                    add_sums(k, i - 1)
                add_sums(k, G - 1)

        @block.tensor
        def _(pe):
            pe.wait_ge(const_ready, N_CONST + 3)
            pe.wait_ge(base_cast, 1)
            nc.tensor.matmul(ps[:, 7, 0:G], ones[0:1, 0:P], base_f[:, :], start=True, stop=True).then_inc(base_bc, 1)
            pe.wait_ge(param_in, 16 * N_PARAMS)
            pe.wait_ge(bias_rows, 1)
            pe.wait_ge(zero_w, 32)

            def transpose_chunk(k, c, b):
                for j in range(CH):
                    last = nc.tensor.transpose(flat[0:C, j * P:j * P + NP], xs[b][:, j * C:(j + 1) * C], ident[0:NP, 0:NP])
                last.then_inc(xs_T[k], 1)

            def project_chunk(k, c, b):
                for j in range(CH):
                    for m in range(3):
                        last = nc.tensor.matmul(ps[0:NP, 2 + 3 * b + m, j * C:(j + 1) * C], xT[b][:, j * NP:(j + 1) * NP],
                                                proj_w[k][:, m * C:(m + 1) * C], start=True, stop=True)
                last.then_inc(proj_done[k], 1)

            def chunk_products(k, i, b):
                c = 2 * i + b
                if k == 0:
                    pe.wait_ge(xs_in[0][b], 16 * (i + 1))
                else:
                    pe.wait_ge(ln_done, c + 1)
                pe.wait_ge(xT_ready[k], c)
                if k == 0:
                    pe.wait_ge(gram_step, c)
                transpose_chunk(k, c, b)
                pe.wait_ge(low_ready[k], c + 1)
                pe.wait_ge(xT_ready[k], c + 1)
                project_chunk(k, c, b)
                if k == 0:
                    pe.wait_ge(uhm_ready[0], c + 1)
                    for j in range(CH):
                        last = nc.tensor.matmul(ps[0:C, 1, 2 * P:2 * P + C1], h_st[b][:, j, 0:C], h_st[b][:, j, :],
                                                start=(j == 0), stop=(j == CH - 1))
                    last.then_inc(nodegram_ready, 1)

            pe.wait_ge(rel_ready, 1)
            with pe.Fori(0, NCH // 2) as i:
                for b in range(2):
                    chunk_products(0, i, b)

            def spread_rows(n):
                for m in range(n):
                    last = nc.tensor.matmul(ps[0:NP, 7, m * C:(m + 1) * C], ones[0:C, 0:NP], diag[:, m, :], start=True, stop=True)
                return last

            pe.wait_ge(diag_ready, 1)
            spread_rows(2).then_inc(rows_spread, 1)

            def attributes_T():
                return nc.tensor.transpose(ps[0:TG * KE, 1, P:2 * P], eas[:, :], ident[:, :])

            def edge_hidden(j, bank=4):
                for t in range(ST):
                    last = nc.tensor.matmul(flat[0:C, bank * 512 + t * P:bank * 512 + (t + 1) * P], we_blk[:, j * ST + t, :], eaT[:, :],
                                            start=True, stop=True)
                return last

            pe.wait_ge(we_ready, 1)
            with pe.Fori(0, G) as i:
                pe.wait_ge(a_ea_in, 16 * (i + 1))
                attributes_T().then_inc(a_eaT, 1)
                pe.wait_ge(a_eaT_sb, i + 1)
                for j in range(STEPS):
                    if j == 0:
                        pe.wait_ge(a_relu, STEPS * i)
                    else:
                        pe.wait_ge(a_relu, STEPS * i + j - 1)
                    edge_hidden(j, 2 + 2 * (j % 2)).then_inc(a_he, 1)

            pe.wait_ge(ce_ready, 1)
            nc.tensor.matmul(ps[0:C1, 7, 0:C], ce_lhs[:, :], wc[:, :], start=True, stop=True).then_inc(ce_done, 1)

            def onehot_T(j):
                for t in range(ST):
                    last = nc.tensor.transpose(flat[:, t * P:(t + 1) * P], onehot[:, j, t * P:(t + 1) * P], ident[:, :])
                return last

            def sum_step(j, width, gram):
                for t in range(ST):
                    first, final = j == 0 and t == 0, j == STEPS - 1 and t == ST - 1
                    last = nc.tensor.matmul(ps[:, 6, 0:width], onehot[:, j, t * P:(t + 1) * P], hm[:, j, t, 0:width],
                                            start=first, stop=final)
                    if gram:
                        last = nc.tensor.matmul(ps[0:C, 7, 0:C1], hm[:, j, t, 0:C], hm[:, j, t, :], start=first, stop=final)
                return last

            s = L0

            def T0(n, j):
                pe.wait_ge(s.onehot_ready, n + 1)
                pe.wait_ge(s.T_copied, n)
                onehot_T(j).then_inc(s.T_done, 1)

            def H0(n, j):
                pe.wait_ge(s.H_relu, n)
                edge_hidden(j).then_inc(s.H_done, 1)

            def EA0(i):
                pe.wait_ge(s.ld_in, 16 * (i + 1))
                attributes_T().then_inc(s.eaT_done, 1)

            def P0(n, j):
                pe.wait_ge(s.H_relu, n + 1)
                pe.wait_ge(s.T_copied, n + 1)
                pe.wait_ge(s.rows_used, n if j == 0 else n - 1)
                for t in range(ST):
                    o = ps[:, 2 + j % 2, t * C:(t + 1) * C]
                    nc.tensor.matmul(o, heT[:, j, t * P:(t + 1) * P], wc1[:, :], start=True, stop=False)
                    for m in range(3):
                        last = nc.tensor.matmul(o, onehotT[:, j, t * P:(t + 1) * P], win[:, m * C:(m + 1) * C],
                                                start=False, stop=(m == 2))
                last.then_inc(s.P_done, 1)

            def S0(n, j):
                pe.wait_ge(s.h_ready, n + 1)
                sum_step(j, C1, True).then_inc(s.onehot_used, 1)

            pe.sem_inc(s.onehot_used, STEPS)
            pe.wait_ge(wc1_ready, 1)
            EA0(0)
            pe.wait_ge(s.eaT_sb, 1)
            T0(0, 0)
            H0(0, 0)
            with pe.Fori(0, G) as i:
                for j in range(STEPS):
                    n = STEPS * i + j
                    if j == 0:
                        pe.wait_ge(s.win_ready, i + 1)
                    P0(n, j)
                    if j == 1:
                        pe.wait_ge(s.seg_out, i)
                    if j:
                        S0(n - 1, j - 1)
                    if j == STEPS - 1:
                        pe.wait_ge(s.eaT_sb, i + 2)
                    T0(n + 1, (j + 1) % STEPS)
                    H0(n + 1, (j + 1) % STEPS)
                    if j == STEPS - 2:
                        pe.wait_ge(s.T_copied, n + 2)
                        EA0(i + 1)
                S0(STEPS * i + STEPS - 1, STEPS - 1)

            pe.wait_ge(diag_ready, 2)
            spread_rows(2).then_inc(rows_spread, 1)
            with pe.Fori(0, NCH // 2) as i:
                for b in range(2):
                    chunk_products(1, i, b)

            s = L1

            def T1(n, j):
                pe.wait_ge(s.onehot_ready, n + 1)
                pe.wait_ge(s.T_copied, n)
                onehot_T(j).then_inc(s.T_done, 1)

            def X1(n, i, j):
                pe.wait_ge(s.T_copied, n + 1)
                pe.wait_ge(s.H_relu, n if j == 0 else n - 1)
                pe.wait_ge(s.gathered[j], 16 * ST * (i + 1))
                at = (2 + 2 * (j % 2)) * 512
                for t in range(ST):
                    o = flat[0:C, at + t * P:at + (t + 1) * P]
                    for m in range(3):
                        nc.tensor.matmul(o, win[:, m * C:(m + 1) * C], onehotT[:, j, t * P:(t + 1) * P],
                                         start=(m == 0), stop=False)
                    last = nc.tensor.matmul(o, grows[:, j, t * C:(t + 1) * C], ident[:, :], start=False, stop=True)
                last.then_inc(s.rows_used, 1)

            def E1(n, j):
                pe.wait_ge(s.H_relu, n + 1)
                pe.wait_ge(s.P_out, n)
                for t in range(ST):
                    last = nc.tensor.matmul(ps[:, 7, t * C:(t + 1) * C], heT[:, j, t * P:(t + 1) * P], wm2[:, :], start=True, stop=True)
                last.then_inc(s.P_done, 1)

            def S1(n, j):
                pe.wait_ge(s.P_out, n + 1)
                sum_step(j, C, False).then_inc(s.onehot_used, 1)

            pe.sem_inc(s.onehot_used, STEPS)
            T1(0, 0)
            with pe.Fori(0, G) as i:
                for j in range(STEPS):
                    n = STEPS * i + j
                    if j == 0:
                        pe.wait_ge(s.win_ready, i + 1)
                    X1(n, i, j)
                    if j:
                        E1(n - 1, j - 1)
                    if j == 2:
                        pe.wait_ge(s.seg_out, i)
                    if j > 1:
                        S1(n - 2, j - 2)
                    T1(n + 1, (j + 1) % STEPS)
                n = STEPS * i + STEPS - 1
                E1(n, STEPS - 1)
                S1(n - 1, STEPS - 2)
                S1(n, STEPS - 1)

            pe.wait_ge(L1.T_copied, STEPS * G + 1)
            def final_chunk(i, b):
                c = 2 * i + b
                pe.wait_ge(f_in[b], 32 * (i + 1))
                pe.wait_ge(f_mT, c)
                for j in range(CH):
                    last = nc.tensor.transpose(flat[0:C, j * P:j * P + NP], xs[b][:, j * C:(j + 1) * C], ident[0:NP, 0:NP])
                last.then_inc(f_T, 1)
                pe.wait_ge(f_mT, c + 1)
                pe.wait_ge(f_zr, c)
                for j in range(CH):
                    last = nc.tensor.matmul(ps[0:NP, 4, j * C:(j + 1) * C], xT[b][0:C, j * NP:(j + 1) * NP], wu1b[:, :], start=True, stop=True)
                last.then_inc(f_z, 1)
                pe.wait_ge(f_zr, c + 1)
                pe.wait_ge(f_zT_sb, c)
                for j in range(CH):
                    last = nc.tensor.transpose(flat[0:C, 2 * 512 + j * P:2 * 512 + j * P + NP], v_r1[b][:, j * C:(j + 1) * C], ident[0:NP, 0:NP])
                last.then_inc(f_zT, 1)
                pe.wait_ge(f_zT_sb, c + 1)
                pe.wait_ge(g_y, c)
                for j in range(CH):
                    last = nc.tensor.matmul(ps[0:NP, 5, j * C:(j + 1) * C], xT[b][:, j * NP:(j + 1) * NP], wu2[:, :], start=True, stop=True)
                last.then_inc(f_o, 1)

            with pe.Fori(0, NCH // 2) as i:
                for b in range(2):
                    final_chunk(i, b)

        @block.scalar
        def _(act):
            act.wait_ge(dst_in, 32)
            nc.scalar.copy(base_f[:, :], base_i[:, :]).then_inc(base_cast, 1)
            nc.scalar.copy(rel[:, 0:G * TG], relraw).then_inc(base_cast, 1)

            def copy_T(k, c, b):
                act.wait_ge(xs_T[k], c + 1)
                nc.scalar.copy(xT[b][0:C, :].rearrange("p (j n) -> p j n", j=CH),
                               flat[0:C, 0:CH * P].rearrange("p (j n) -> p j n", j=CH)[:, :, 0:NP]).then_inc(xT_ready[k], 1)

            def unload_chunk(k, i, b):
                c = 2 * i + b
                copy_T(k, c, b)
                act.wait_ge(proj_done[k], c + 1)
                act.wait_ge(u_out[k][b], 16 * i)
                act.wait_ge(v_out[k][b], 16 * i)
                nc.scalar.copy(u_st[b][:, :], ps[0:NP, 2 + 3 * b, 0:CHC])
                nc.scalar.copy(v_st[b][:, :, 0, :], ps[0:NP, 3 + 3 * b, 0:CHC].rearrange("p (a b) -> p a b", b=C))
                if k == 0:
                    act.wait_ge(nodegram_ready, c)
                    act.wait_ge(h_copied, c)
                    nc.scalar.activation(h_st[b][:, :, 0:C], ps[0:NP, 4 + 3 * b, 0:CHC].rearrange("p (a b) -> p a b", b=C),
                                         ACT.Relu).then_inc(uhm_ready[k], 1)
                else:
                    nc.scalar.copy(h_all[:, bass.ds(c * CHC, CHC)], ps[0:NP, 4 + 3 * b, 0:CHC]).then_inc(uhm_ready[k], 1)
                act.wait_ge(r1_ready[k], c + 1)
                nc.scalar.copy(v_st[b][:, :, 1, :], v_r1[b][:, :].rearrange("p (a b) -> p a b", b=C)).then_inc(mid_ready[k], 1)

            act.wait_ge(const_ready, N_CONST + 3)
            with act.Fori(0, NCH // 2) as i:
                for b in range(2):
                    unload_chunk(0, i, b)

            def coefficient_root(n):
                act.wait_ge(root_wanted, n + 1)
                nc.scalar.activation(stat[:, ROOT:ROOT + 1], stat[:, VAR:VAR + 1], ACT.Sqrt).then_inc(root_ready, 1)

            coefficient_root(0)

            def attributes_copy(done, arrived, i):
                act.wait_ge(arrived, i + 1)
                nc.scalar.copy(eaT[:, :], ps[0:TG * KE, 1, P:2 * P]).then_inc(done, 1)

            def hidden_relu(j, bank=4):
                return nc.scalar.activation(heT[0:C, j, :], flat[0:C, bank * 512:bank * 512 + ST * P], ACT.Relu,
                                            bias=cols[:, BE:BE + 1])

            with act.Fori(0, G) as i:
                attributes_copy(a_eaT_sb, a_eaT, i)
                for j in range(STEPS):
                    n = STEPS * i + j
                    act.wait_ge(a_he, n + 1)
                    act.wait_ge(a_bn, n + 1)
                    hidden_relu(j, 2 + 2 * (j % 2)).then_inc(a_relu, 1)
            coefficient_root(1)

            def copy_onehot_T(s, n, j):
                act.wait_ge(s.T_done, n + 1)
                nc.scalar.copy(onehotT[:, j, :], flat[:, 0:ST * P]).then_inc(s.T_copied, 1)

            s = L0

            def HE(n, j):
                act.wait_ge(s.H_done, n + 1)
                hidden_relu(j).then_inc(s.H_relu, 1)

            attributes_copy(s.eaT_sb, s.eaT_done, 0)
            copy_onehot_T(s, 0, 0)
            HE(0, 0)
            with act.Fori(0, G) as i:
                for j in range(STEPS):
                    n = STEPS * i + j
                    act.wait_ge(s.rows_used, n + 1)
                    nc.scalar.activation(hm[:, j, :, 0:C], pre[:, j, :].rearrange("p (a b) -> p a b", b=C), ACT.Relu)\
                      .then_inc(s.h_ready, 1)
                    copy_onehot_T(s, n + 1, (j + 1) % STEPS)
                    HE(n + 1, (j + 1) % STEPS)
                    if j == STEPS - 2:
                        attributes_copy(s.eaT_sb, s.eaT_done, i + 1)
            coefficient_root(2)

            def norm(i, b, x_t, y_t, sq, root, cc, done):
                c = 2 * i + b
                act.wait_ge(sq, c + 1)
                nc.scalar.activation(ln_rs[b][:, :], ln_mv[b][:, :, 1], ACT.Sqrt).then_inc(root, 1)
                act.wait_ge(cc, c + 1)
                for j in range(CH):
                    last = nc.scalar.activation(x_t[b][:, j * C:(j + 1) * C], y_t[b][:, j * C:(j + 1) * C], ACT.Identity,
                                                bias=ln_nb[b][:, j:j + 1], scale=ln_rs[b][:, j:j + 1])
                last.then_inc(done, 1)

            with act.Fori(0, NCH // 2) as i:
                for b in range(2):
                    act.wait_ge(h1_out[b], 16 * i)
                    norm(i, b, xs, y_ch, ln_sq, ln_root, ln_c, ln_done)
                for b in range(2):
                    unload_chunk(1, i, b)

            s = L1
            copy_onehot_T(s, 0, 0)
            with act.Fori(0, G) as i:
                for j in range(STEPS):
                    n = STEPS * i + j
                    act.wait_ge(s.rows_used, n + 1)
                    at = (2 + 2 * (j % 2)) * 512
                    nc.scalar.activation(heT[0:C, j, :], flat[0:C, at:at + ST * P], ACT.Relu).then_inc(s.H_relu, 1)
                    copy_onehot_T(s, n + 1, (j + 1) % STEPS)

            with act.Fori(0, NCH // 2) as i:
                for b in range(2):
                    c = 2 * i + b
                    act.wait_ge(f_T, c + 1)
                    nc.scalar.copy(xT[b][0:C, :].rearrange("p (j n) -> p j n", j=CH),
                                   flat[0:C, 0:CH * P].rearrange("p (j n) -> p j n", j=CH)[:, :, 0:NP]).then_inc(f_mT, 1)
                    act.wait_ge(f_zT, c + 1)
                    nc.scalar.copy(xT[b][0:C, :].rearrange("p (j n) -> p j n", j=CH),
                                   flat[0:C, 1024:1024 + CH * P].rearrange("p (j n) -> p j n", j=CH)[:, :, 0:NP]).then_inc(f_zT_sb, 1)
                    act.wait_ge(o_out[b], 16 * i)
                    norm(i, b, u_st, y_ch, g_sq, g_root, g_c, g_done)

        @block.vector
        def _(dve):
            chain = [0]

            def link(ins):
                chain[0] += 1
                ins.then_inc(link_v, 1)
                dve.wait_ge(link_v, chain[0])

            for k in range(2):
                dve.sem_inc(low_ready[k], CR)
            dve.sem_inc(a_bn, STEPS)

            for b in range(2):
                nc.vector.memset(xT[b][C:C1, :], 1.0)
            nc.vector.memset(heT[C:C1, :, :], 1.0).then_inc(bias_rows, 1)

            def col(i):
                return stat[:, i:i + 1]

            dve.wait_ge(const_ready, N_CONST + 3)
            nc.vector.tensor_copy(iota[:, :], iota_i[:, :])
            dve.wait_ge(base_cast, 2)
            dve.wait_ge(base_bc, 1)
            r3 = rel[:, 0:G * TG].rearrange("p (g t) -> p g t", t=TG)
            nc.vector.tensor_tensor(r3, r3, ps[:, 7, 0:G].unsqueeze(2).to_broadcast([P, G, TG]), ALU.subtract)\
              .then_inc(rel_ready, 1)
            dve.wait_ge(param_in, 16 * N_PARAMS)
            nc.vector.tensor_tensor(we_blk[:, :, :], we_rep[:, :].unsqueeze(1).to_broadcast([TG * KE, TG, C]),
                                    blockmask[:, :].unsqueeze(2).to_broadcast([TG * KE, TG, C]), ALU.mult).then_inc(we_ready, 1)
            link(nc.vector.memset(gram_n[:, :], 0.0))
            link(nc.vector.memset(gram_m[:, :], 0.0))

            def split_chunk(k, c, b):
                dve.wait_ge(uhm_ready[k], c + 1)
                vp = ps[0:NP, 3 + 3 * b, 0:CHC].rearrange("p (a b) -> p a b", b=C)
                r1 = v_r1[b][:, :].rearrange("p (a b) -> p a b", b=C)
                nc.vector.tensor_tensor(r1, vp, v_st[b][:, :, 0, :], ALU.subtract).then_inc(r1_ready[k], 1)

            def split_low(k, c, b):
                r1 = v_r1[b][:, :].rearrange("p (a b) -> p a b", b=C)
                dve.wait_ge(mid_ready[k], c + 1)
                nc.vector.tensor_tensor(v_st[b][:, :, 2, :], r1, v_st[b][:, :, 1, :], ALU.subtract).then_inc(low_ready[k], 1)

            with dve.Fori(0, NCH // 2) as i:
                for b in range(2):
                    c = 2 * i + b
                    split_chunk(0, c, b)
                    nc.vector.tensor_copy(h_all[:, bass.ds(c * CHC, CHC)].rearrange("p (a b) -> p a b", b=C),
                                          h_st[b][:, :, 0:C]).then_inc(h_copied, 1)
                    split_low(0, c, b)
                    dve.wait_ge(nodegram_ready, c + 1)
                    nc.vector.tensor_tensor(gram_n[:, :], gram_n[:, :], ps[0:C, 1, 2 * P:2 * P + C1], ALU.add).then_inc(gram_step, 1)

            roots = [0]

            def coefficients(mean, a, c, gamma, beta):
                nc.vector.tensor_scalar(col(VAR), col(VAR), 0.0, EPS, ALU.max, ALU.add).then_inc(root_wanted, 1)
                roots[0] += 1
                dve.wait_ge(root_ready, roots[0])
                link(nc.vector.reciprocal(col(INV), col(ROOT)))
                link(nc.vector.tensor_tensor(col(a), col(INV), cols[:, gamma:gamma + 1], ALU.mult))
                link(nc.vector.tensor_tensor(col(INV), col(a), col(mean), ALU.mult))
                link(nc.vector.tensor_tensor(col(c), cols[:, beta:beta + 1], col(INV), ALU.subtract))

            def gram_coefficients(gram, count, mean, a, c, gamma, beta):
                link(nc.vector.tensor_tensor(diag[:, 0, :], gram[:, 0:C], ident[0:C, 0:C], ALU.mult))
                link(nc.vector.reduce_sum(col(VAR), diag[:, 0, :], AX.X))
                link(nc.vector.tensor_scalar(col(VAR), col(VAR), 1.0 / count, None, ALU.mult))
                link(nc.vector.tensor_scalar(col(mean), gram[:, C:C1], 1.0 / count, None, ALU.mult))
                link(nc.vector.tensor_tensor(col(INV), col(mean), col(mean), ALU.mult))
                link(nc.vector.tensor_tensor(col(VAR), col(VAR), col(INV), ALU.subtract))
                coefficients(mean, a, c, gamma, beta)

            def spread(a, c, nth):
                link(nc.vector.tensor_scalar(diag[:, 0, :], ident[0:C, 0:C], col(a), None, ALU.mult))
                nc.vector.tensor_scalar(diag[:, 1, :], ident[0:C, 0:C], col(c), None, ALU.mult).then_inc(diag_ready, 1)
                dve.wait_ge(rows_spread, nth)
                link(nc.vector.tensor_copy(rows[:, :, :].rearrange("p a b -> p (a b)"), ps[0:NP, 7, 0:2 * C]))

            dve.wait_ge(gram_step, NCH)
            gram_coefficients(gram_n, N, 0, 1, 2, GN, BN)
            spread(1, 2, 1)
            dve.wait_ge(xall_in, 16)
            x3 = x_all[:, :].rearrange("p (j c) -> p j c", c=C)
            h3 = h_all[:, :].rearrange("p (j c) -> p j c", c=C)

            def row(m, n):
                return rows[:, m, :].unsqueeze(1).to_broadcast([NP, n, C])

            link(nc.vector.tensor_tensor(h3, h3, row(0, NT), ALU.mult))
            link(nc.vector.tensor_tensor(x_all[:, :], x_all[:, :], h_all[:, :], ALU.add))
            link(nc.vector.tensor_tensor(x3, x3, row(1, NT), ALU.add))

            with dve.Fori(0, G) as i:
                for j in range(STEPS):
                    dve.wait_ge(a_relu, STEPS * i + j + 1)
                    half = ST * P // 2
                    nc.vector.bn_stats(bn_edge[:, 2 * j, :], heT[0:C, j, 0:half])
                    nc.vector.bn_stats(bn_edge[:, 2 * j + 1, :], heT[0:C, j, half:2 * half]).then_inc(a_bn, 1)
                dve.wait_ge(a_bn, STEPS * (i + 2))
                dve.sem_inc(a_turn, 1)
                nc.vector.bn_aggr(mv_group[:, :], bn_edge[:, :, :].rearrange("p a b -> p (a b)")).then_inc(a_mv, 1)
                dve.wait_ge(a_mv, 2 * i + 1)
                nc.vector.tensor_copy(mv_edge[:, bass.ds(i, 1), :].rearrange("p a b -> p (a b)"), mv_group[:, :])\
                  .then_inc(a_mv, 1)
            dve.wait_ge(a_mv, 2 * G)
            link(nc.vector.reduce_sum(col(3), mv_edge[:, :, 0], AX.X))
            link(nc.vector.reduce_sum(col(6), mv_edge[:, :, 1], AX.X))
            link(nc.vector.tensor_scalar(col(3), col(3), 1.0 / G, None, ALU.mult))
            link(nc.vector.tensor_scalar(mv_edge[:, :, 0], mv_edge[:, :, 0], col(3), None, ALU.subtract))
            link(nc.vector.tensor_tensor(mv_edge[:, :, 1], mv_edge[:, :, 0], mv_edge[:, :, 0], ALU.mult))
            link(nc.vector.reduce_sum(col(VAR), mv_edge[:, :, 1], AX.X))
            link(nc.vector.tensor_tensor(col(VAR), col(VAR), col(6), ALU.add))
            link(nc.vector.tensor_scalar(col(VAR), col(VAR), 1.0 / G, None, ALU.mult))
            coefficients(3, 4, 5, GEDGE, BEDGE)
            link(nc.vector.tensor_scalar(wc1[0:C, :], wc[:, :], col(4), None, ALU.mult))
            nc.vector.tensor_copy(ce_lhs[:, C:C1], col(5)).then_inc(ce_ready, 1)
            dve.wait_ge(ce_done, 1)
            nc.vector.tensor_tensor(wc1[C:C1, :], ps[C:C1, 7, 0:C], bmsg_row[C:C1, :], ALU.add).then_inc(wc1_ready, 1)

            def make_onehot(s, n, j):
                dve.wait_ge(s.onehot_used, n + 1)
                nc.vector.tensor_tensor(onehot[:, j, :].rearrange("p (t w) -> p t w", w=P),
                                        iota[:, :].unsqueeze(1).to_broadcast([P, ST, P]),
                                        rel[:, bass.ds(n * ST, ST)].unsqueeze(2).to_broadcast([P, ST, P]),
                                        ALU.is_equal).then_inc(s.onehot_ready, 1)

            def copy_window(s, i):
                dve.wait_ge(s.win_in, 16 * (i + 1))
                nc.vector.tensor_copy(win[:, :], win_ld[:, :]).then_inc(s.win_ready, 1)

            def norm_stats(c, b, own, sq):
                bnd, turn, agg, _ = own
                for j in range(CH):
                    last = nc.vector.bn_stats(ln_bn[b][:, j, :], y_ch[b][:, j * C:(j + 1) * C])
                last.then_inc(bnd, 1)
                dve.wait_ge(bnd, c + 1)
                dve.sem_inc(turn, 1)
                for j in range(CH):
                    last = nc.vector.bn_aggr(ln_mv[b][:, j, :], ln_bn[b][:, j, :])
                last.then_inc(agg, 1)
                dve.wait_ge(agg, c + 1)
                nc.vector.tensor_scalar(ln_mv[b][:, :, 1], ln_mv[b][:, :, 1], EPS, None, ALU.add).then_inc(sq, 1)

            def norm_scale(c, b, own, root, ready):
                dve.wait_ge(root, c + 1)
                nc.vector.reciprocal(ln_rs[b][:, :], ln_rs[b][:, :]).then_inc(own[3], 1)
                dve.wait_ge(own[3], c + 1)
                nc.vector.scalar_tensor_tensor(ln_nb[b][:, :], ln_mv[b][:, :, 0], -1.0, ln_rs[b][:, :], ALU.mult, ALU.mult)\
                  .then_inc(ready, 1)

            def between_layers():
                with dve.Fori(0, NCH // 2) as i:
                    for b in range(2):
                        c = 2 * i + b
                        dve.wait_ge(s_in[b], 16 * (i + 1))
                        y3 = y_ch[b][:, :].rearrange("p (a b) -> p a b", b=C)
                        nc.vector.tensor_tensor(y3, s_ch[b][:, :, 0:C], row(0, CH), ALU.mult).then_inc(y_scaled, 1)
                        dve.wait_ge(y_scaled, c + 1)
                        nc.vector.tensor_tensor(y_ch[b][:, :], y_ch[b][:, :], x_all[:, bass.ds(c * CHC, CHC)], ALU.add)\
                          .then_inc(y_added, 1)
                        dve.wait_ge(y_added, c + 1)
                        for j in range(CH):
                            last = nc.vector.scalar_tensor_tensor(y3[:, j, :], rows[:, 1, :], s_ch[b][:, j, C:C1], y3[:, j, :],
                                                                  ALU.mult, ALU.add)
                        last.then_inc(ln_y, 1)
                        dve.wait_ge(ln_y, c + 1)
                        norm_stats(c, b, ln_own, ln_sq)
                    for b in range(2):
                        norm_scale(2 * i + b, b, ln_own, ln_root, ln_c)
                    for b in range(2):
                        split_chunk(1, 2 * i + b, b)
                        split_low(1, 2 * i + b, b)

            def finish():
                with dve.Fori(0, NCH // 2) as i:
                    for b in range(2):
                        c = 2 * i + b
                        dve.wait_ge(f_z, c + 1)
                        nc.vector.tensor_tensor(v_r1[b][:, :], ps[0:NP, 4, 0:CHC], h_all[:, bass.ds(c * CHC, CHC)], ALU.add)\
                          .then_inc(z_summed, 1)
                        dve.wait_ge(z_summed, c + 1)
                        nc.vector.tensor_scalar(v_r1[b][:, :], v_r1[b][:, :], 0.0, None, ALU.max).then_inc(f_zr, 1)
                        dve.wait_ge(f_o, c + 1)
                        nc.vector.tensor_tensor(y_ch[b][:, :], ps[0:NP, 5, 0:CHC], y_ch[b][:, :], ALU.add).then_inc(g_y, 1)
                        dve.wait_ge(g_y, c + 1)
                        norm_stats(c, b, g_own, g_sq)
                        norm_scale(c, b, g_own, g_root, g_c)

            for k in range(2):
                s = L[k]
                copy_window(s, 0)
                make_onehot(s, 0, 0)
                make_onehot(s, 1, 1)
                with dve.Fori(0, G) as i:
                    for j in range(STEPS):
                        n = STEPS * i + j
                        make_onehot(s, n + 2, (j + 2) % STEPS)
                        dve.wait_ge(s.P_done, n + 1)
                        if k == 0:
                            dve.wait_ge(s.gathered[j], 16 * ST * (i + 1))
                            nc.vector.tensor_tensor(pre[:, j, :], ps[:, 2 + j % 2, 0:STC], grows[:, j, :], ALU.add)\
                              .then_inc(s.rows_used, 1)
                        else:
                            dve.wait_ge(s.mask_in[j], 16 * (i + 1))
                            nc.vector.tensor_tensor(hm[:, j, :, 0:C], ps[:, 7, 0:STC].rearrange("p (a b) -> p a b", b=C),
                                                    mtile[:, j, :].rearrange("p (a b) -> p a b", b=C), ALU.mult)\
                              .then_inc(s.P_out, 1)
                    copy_window(s, i + 1)
                    dve.wait_ge(s.onehot_used, STEPS * (i + 2))
                    dve.wait_ge(s.added, 16 * i)
                    if k == 0:
                        nc.vector.tensor_copy(seg_sb[:, :], ps[:, 6, 0:C1])
                        nc.vector.tensor_tensor(gram_m[:, :], gram_m[:, :], ps[0:C, 7, 0:C1], ALU.add).then_inc(s.seg_out, 1)
                    else:
                        nc.vector.tensor_copy(seg_sb[:, 0:C], ps[:, 6, 0:C]).then_inc(s.seg_out, 1)

                if k == 0:
                    dve.wait_ge(s.seg_out, G)
                    gram_coefficients(gram_m, E, 7, 8, 9, GM, BM)
                    spread(8, 9, 2)
                    between_layers()
                else:
                    finish()


_INS = ["x", "src", "dst", "edge_attr_4", "edge_attr_96", "L0_gnn_W_node", "L0_gnn_b_node", "L0_gnn_g_node",
        "L0_gnn_beta_node", "L0_gnn_W_edge", "L0_gnn_b_edge", "L0_gnn_g_edge", "L0_gnn_beta_edge", "L0_gnn_W_msg",
        "L0_gnn_b_msg", "L0_gnn_g_msg", "L0_gnn_beta_msg", "L1_gnn_Wm1", "L1_gnn_bm1", "L1_gnn_Wm2", "L1_gnn_bm2",
        "L1_gnn_Wu1", "L1_gnn_bu1", "L1_gnn_Wu2", "L1_gnn_bu2"]


def kernel(**inputs):
    import numpy as np
    import concourse.bacc as bacc
    from concourse.bass_utils import run_bass_kernel_spmd

    nc = bacc.Bacc("TRN2", target_bir_lowering=False, num_devices=1)
    arrays, args = {}, []
    for name in _INS:
        a = np.ascontiguousarray(inputs[name])
        arrays[f"in_{name}"] = a
        args.append(nc.dram_tensor(f"in_{name}", a.shape, mybir.dt.from_np(a.dtype), kind="ExternalInput").ap())
    out = nc.dram_tensor("out_nodes", inputs["x"].shape, F32, kind="ExternalOutput").ap()
    build_gnn(nc, *args, out)
    r = run_bass_kernel_spmd(nc, [arrays], core_ids=[0])
    return r.results[0]["out_nodes"]
```

```python
import concourse.bass as bass
from concourse import mybir
from contextlib import ExitStack

F32 = mybir.dt.float32
BF16 = mybir.dt.bfloat16
I32 = mybir.dt.int32
ALU = mybir.AluOpType
ACT = mybir.ActivationFunctionType
AX = mybir.AxisListType

P = 128
BANK = 512
EPS = 1e-5


def build_gnn(nc, x, src, dst, edge4, factors, W_node, b_node, g_node, beta_node, W_edge, b_edge, g_edge,
              beta_edge, W_msg, b_msg, g_msg, beta_msg, Wm1, bm1, Wm2, bm2, Wu1, bu1, Wu2, bu2, out):
    N, C = x.shape
    E, KE = edge4.shape
    STEPS, ST = 5, 5
    TG = STEPS * ST
    GE = TG * P
    G = E // GE
    NT, CH = 100, 5
    NP = N // NT
    NCH = NT // CH
    assert G * GE == E and NP * NT == N and NP <= P and NCH % 2 == 0 and NT <= G
    C1 = C + 1
    STC = ST * C
    CHC = CH * C
    NR = N + P
    PARTS = 3
    RT = PARTS * PARTS * KE
    TR = P // RT
    NB = -(-TG // TR)
    RB = TR * RT

    src_v = src.rearrange("(g p t) -> g p t", p=P, t=TG)
    dst_v = dst.rearrange("(g p t) -> p g t", p=P, t=TG)
    edge4_v = edge4.rearrange("(g p t) k -> g p (t k)", p=P, t=TG)
    factors_v = factors.rearrange("(g p t) c -> g p (t c)", p=P, t=TG)
    x_v = x.rearrange("(p j) c -> p (j c)", j=NT)
    out_v = out.rearrange("(p j) c -> p (j c)", j=NT)

    def dram(name, shape, dt=F32):
        return nc.dram_tensor(name, shape, dt, kind="Internal").ap()

    srows = [dram(f"source_rows{k}", (N, C)) for k in range(2)]
    drows = [dram(f"dest_rows{k}", (NR, PARTS * C), BF16) for k in range(2)]
    sums = [dram("sums0", (NR, C1)), dram("sums1", (NR, C))]
    h1_dram = dram("h1_rows", (N, C))
    queue = dram("gathered_queue", (G, P, TG * C))
    srows_v = [t.rearrange("(p j) c -> p (j c)", j=NT) for t in srows]
    drows_v = [t[0:N, :].rearrange("(p j) c -> p (j c)", j=NT) for t in drows]
    sums_v = [t[0:N, :].rearrange("(p j) c -> p (j c)", j=NT) for t in sums]
    h1_v = h1_dram.rearrange("(p j) c -> p (j c)", j=NT)
    WIDTH = (C1, C)

    ctx = ExitStack()
    with ctx:
        def sb(name, shape, dt=F32):
            return ctx.enter_context(nc.sbuf_tensor(name, shape, dt))

        def sem(name):
            return ctx.enter_context(nc.semaphore(name))

        ident = sb("ident", [P, P])
        ident_b = sb("ident_b", [P, P], BF16)
        ones = sb("ones", [P, P])
        iota_i = sb("iota_i", [P, P], I32)
        iota = sb("iota", [P, P])
        iotap_i = sb("iotap_i", [P, 1], I32)
        iotap = sb("iotap", [P, 1])
        zeros = sb("zeros", [P, CH * C1])
        rel = sb("rel", [P, (G + 1) * TG])
        base_i = sb("base_i", [1, G], I32)
        base_f = sb("base_f", [1, G])
        base_all = sb("base_all", [P, G])
        carry_all = sb("carry_all", [P, G + 1])
        kept_all = sb("kept_all", [P, G])
        part_mask = sb("part_mask", [RB, TR, PARTS, PARTS])
        pm = sb("pm", [RB, TR, PARTS])
        we_rep = sb("we_rep", [RB, C])
        we_r = sb("we_r", [RB, C])
        we_acc = sb("we_acc", [RB, C])
        we_b = sb("we_b", [RB, PARTS, C], BF16)
        we_blk = sb("we_blk", [RB, TR, C], BF16)
        proj_w = [sb(f"proj_w{k}", [C1, 3 * C]) for k in range(2)]
        wc = sb("wc", [C, C])
        wc1 = sb("wc1", [C1, C])
        bmsg_row = sb("bmsg_row", [C1, C])
        wm2 = sb("wm2", [C1, C])
        wu1b = sb("wu1b", [C, C])
        wu2 = sb("wu2", [C1, C])
        cols = sb("cols", [C, 8])
        stat = sb("stat", [C, 16])
        ce_lhs = sb("ce_lhs", [C, C1])
        diag = sb("diag", [C, 2, C])
        rows = sb("rows", [NP, 2, C])
        bn_edge = sb("bn_edge", [C, 2 * STEPS, 6])
        mv_group = sb("mv_group", [C, 2])
        mv_edge = sb("mv_edge", [C, G, 2])
        part_sums = sb("part_sums", [P, 2, C])
        acc_sum = sb("acc_sum", [P, C1])
        acc_sq = sb("acc_sq", [P, STC])

        x_all = sb("x_all", [NP, NT * C])
        h_all = sb("h_all", [NP, NT * C])
        xs = [sb(f"xs{b}", [NP, CHC]) for b in range(2)]
        xT = [sb(f"xT{b}", [C1, CH * NP]) for b in range(2)]
        u_st = [sb(f"u_st{b}", [NP, CHC]) for b in range(2)]
        v_st = [sb(f"v_st{b}", [NP, CH, PARTS, C], BF16) for b in range(2)]
        r1 = [sb(f"r1{b}", [NP, CHC]) for b in range(2)]
        h_sq = [sb(f"h_sq{b}", [NP, CHC]) for b in range(2)]
        s_ch = [sb(f"s_ch{b}", [NP, CH, C1]) for b in range(2)]
        y_ch = [sb(f"y_ch{b}", [NP, CHC]) for b in range(2)]
        ln_bn = [sb(f"ln_bn{b}", [NP, CH, 6]) for b in range(2)]
        ln_mv = [sb(f"ln_mv{b}", [NP, CH, 2]) for b in range(2)]
        ln_rs = [sb(f"ln_rs{b}", [NP, CH]) for b in range(2)]
        ln_nb = [sb(f"ln_nb{b}", [NP, CH]) for b in range(2)]

        idx = sb("idx", [P, STEPS, ST], I32)
        grows = sb("grows", [P, STEPS, STC])
        onehot = sb("onehot", [P, STEPS, ST * P])
        onehotT = sb("onehotT", [P, STEPS, ST * P], BF16)
        eas = sb("eas", [P, TG, KE])
        ea_r = sb("ea_r", [P, TG, KE])
        ea9 = sb("ea9", [P, TG, PARTS, PARTS, KE], BF16)
        eaT = sb("eaT", [RB, NB * P], BF16)
        heT = sb("heT", [C1, STEPS, ST * P])
        pre = sb("pre", [P, STEPS, STC])
        hm = sb("hm", [P, STEPS, ST, C1])
        win_ld = sb("win_ld", [P, PARTS * C], BF16)
        win = sb("win", [P, PARTS * C], BF16)
        seg_sb = sb("seg_sb", [P, C1])
        carry = sb("carry", [P, P])
        relraw = onehot[:, :, :].rearrange("p s n -> p (s n)")[:, 0:G * TG].bitcast(I32)
        hsum = pre[:, :, :].rearrange("p s n -> p (s n)")[0:NP, 0:NCH * C].rearrange("p (n c) -> p n c", c=C)
        hsqsum = onehot[:, :, :].rearrange("p s n -> p (s n)")[0:NP, 0:NCH * C].rearrange("p (n c) -> p n c", c=C)

        ps = ctx.enter_context(nc.psum_tensor("ps", [P, 8, BANK], F32))
        flat = ps[:, :, :].rearrange("p b n -> p (b n)")
        flat_b = flat.bitcast(BF16)

        link_v = sem("link_v")
        const_ready = sem("const_ready")
        bias_rows = sem("bias_rows")
        identb_ready = sem("identb_ready")
        zero_w, zero_in, param_in, dst_in, xall_in = (sem(n) for n in ("zero_w", "zero_in", "param_in", "dst_in", "xall_in"))
        base_cast, base_bc, rel_ready, we_ready = (sem(n) for n in ("base_cast", "base_bc", "rel_ready", "we_ready"))
        xs_in = [sem(f"xs_in{b}") for b in range(2)]
        xs_T = [sem(f"xs_T{k}") for k in range(2)]
        xT_ready = [sem(f"xT_ready{k}") for k in range(2)]
        proj_done = [sem(f"proj_done{k}") for k in range(2)]
        uhm_ready = [sem(f"uhm_ready{k}") for k in range(2)]
        r1_ready = [sem(f"r1_ready{k}") for k in range(2)]
        mid_ready = [sem(f"mid_ready{k}") for k in range(2)]
        low_ready = [sem(f"low_ready{k}") for k in range(2)]
        u_out = [[sem(f"u_out{k}{b}") for b in range(2)] for k in range(2)]
        v_out = [[sem(f"v_out{k}{b}") for b in range(2)] for k in range(2)]
        squared, chunk_summed, node_sums = sem("squared"), sem("chunk_summed"), sem("node_sums")
        root_wanted, root_ready = sem("root_wanted"), sem("root_ready")
        sums_wanted, diag_ready, rows_spread = sem("sums_wanted"), sem("diag_ready"), sem("rows_spread")
        rows_read = sem("rows_read")
        ce_ready, ce_done, wc1_ready = sem("ce_ready"), sem("ce_done"), sem("wc1_ready")
        ea_in, ea_hi, ea_rest, ea_mid, ea_split, eaT_done, eaT_sb = (sem(n) for n in (
            "ea_in", "ea_hi", "ea_rest", "ea_mid", "ea_split", "eaT_done", "eaT_sb"))
        a_he, a_relu, a_bn, a_turn, a_mv = (sem(n) for n in ("a_he", "a_relu", "a_bn", "a_turn", "a_mv"))
        xn_scaled, xn_added, xn_done = (sem(n) for n in ("xn_scaled", "xn_added", "xn_done"))

        class EdgeSems:

            def __init__(self, k):
                self.rows_used = sem(f"rows_used{k}")
                self.onehot_ready = sem(f"onehot_ready{k}")
                self.onehot_used = sem(f"onehot_used{k}")
                self.T_done = sem(f"T_done{k}")
                self.T_copied = sem(f"T_copied{k}")
                self.H_relu = sem(f"H_relu{k}")
                self.P_done = sem(f"P_done{k}")
                self.win_in = sem(f"win_in{k}")
                self.win_ready = sem(f"win_ready{k}")
                self.seg_out = sem(f"seg_out{k}")
                self.sums_out = sem(f"sums_out{k}")
                self.turn = sem(f"turn{k}")

        L0, L1 = L = (EdgeSems(0), EdgeSems(1))
        idx_in = [sem(f"idx_in{j}") for j in range(STEPS)]
        gathered = [sem(f"gathered{j}") for j in range(STEPS)]
        stored = [sem(f"stored{j}") for j in range(STEPS)]
        rows_in = [sem(f"rows_in{j}") for j in range(STEPS)]
        H_done, h_ready = sem("H_done"), sem("h_ready")
        factors_in = [sem(f"factors_in{j}") for j in range(STEPS)]
        P_out = sem("P_out")
        msg_squared, msg_added = sem("msg_squared"), sem("msg_added")
        s_in = [sem(f"s_in{b}") for b in range(2)]
        y_scaled, y_added, y_ready, z_summed = (sem(n) for n in ("y_scaled", "y_added", "y_ready", "z_summed"))
        h1_out = [sem(f"h1_out{b}") for b in range(2)]
        m_in = [sem(f"m_in{b}") for b in range(2)]
        h1_in = [sem(f"h1_in{b}") for b in range(2)]
        o_out = [sem(f"o_out{b}") for b in range(2)]
        f_T, f_mT, f_z, f_zr, f_zT, f_zT_sb, f_o, f_y = (sem("f_" + n) for n in ("T", "mT", "z", "zr", "zT", "zT_sb", "o", "y"))

        norm_bnd, norm_turn, norm_agg, norm_eps, norm_root, norm_inv, norm_scaled, norm_done = (
            sem("norm_" + n) for n in ("bnd", "turn", "agg", "eps", "root", "inv", "scaled", "done"))

        PARAMS = [(proj_w[0][0:C, 0:C], W_msg[0:C, :]), (proj_w[0][0:C, C:2 * C], W_msg[C:2 * C, :]),
                  (proj_w[0][0:C, 2 * C:3 * C], W_node), (proj_w[0][C:C1, 2 * C:3 * C], b_node.unsqueeze(0)),
                  (proj_w[1][0:C, 0:C], Wm1[0:C, :]), (proj_w[1][0:C, C:2 * C], Wm1[C:2 * C, :]),
                  (proj_w[1][0:C, 2 * C:3 * C], Wu1[0:C, :]), (proj_w[1][C:C1, C:2 * C], bm1.unsqueeze(0)),
                  (proj_w[1][C:C1, 2 * C:3 * C], bu1.unsqueeze(0)),
                  (wc[:, :], W_msg[2 * C:3 * C, :]), (bmsg_row[C:C1, :], b_msg.unsqueeze(0)),
                  (wm2[0:C, :], Wm2), (wm2[C:C1, :], bm2.unsqueeze(0)), (wu1b[:, :], Wu1[C:2 * C, :]),
                  (wu2[0:C, :], Wu2), (wu2[C:C1, :], bu2.unsqueeze(0))]
        PARAMS += [(cols[:, i:i + 1], v.unsqueeze(1)) for i, v in
                   enumerate((b_edge, g_edge, beta_edge, g_node, beta_node, g_msg, beta_msg))]
        PARAMS += [(we_rep[KE * t:KE * (t + 1), :], W_edge) for t in range(RB // KE)]
        BE, GEDGE, BEDGE, GN, BN, GM, BM = range(7)
        MEAN, SCALE, SHIFT, VAR, ROOT, TMP = range(6)
        ONE = 1
        N_ZEROS = NCH + 1
        N_CONST = 9
        N_CONSTS = N_CONST + 5

        def after(eng, s, value):
            if not (isinstance(value, int) and value <= 0):
                eng.wait_ge(s, value)

        PEEL = 2

        def over_chunks(eng, body):
            def pair(i):
                for b in range(2):
                    body(2 * i + b, i, b)
            for i in range(PEEL):
                pair(i)
            with eng.Fori(PEEL, NCH // 2 - 1) as i:
                pair(i)
            pair(NCH // 2 - 1)

        def chunk_before(c, i, b):
            return c - 1, (i if b else i - 1), 1 - b

        def first_chunk(c):
            return isinstance(c, int) and c == 0

        LAST = (NCH - 1, NCH // 2 - 1, 1)

        def step_before(i, j, lag=1):
            back = int(j < lag)
            return STEPS * i + j - lag, i - back, (j - lag) % STEPS

        def over_groups(eng, body):
            body(0, True, False)
            with eng.Fori(1, G - 1) as i:
                body(i, False, False)
            body(G - 1, False, True)

        block = ctx.enter_context(nc.Block())

        @block.sync
        def _(sp):
            def load_x(c, b):
                sp.dma_start(xs[b][:, :], x_v[:, bass.ds(c * CHC, CHC)]).then_inc(xs_in[b], 16)

            for b in range(2):
                load_x(b, b)
            with nc.allow_non_contiguous_dma(reason="columns of parameters and first destinations, once"):
                for to, of in PARAMS:
                    sp.dma_start(to, of).then_inc(param_in, 16)
                first = dst.rearrange("(g e) -> g e", e=GE)[:, 0:1].rearrange("g a -> a g")
                sp.dma_start(base_i[:, :], first).then_inc(dst_in, 16)
            sp.wait_ge(const_ready, 1)
            sp.dma_start(proj_w[0][C:C1, 0:2 * C], zeros[0:1, 0:2 * C]).then_inc(zero_w, 16)
            sp.dma_start(proj_w[1][C:C1, 0:C], zeros[0:1, 0:C]).then_inc(zero_w, 16)
            sp.dma_start(relraw.rearrange("p (g t) -> p g t", t=TG), dst_v).then_inc(dst_in, 16)
            for k in range(2):
                sp.dma_start(drows[k][N:NR, :], zeros[:, 0:PARTS * C // 2].bitcast(BF16)).then_inc(zero_in, 16)

            def store_chunk(k, c, i, b):
                sp.wait_ge(uhm_ready[k], c + 1)
                sp.dma_start(srows_v[k][:, bass.ds(c * CHC, CHC)], u_st[b][:, :]).then_inc(u_out[k][b], 16)
                sp.wait_ge(low_ready[k], c + 1)
                sp.dma_start(drows_v[k][:, bass.ds(c * PARTS * CHC, PARTS * CHC)],
                             v_st[b][:, :, :, :].rearrange("p a b c -> p (a b c)")).then_inc(v_out[k][b], 16)

            def x_chunk(c, i, b):
                if not (isinstance(c, int) and c + 2 >= NCH):
                    sp.wait_ge(xs_T[0], c + 1)
                    load_x(c + 2, b)
                if not first_chunk(c):
                    store_chunk(0, *chunk_before(c, i, b))

            over_chunks(sp, x_chunk)
            store_chunk(0, *LAST)

            def load_indices(k, i, j):
                sp.dma_start(idx[:, j, :], src_v[bass.ds(i, 1), :, j * ST:(j + 1) * ST].rearrange("a p t -> (a p) t"))\
                  .then_inc(idx_in[j], 16)

            for j in range(STEPS):
                load_indices(0, 0, j)
            LAG = 2

            def enqueue(i, j, more):
                sp.wait_ge(gathered[j], 16 * ST * (i + 1))
                sp.dma_start(queue[bass.ds(i, 1), :, j * STC:(j + 1) * STC].rearrange("a p n -> (a p) n"), grows[:, j, :])\
                  .then_inc(stored[j], 16)
                if more and j >= LAG:
                    sp.wait_ge(stored[j - LAG], 16 * (i + 1))
                    load_indices(0, i + 1, j - LAG)

            def queue_group(i):
                for j in range(STEPS):
                    enqueue(i, j, True)
                for j in range(STEPS - LAG, STEPS):
                    sp.wait_ge(stored[j], 16 * (i + 1))
                    load_indices(0, i + 1, j)

            with sp.Fori(0, NCH) as i:
                queue_group(i)
                sp.dma_start(x_all[:, bass.ds(i * CHC, CHC)], x_v[:, bass.ds(i * CHC, CHC)]).then_inc(xall_in, 16)
                for k in range(2):
                    n = CH * WIDTH[k]
                    sp.dma_start(sums_v[k][:, bass.ds(i * n, n)], zeros[0:NP, 0:n]).then_inc(L[k].sums_out, 16)
            for k in range(2):
                sp.dma_start(sums[k][N:NR, :], zeros[:, 0:WIDTH[k]]).then_inc(L[k].sums_out, 16)
            with sp.Fori(NCH, G - 1) as i:
                queue_group(i)
            for j in range(STEPS):
                enqueue(G - 1, j, False)

            def load_sums(c, b):
                sp.dma_start(s_ch[b][:, :, :].rearrange("p a b -> p (a b)"), sums_v[0][:, bass.ds(c * CH * C1, CH * C1)])\
                  .then_inc(s_in[b], 16)

            def middle_chunk(c, i, b):
                if not (isinstance(c, int) and c + 2 >= NCH):
                    sp.wait_ge(y_ready, c + 1)
                    load_sums(c + 2, b)
                sp.wait_ge(norm_done, c + 1)
                sp.dma_start(h1_v[:, bass.ds(c * CHC, CHC)], xs[b][:, :]).then_inc(h1_out[b], 16)
                if not first_chunk(c):
                    store_chunk(1, *chunk_before(c, i, b))

            sp.wait_ge(L0.sums_out, 16 * (N_ZEROS + G))
            for b in range(2):
                load_sums(b, b)
            over_chunks(sp, middle_chunk)
            store_chunk(1, *LAST)

            def first_of(i):
                return sp.value_load(dst[bass.ds(i * GE, 1)].unsqueeze(0), min_val=0, max_val=N - 1)

            def load_window(first):
                sp.dma_start(win_ld[:, :], drows[1][bass.ds(first, P), :]).then_inc(L1.win_in, 16)

            def load_factors(i, j):
                sp.dma_start(pre[:, j, :], factors_v[bass.ds(i, 1), :, j * STC:(j + 1) * STC].rearrange("a p n -> (a p) n"))\
                  .then_inc(factors_in[j], 16)

            def store_sums(i):
                first = first_of(i)
                sp.wait_ge(L1.seg_out, i + 2)
                sp.wait_ge(L1.sums_out, 16 * (N_ZEROS + i))
                sp.dma_start(sums[1][bass.ds(first, P), :], seg_sb[:, 0:C]).then_inc(L1.sums_out, 16)

            for j in range(STEPS):
                load_indices(1, 0, j)
                load_factors(0, j)
            first = first_of(0)
            for b in range(2):
                sp.wait_ge(v_out[1][b], 16 * (NCH // 2))
            sp.wait_ge(zero_in, 32)
            load_window(first)
            def refill(i, store):
                first = first_of(i)
                sp.wait_ge(L1.win_ready, i)
                load_window(first)
                for j in range(STEPS):
                    sp.wait_ge(L1.rows_used, ONE + STEPS * (i - 1) + j + 1)
                    load_indices(1, i, j)
                    if j:
                        sp.wait_ge(P_out, ONE + STEPS * (i - 1) + j)
                        load_factors(i, j - 1)
                    if j == 3 and store:
                        store_sums(i - 2)
                sp.wait_ge(P_out, ONE + STEPS * i)
                load_factors(i, STEPS - 1)

            refill(1, False)
            with sp.Fori(2, G) as i:
                refill(i, True)
            first = first_of(0)
            sp.wait_ge(L1.win_ready, G)
            load_window(first)
            store_sums(G - 2)
            store_sums(G - 1)

            def load_m(c, b):
                sp.dma_start(xs[b][:, :], sums_v[1][:, bass.ds(c * CHC, CHC)]).then_inc(m_in[b], 16)

            def load_h1(c, b):
                sp.dma_start(y_ch[b][:, :], h1_v[:, bass.ds(c * CHC, CHC)]).then_inc(h1_in[b], 16)

            def store_out(c, i, b):
                sp.wait_ge(norm_done, NCH + c + 1)
                sp.dma_start(out_v[:, bass.ds(c * CHC, CHC)], u_st[b][:, :]).then_inc(o_out[b], 16)

            def last_chunk(c, i, b):
                if not (isinstance(c, int) and c + 2 >= NCH):
                    sp.wait_ge(f_T, c + 1)
                    load_m(c + 2, b)
                if not first_chunk(c):
                    pc, pi, pb = chunk_before(c, i, b)
                    store_out(pc, pi, pb)
                    if not (isinstance(c, int) and c + 1 >= NCH):
                        load_h1(c + 1, pb)

            for b in range(2):
                sp.wait_ge(h1_out[b], 16 * (NCH // 2))
                load_h1(b, b)
            sp.wait_ge(L1.sums_out, 16 * (N_ZEROS + G))
            for b in range(2):
                load_m(b, b)
            over_chunks(sp, last_chunk)
            store_out(*LAST)
            for b in range(2):
                sp.wait_ge(o_out[b], 16 * (NCH // 2))
                for k in range(2):
                    sp.wait_ge(u_out[k][b], 16 * (NCH // 2))

        @block.gpsimd
        def _(pool):
            pool.memset(zeros[:, :], 0.0).then_inc(const_ready, 1)
            pool.memset(ones[:, :], 1.0).then_inc(const_ready, 1)
            pool.iota(iota_i[:, :], pattern=[[1, P]], base=0, channel_multiplier=0).then_inc(const_ready, 1)
            pool.iota(iotap_i[:, :], pattern=[[0, 1]], base=0, channel_multiplier=1).then_inc(const_ready, 1)
            pool.memset(ident[:, :], 0.0).then_inc(const_ready, 1)
            pool.memset(part_mask[:, :, :, :], 1.0).then_inc(const_ready, 1)
            pool.memset(hm[:, :, :, C:C1], 1.0).then_inc(const_ready, 1)
            pool.memset(rel[:, G * TG:], 0.0).then_inc(const_ready, 1)
            pool.memset(ce_lhs[:, :], 0.0).then_inc(const_ready, 1)
            pool.wait_ge(const_ready, N_CONST)
            pool.affine_select(out=ident[:, :], in_=ident[:, :], compare_op=ALU.not_equal, fill=1.0, base=0,
                               pattern=[[-1, P]], channel_multiplier=1).then_inc(const_ready, 1)
            row_of = [[RT, TR], [KE, PARTS], [PARTS * KE, PARTS]]
            pool.affine_select(out=part_mask[:, :, :, :], in_=part_mask[:, :, :, :], compare_op=ALU.is_ge, fill=0.0, base=0,
                               pattern=[[-s, n] for s, n in row_of], channel_multiplier=1).then_inc(const_ready, 1)
            pool.wait_ge(const_ready, N_CONST + 2)
            pool.affine_select(out=part_mask[:, :, :, :], in_=part_mask[:, :, :, :], compare_op=ALU.is_ge, fill=0.0,
                               base=KE - 1, pattern=row_of, channel_multiplier=-1).then_inc(const_ready, 1)
            pool.memset(carry[:, :], 0.0).then_inc(const_ready, 1)
            pool.memset(carry_all[:, 0:1], 0.0).then_inc(const_ready, 1)
            pool.wait_ge(const_ready, N_CONSTS)

            for k in range(2):
                for b in range(2):
                    pool.wait_ge(u_out[k][b], 16 * (NCH // 2))
                with pool.Fori(0, G) as i:
                    pool.wait_ge(idx_in[0], 16 * (k * G + 1) + 16 * i)
                    pool.sem_inc(L[k].turn, 1)
                    for j in range(STEPS):
                        if j:
                            pool.wait_ge(u_out[k][1], 16 * (NCH // 2))
                            pool.wait_ge(idx_in[j], 16 * (k * G + 1) + 16 * i)
                        for t in range(ST):
                            pool.indirect_dma_start(
                                out=grows[:, j, t * C:(t + 1) * C], out_offset=None, in_=srows[k],
                                in_offset=bass.IndirectOffsetOnAxis(ap=idx[:, j, t:t + 1], axis=0)).then_inc(gathered[j], 16)

        @block.tensor
        def _(pe):
            def in_bank(bank, t, rows_=C, width=P):
                return flat[0:rows_, bank * BANK + t * P:bank * BANK + t * P + width]

            pe.wait_ge(const_ready, N_CONSTS)
            pe.wait_ge(base_cast, 1)
            nc.tensor.matmul(ps[:, 7, 0:G], ones[0:1, 0:P], base_f[:, :], start=True, stop=True).then_inc(base_bc, 1)
            pe.wait_ge(param_in, 16 * len(PARAMS))
            pe.wait_ge(bias_rows, 1)
            pe.wait_ge(zero_w, 32)
            pe.wait_ge(rel_ready, 1)

            def transpose_chunk(k, c, i, b):
                if k == 0:
                    pe.wait_ge(xs_in[b], 16 * (i + 1))
                else:
                    pe.wait_ge(norm_done, c + 1)
                after(pe, xT_ready[k], c)
                for j in range(CH):
                    last = nc.tensor.transpose(in_bank(0, j, C, NP), xs[b][:, j * C:(j + 1) * C], ident[0:NP, 0:NP])
                last.then_inc(xs_T[k], 1)

            def project_chunk(k, c, i, b):
                pe.wait_ge(xT_ready[k], c + 1)
                after(pe, low_ready[k], c - 1)
                if k == 0:
                    after(pe, uhm_ready[k], c - 1)
                for j in range(CH):
                    for m in range(3):
                        last = nc.tensor.matmul(ps[0:NP, 2 + 3 * b + m, j * C:(j + 1) * C], xT[b][:, j * NP:(j + 1) * NP],
                                                proj_w[k][:, m * C:(m + 1) * C], start=True, stop=True)
                last.then_inc(proj_done[k], 1)

            def project(k):
                def body(c, i, b):
                    if k == 1 and not first_chunk(c):
                        project_chunk(k, *chunk_before(c, i, b))
                    transpose_chunk(k, c, i, b)
                    if k == 0 and not first_chunk(c):
                        project_chunk(k, *chunk_before(c, i, b))
                over_chunks(pe, body)
                project_chunk(k, *LAST)

            project(0)

            def sum_partitions(nth, n):
                pe.wait_ge(sums_wanted, nth)
                for m in range(2):
                    last = nc.tensor.matmul(ps[0:C, 7, m:m + 1], part_sums[0:n, m, :], ones[0:n, 0:1], start=True, stop=True)
                last.then_inc(node_sums, 1)

            sum_partitions(1, NP)

            def spread_rows():
                for m in range(2):
                    last = nc.tensor.matmul(ps[0:NP, 7, m * C:(m + 1) * C], ones[0:C, 0:NP], diag[:, m, :], start=True, stop=True)
                last.then_inc(rows_spread, 1)

            pe.wait_ge(diag_ready, 1)
            spread_rows()

            def attributes_T(m):
                pe.wait_ge(ea_split, m + 1)
                flat_ea = ea9[:, :, :, :, :].rearrange("p t a b k -> p (t a b k)")
                for q in range(NB):
                    width = min(RB, (TG - q * TR) * RT)
                    last = nc.tensor.transpose(flat_b[0:width, q * P:(q + 1) * P], flat_ea[:, q * RB:q * RB + width], ident_b[:, :])
                last.then_inc(eaT_done, 1)

            def edge_hidden(j, bank):
                for t in range(ST):
                    q, r = divmod(j * ST + t, TR)
                    rows_ = min(RB, (TG - q * TR) * RT)
                    last = nc.tensor.matmul(in_bank(bank, t), we_blk[0:rows_, r, :], eaT[0:rows_, q * P:(q + 1) * P],
                                            start=True, stop=True)
                return last

            pe.wait_ge(we_ready, 1)
            pe.wait_ge(identb_ready, 1)
            attributes_T(0)
            with pe.Fori(0, G) as i:
                pe.wait_ge(eaT_sb, i + 1)
                for j in range(STEPS):
                    pe.wait_ge(a_relu, ONE + STEPS * i + (j - 1 if j else 0))
                    edge_hidden(j, 2 + 2 * (j % 2)).then_inc(a_he, 1)
                attributes_T(i + 1)

            pe.wait_ge(ce_ready, 1)
            nc.tensor.matmul(ps[0:C1, 7, 0:C], ce_lhs[:, :], wc[:, :], start=True, stop=True).then_inc(ce_done, 1)

            def onehot_T(s, n, j, bank):
                pe.wait_ge(s.onehot_ready, n + 1)
                after(pe, s.T_copied, n)
                high = onehot[:, j, :].bitcast(BF16).rearrange("p (n h) -> p n h", h=2)[:, :, 1]
                for t in range(ST):
                    at = 2 * bank * BANK + t * P
                    last = nc.tensor.transpose(flat_b[:, at:at + P], high[:, t * P:(t + 1) * P], ident_b[:, :])
                last.then_inc(s.T_done, 1)

            def sum_step(s, k, j):
                if j == 0:
                    nc.tensor.matmul(ps[:, 6, 0:WIDTH[k]], carry[:, :], seg_sb[:, 0:WIDTH[k]], start=True, stop=False)
                for t in range(ST):
                    last = nc.tensor.matmul(ps[:, 6, 0:WIDTH[k]], onehot[:, j, t * P:(t + 1) * P], hm[:, j, t, 0:WIDTH[k]],
                                            start=False, stop=(j == STEPS - 1 and t == ST - 1))
                last.then_inc(s.onehot_used, 1)

            s = L0

            def H0(n, j):
                after(pe, s.H_relu, n)
                edge_hidden(j, 4).then_inc(H_done, 1)

            def P0(n, j):
                pe.wait_ge(s.H_relu, n + 1)
                pe.wait_ge(s.T_copied, n + 1)
                pe.wait_ge(s.rows_used, ONE + n if j == 0 else ONE + n - 1)
                for t in range(ST):
                    o = ps[:, 2 + j % 2, t * C:(t + 1) * C]
                    nc.tensor.matmul(o, heT[:, j, t * P:(t + 1) * P], wc1[:, :], start=True, stop=False)
                    for m in range(PARTS):
                        last = nc.tensor.matmul(o, onehotT[:, j, t * P:(t + 1) * P], win[:, m * C:(m + 1) * C],
                                                start=False, stop=(m == PARTS - 1))
                last.then_inc(s.P_done, 1)

            def S0(n, j):
                pe.wait_ge(h_ready, n + 1)
                sum_step(s, 0, j)

            pe.sem_inc(s.onehot_used, STEPS)
            pe.wait_ge(wc1_ready, 1)
            pe.wait_ge(eaT_sb, G + 1)
            onehot_T(s, 0, 0, 7)
            H0(0, 0)

            def layer0_group(i, first, last):
                for j in range(STEPS):
                    n = STEPS * i + j
                    onehot_T(s, n + 1, (j + 1) % STEPS, 7)
                    if j == STEPS - 1:
                        pe.wait_ge(eaT_sb, G + i + 2)
                    H0(n + 1, (j + 1) % STEPS)
                    if j == 0:
                        pe.wait_ge(s.win_ready, i + 1)
                    P0(n, j)
                    if j == 1:
                        pe.wait_ge(s.seg_out, i + 1)
                    if not (first and j == 0):
                        m, _, slot = step_before(i, j)
                        S0(m, slot)
                    if j == STEPS - 3:
                        attributes_T(G + i + 1)

            over_groups(pe, layer0_group)
            S0(STEPS * G - 1, STEPS - 1)

            sum_partitions(2, P)
            pe.wait_ge(diag_ready, 2)
            spread_rows()
            pe.wait_ge(rows_read, 2)
            project(1)

            s = L1

            def X1(n, i, j):
                pe.wait_ge(s.T_copied, n + 1)
                pe.wait_ge(s.H_relu, ONE + n if j == 0 else ONE + n - 1)
                pe.wait_ge(gathered[j], 16 * ST * (G + 1) + 16 * ST * i)
                for t in range(ST):
                    o = in_bank(2 + 2 * (j % 2), t)
                    for m in range(PARTS):
                        nc.tensor.matmul(o, win[:, m * C:(m + 1) * C], onehotT[:, j, t * P:(t + 1) * P],
                                         start=(m == 0), stop=False)
                    last = nc.tensor.matmul(o, grows[:, j, t * C:(t + 1) * C], ident[:, :], start=False, stop=True)
                last.then_inc(s.rows_used, 1)

            def E1(n, j):
                pe.wait_ge(s.H_relu, ONE + n + 1)
                pe.wait_ge(P_out, ONE + n)
                for t in range(ST):
                    last = nc.tensor.matmul(ps[:, 7, t * C:(t + 1) * C], heT[:, j, t * P:(t + 1) * P], wm2[:, :],
                                            start=True, stop=True)
                last.then_inc(s.P_done, 1)

            def S1(n, j):
                pe.wait_ge(P_out, ONE + n + 1)
                sum_step(s, 1, j)

            pe.sem_inc(s.onehot_used, STEPS)
            pe.sem_inc(s.rows_used, ONE)
            pe.wait_ge(low_ready[1], NCH)
            pe.wait_ge(uhm_ready[1], NCH)
            onehot_T(s, 0, 0, 0)

            def layer1_group(i, first, last):
                for j in range(STEPS):
                    n = STEPS * i + j
                    onehot_T(s, n + 1, (j + 1) % STEPS, 0)
                    if j == 0:
                        pe.wait_ge(s.win_ready, i + 1)
                    X1(n, i, j)
                    if not (first and j == 0):
                        m, _, slot = step_before(i, j)
                        E1(m, slot)
                    if j == 2:
                        pe.wait_ge(s.seg_out, i + 1)
                    if not (first and j < 2):
                        m, _, slot = step_before(i, j, 2)
                        S1(m, slot)

            over_groups(pe, layer1_group)
            n = STEPS * G - 1
            E1(n, STEPS - 1)
            S1(n - 1, STEPS - 2)
            S1(n, STEPS - 1)

            pe.wait_ge(s.T_copied, STEPS * G + 1)
            pe.wait_ge(s.seg_out, G + 1)

            def sums_T(c, i, b):
                pe.wait_ge(m_in[b], 16 * (i + 1))
                after(pe, f_mT, c)
                for j in range(CH):
                    last = nc.tensor.transpose(in_bank(0, j, C, NP), xs[b][:, j * C:(j + 1) * C], ident[0:NP, 0:NP])
                last.then_inc(f_T, 1)

            def hidden_T(c, i, b):
                pe.wait_ge(f_zr, c + 1)
                after(pe, f_zT_sb, c)
                for j in range(CH):
                    last = nc.tensor.transpose(in_bank(2, j, C, NP), r1[b][:, j * C:(j + 1) * C], ident[0:NP, 0:NP])
                last.then_inc(f_zT, 1)

            def hidden(c, i, b):
                pe.wait_ge(f_mT, c + 1)
                after(pe, f_zr, c - 1)
                for j in range(CH):
                    last = nc.tensor.matmul(ps[0:NP, 4 + 2 * b, j * C:(j + 1) * C], xT[b][0:C, j * NP:(j + 1) * NP], wu1b[:, :],
                                            start=True, stop=True)
                last.then_inc(f_z, 1)

            def update(c, i, b):
                pe.wait_ge(f_zT_sb, c + 1)
                after(pe, f_y, c - 1)
                for j in range(CH):
                    last = nc.tensor.matmul(ps[0:NP, 5 + 2 * b, j * C:(j + 1) * C], xT[b][:, j * NP:(j + 1) * NP], wu2[:, :],
                                            start=True, stop=True)
                last.then_inc(f_o, 1)

            def end_chunk(c, i, b):
                sums_T(c, i, b)
                if not first_chunk(c):
                    hidden_T(*chunk_before(c, i, b))
                hidden(c, i, b)
                if not first_chunk(c):
                    update(*chunk_before(c, i, b))

            over_chunks(pe, end_chunk)
            hidden_T(*LAST)
            update(*LAST)

        @block.scalar
        def _(act):
            def of_nodes(b):
                return xT[b][0:C, :].rearrange("p (j n) -> p j n", j=CH)

            def from_bank(bank):
                return flat[0:C, bank * BANK:bank * BANK + CH * P].rearrange("p (j n) -> p j n", j=CH)[:, :, 0:NP]

            act.sem_inc(a_relu, ONE)
            act.sem_inc(L1.H_relu, ONE)
            act.wait_ge(dst_in, 32)
            nc.scalar.copy(base_f[:, :], base_i[:, :]).then_inc(base_cast, 1)
            nc.scalar.copy(rel[:, 0:G * TG], relraw).then_inc(base_cast, 1)
            act.wait_ge(const_ready, N_CONSTS)
            nc.scalar.copy(ident_b[:, :], ident[:, :]).then_inc(identb_ready, 1)

            def copy_T(k, c, b):
                act.wait_ge(xs_T[k], c + 1)
                nc.scalar.copy(of_nodes(b), from_bank(0)).then_inc(xT_ready[k], 1)

            def unload_chunk(k, c, i, b):
                act.wait_ge(proj_done[k], c + 1)
                after(act, u_out[k][b], 16 * i)
                after(act, v_out[k][b], 16 * i)
                nc.scalar.copy(u_st[b][:, :], ps[0:NP, 2 + 3 * b, 0:CHC])
                nc.scalar.copy(v_st[b][:, :, 0, :], ps[0:NP, 3 + 3 * b, 0:CHC].rearrange("p (a b) -> p a b", b=C))
                third = h_all[:, bass.ds(c * CHC, CHC)]
                if k == 0:
                    nc.scalar.activation(third, ps[0:NP, 4 + 3 * b, 0:CHC], ACT.Relu).then_inc(uhm_ready[k], 1)
                else:
                    nc.scalar.copy(third, ps[0:NP, 4 + 3 * b, 0:CHC]).then_inc(uhm_ready[k], 1)
                if k == 0:
                    act.wait_ge(uhm_ready[k], c + 1)
                act.wait_ge(r1_ready[k], c + 1)
                nc.scalar.copy(v_st[b][:, :, 1, :], r1[b][:, :].rearrange("p (a b) -> p a b", b=C)).then_inc(mid_ready[k], 1)
                if k == 0:
                    nc.scalar.activation(h_sq[b][:, :], third, ACT.Square).then_inc(squared, 1)

            def x_chunk(c, i, b):
                copy_T(0, c, b)
                if not first_chunk(c):
                    unload_chunk(0, *chunk_before(c, i, b))

            over_chunks(act, x_chunk)
            unload_chunk(0, *LAST)

            def coefficient_root(n):
                act.wait_ge(root_wanted, n)
                nc.scalar.activation(stat[:, ROOT:ROOT + 1], stat[:, VAR:VAR + 1], ACT.Sqrt).then_inc(root_ready, 1)

            def load_attributes(i):
                act.dma_start(eas[:, :, :].rearrange("p t k -> p (t k)"), edge4_v[bass.ds(i, 1), :, :].rearrange("a p n -> (a p) n"))\
                   .then_inc(ea_in, 16)

            def copy_attributes_T(m):
                act.wait_ge(eaT_done, m + 1)
                whole = (NB - 1) * P
                nc.scalar.copy(eaT[:, 0:whole], flat_b[0:RB, 0:whole])
                rest = (TG - (NB - 1) * TR) * RT
                nc.scalar.copy(eaT[0:rest, whole:], flat_b[0:rest, whole:whole + P]).then_inc(eaT_sb, 1)

            def hidden_relu(j, bank):
                return nc.scalar.activation(heT[0:C, j, :], flat[0:C, bank * BANK:bank * BANK + ST * P], ACT.Relu,
                                            bias=cols[:, BE:BE + 1])

            load_attributes(0)
            coefficient_root(1)
            copy_attributes_T(0)

            def statistics_group(i, next_group):
                act.wait_ge(ea_split, i + 1)
                load_attributes(next_group)
                for j in range(STEPS):
                    n = STEPS * i + j
                    act.wait_ge(a_he, n + 1)
                    act.wait_ge(a_bn, n + 1)
                    hidden_relu(j, 2 + 2 * (j % 2)).then_inc(a_relu, 1)
                copy_attributes_T(i + 1)

            with act.Fori(0, G - 1) as i:
                statistics_group(i, i + 1)
            statistics_group(G - 1, 0)
            coefficient_root(2)

            def copy_onehot_T(s, n, j, bank):
                act.wait_ge(s.T_done, n + 1)
                nc.scalar.copy(onehotT[:, j, :], flat_b[:, 2 * bank * BANK:2 * bank * BANK + ST * P]).then_inc(s.T_copied, 1)

            s = L0

            def first_of(i):
                return act.value_load(dst[bass.ds(i * GE, 1)].unsqueeze(0), min_val=0, max_val=N - 1)

            def load_window(first):
                act.dma_start(win_ld[:, :], drows[0][bass.ds(first, P), :]).then_inc(s.win_in, 16)

            def dequeue(i, j):
                act.wait_ge(stored[j], 16 * (i + 1))
                act.dma_start(pre[:, j, :], queue[bass.ds(i, 1), :, j * STC:(j + 1) * STC].rearrange("a p n -> (a p) n"))\
                   .then_inc(rows_in[j], 16)

            def HE(n, j):
                act.wait_ge(H_done, n + 1)
                hidden_relu(j, 4).then_inc(s.H_relu, 1)

            def store_sums(i):
                first = first_of(i)
                act.wait_ge(s.sums_out, 16 * (N_ZEROS + i))
                act.wait_ge(s.seg_out, i + 2)
                act.dma_start(sums[0][bass.ds(first, P), :], seg_sb[:, :]).then_inc(s.sums_out, 16)

            first = first_of(0)
            for b in range(2):
                act.wait_ge(v_out[0][b], 16 * (NCH // 2))
            act.wait_ge(zero_in, 32)
            load_window(first)
            act.wait_ge(chunk_summed, NCH)
            AHEAD = 3
            for j in range(AHEAD):
                dequeue(0, j)
            copy_onehot_T(s, 0, 0, 7)
            HE(0, 0)

            def message_relu(n, j):
                act.wait_ge(s.rows_used, ONE + n + 1)
                nc.scalar.activation(hm[:, j, :, 0:C], pre[:, j, :].rearrange("p (a b) -> p a b", b=C), ACT.Relu)\
                  .then_inc(h_ready, 1)

            def message_square(n, j):
                act.wait_ge(h_ready, n + 1)
                nc.scalar.activation(pre[:, j, :].rearrange("p (a b) -> p a b", b=C), hm[:, j, :, 0:C], ACT.Square)\
                  .then_inc(msg_squared, 1)

            def layer0_group(i, first, last):
                act.wait_ge(ea_split, G + i + 1)
                load_attributes(0 if last else i + 1)
                start = first_of(0 if last else i + 1)
                act.wait_ge(s.win_ready, i + 1)
                load_window(start)
                for j in range(STEPS):
                    n = STEPS * i + j
                    m, _, slot = step_before(i, j)
                    before = not (first and j == 0)
                    if before:
                        message_relu(m, slot)
                    copy_onehot_T(s, n + 1, (j + 1) % STEPS, 7)
                    HE(n + 1, (j + 1) % STEPS)
                    if before:
                        message_square(m, slot)
                    if j == STEPS - 2:
                        copy_attributes_T(G + i + 1)
                    if not (last and j + AHEAD >= STEPS):
                        after(act, msg_added, n - 1)
                        dequeue(i + (j + AHEAD) // STEPS, (j + AHEAD) % STEPS)
                    if j == 2 and not first:
                        store_sums(i - 1)

            over_groups(act, layer0_group)
            message_relu(STEPS * G - 1, STEPS - 1)
            message_square(STEPS * G - 1, STEPS - 1)
            store_sums(G - 1)
            coefficient_root(3)

            def take_root(k, c, b):
                act.wait_ge(norm_eps, NCH * k + c + 1)
                nc.scalar.activation(ln_rs[b][:, :], ln_mv[b][:, :, 1], ACT.Sqrt).then_inc(norm_root, 1)

            def norm_apply(k, c, b, to):
                act.wait_ge(norm_scaled, NCH * k + c + 1)
                for j in range(CH):
                    last = nc.scalar.activation(to[b][:, j * C:(j + 1) * C], y_ch[b][:, j * C:(j + 1) * C], ACT.Identity,
                                                bias=ln_nb[b][:, j:j + 1], scale=ln_rs[b][:, j:j + 1])
                last.then_inc(norm_done, 1)

            def middle_chunk(c, i, b):
                take_root(0, c, b)
                after(act, h1_out[b], 16 * i)
                norm_apply(0, c, b, xs)
                copy_T(1, c, b)
                if not first_chunk(c):
                    unload_chunk(1, *chunk_before(c, i, b))

            over_chunks(act, middle_chunk)
            unload_chunk(1, *LAST)

            s = L1
            copy_onehot_T(s, 0, 0, 0)
            with act.Fori(0, G) as i:
                for j in range(STEPS):
                    n = STEPS * i + j
                    copy_onehot_T(s, n + 1, (j + 1) % STEPS, 0)
                    act.wait_ge(s.rows_used, ONE + n + 1)
                    at = (2 + 2 * (j % 2)) * BANK
                    nc.scalar.activation(heT[0:C, j, :], flat[0:C, at:at + ST * P], ACT.Relu).then_inc(s.H_relu, 1)

            def end_chunk(c, i, b):
                act.wait_ge(f_T, c + 1)
                nc.scalar.copy(of_nodes(b), from_bank(0)).then_inc(f_mT, 1)
                if not first_chunk(c):
                    end_norm(*chunk_before(c, i, b))

            def end_norm(c, i, b):
                act.wait_ge(f_zT, c + 1)
                nc.scalar.copy(of_nodes(b), from_bank(2)).then_inc(f_zT_sb, 1)
                take_root(1, c, b)
                after(act, o_out[b], 16 * i)
                norm_apply(1, c, b, u_st)

            over_chunks(act, end_chunk)
            end_norm(*LAST)

        @block.vector
        def _(dve):
            chain = [0]

            def link(ins):
                chain[0] += 1
                ins.then_inc(link_v, 1)
                dve.wait_ge(link_v, chain[0])

            def step(ins, s, value):
                ins.then_inc(s, 1)
                dve.wait_ge(s, value)

            dve.sem_inc(a_bn, STEPS)
            dve.sem_inc(L0.rows_used, ONE)
            dve.sem_inc(P_out, ONE)

            for b in range(2):
                nc.vector.memset(xT[b][C:C1, :], 1.0)
            nc.vector.memset(heT[C:C1, :, :], 1.0).then_inc(bias_rows, 1)

            def col(i):
                return stat[:, i:i + 1]

            dve.wait_ge(const_ready, N_CONSTS)
            nc.vector.tensor_copy(iota[:, :], iota_i[:, :])
            nc.vector.tensor_copy(iotap[:, :], iotap_i[:, :])
            dve.wait_ge(base_bc, 1)
            link(nc.vector.tensor_copy(base_all[:, :], ps[:, 7, 0:G]))
            dve.wait_ge(base_cast, 2)
            r3 = rel[:, 0:G * TG].rearrange("p (g t) -> p g t", t=TG)
            nc.vector.tensor_tensor(r3, r3, base_all[:, :].unsqueeze(2).to_broadcast([P, G, TG]), ALU.subtract).then_inc(rel_ready, 1)
            link(nc.vector.tensor_tensor(carry_all[:, 1:G], base_all[:, 1:G], base_all[:, 0:G - 1], ALU.subtract))
            nc.vector.memset(carry_all[:, G:G + 1], 0.0)
            link(nc.vector.tensor_scalar(carry_all[:, 1:G], carry_all[:, 1:G], iotap[:, :], None, ALU.is_equal))
            nc.vector.tensor_scalar(kept_all[:, :], carry_all[:, 1:G + 1], -1.0, 1.0, ALU.mult, ALU.add)

            dve.wait_ge(param_in, 16 * len(PARAMS))
            link(nc.vector.reduce_sum(pm[:, :, :].rearrange("p r b -> p (r b)"),
                                      part_mask[:, :, :, :].rearrange("p r b a -> p (r b) a"), AX.X))
            link(nc.vector.tensor_copy(we_b[:, 0, :], we_rep[:, :]))
            link(nc.vector.tensor_tensor(we_r[:, :], we_rep[:, :], we_b[:, 0, :], ALU.subtract))
            link(nc.vector.tensor_copy(we_b[:, 1, :], we_r[:, :]))
            link(nc.vector.tensor_tensor(we_b[:, 2, :], we_r[:, :], we_b[:, 1, :], ALU.subtract))
            for r in range(TR):
                link(nc.vector.tensor_scalar(we_acc[:, :], we_b[:, 0, :], pm[:, r, 0:1], None, ALU.mult))
                link(nc.vector.scalar_tensor_tensor(we_acc[:, :], we_b[:, 1, :], pm[:, r, 1:2], we_acc[:, :], ALU.mult, ALU.add))
                link(nc.vector.scalar_tensor_tensor(we_blk[:, r, :], we_b[:, 2, :], pm[:, r, 2:3], we_acc[:, :], ALU.mult, ALU.add))
            nc.vector.memset(acc_sum[:, :], 0.0)
            nc.vector.memset(acc_sq[:, :], 0.0).then_inc(we_ready, 1)

            def split_chunk(k, c, b):
                dve.wait_ge(uhm_ready[k], c + 1)
                rv = r1[b][:, :].rearrange("p (a b) -> p a b", b=C)
                nc.vector.tensor_tensor(rv, ps[0:NP, 3 + 3 * b, 0:CHC].rearrange("p (a b) -> p a b", b=C), v_st[b][:, :, 0, :],
                                        ALU.subtract).then_inc(r1_ready[k], 1)
                if k == 0:
                    nc.vector.reduce_sum(hsum[:, bass.ds(c, 1), :].rearrange("p a c -> p (a c)"),
                                         h_all[:, bass.ds(c * CHC, CHC)].rearrange("p (a c) -> p c a", c=C), AX.X)
                dve.wait_ge(mid_ready[k], c + 1)
                nc.vector.tensor_tensor(v_st[b][:, :, 2, :], rv, v_st[b][:, :, 1, :], ALU.subtract).then_inc(low_ready[k], 1)
                if k == 0:
                    dve.wait_ge(squared, c + 1)
                    nc.vector.reduce_sum(hsqsum[:, bass.ds(c, 1), :].rearrange("p a c -> p (a c)"),
                                         h_sq[b][:, :].rearrange("p (a c) -> p c a", c=C), AX.X).then_inc(chunk_summed, 1)

            over_chunks(dve, lambda c, i, b: split_chunk(0, c, b))
            roots = [0]

            def coefficients(gamma, beta):
                nc.vector.tensor_scalar(col(VAR), col(VAR), 0.0, EPS, ALU.max, ALU.add).then_inc(root_wanted, 1)
                roots[0] += 1
                dve.wait_ge(root_ready, roots[0])
                link(nc.vector.reciprocal(col(TMP), col(ROOT)))
                link(nc.vector.tensor_tensor(col(SCALE), col(TMP), cols[:, gamma:gamma + 1], ALU.mult))
                link(nc.vector.tensor_tensor(col(TMP), col(SCALE), col(MEAN), ALU.mult))
                link(nc.vector.tensor_tensor(col(SHIFT), cols[:, beta:beta + 1], col(TMP), ALU.subtract))

            def coefficients_of_sums(total, squares, count, gamma, beta):
                link(nc.vector.tensor_scalar(col(MEAN), total, 1.0 / count, None, ALU.mult))
                link(nc.vector.tensor_scalar(col(VAR), squares, 1.0 / count, None, ALU.mult))
                link(nc.vector.tensor_tensor(col(TMP), col(MEAN), col(MEAN), ALU.mult))
                link(nc.vector.tensor_tensor(col(VAR), col(VAR), col(TMP), ALU.subtract))
                coefficients(gamma, beta)

            def spread(nth):
                nc.vector.tensor_scalar(diag[:, 0, :], ident[0:C, 0:C], col(SCALE), None, ALU.mult)
                nc.vector.tensor_scalar(diag[:, 1, :], ident[0:C, 0:C], col(SHIFT), None, ALU.mult).then_inc(diag_ready, 1)
                dve.wait_ge(rows_spread, nth)
                step(nc.vector.tensor_copy(rows[:, :, :].rearrange("p a b -> p (a b)"), ps[0:NP, 7, 0:2 * C]), rows_read, nth)

            dve.wait_ge(chunk_summed, NCH)
            link(nc.vector.reduce_sum(part_sums[0:NP, 0, :], hsum.rearrange("p n c -> p c n"), AX.X))
            nc.vector.reduce_sum(part_sums[0:NP, 1, :], hsqsum.rearrange("p n c -> p c n"), AX.X).then_inc(sums_wanted, 1)
            dve.wait_ge(node_sums, 1)
            coefficients_of_sums(ps[0:C, 7, 0:1], ps[0:C, 7, 1:2], N, GN, BN)
            spread(1)

            def beside(a):
                return a.unsqueeze(2).to_broadcast([P, TG, PARTS, KE])

            def split_high(m):
                dve.wait_ge(ea_in, 16 * (m + 1))
                after(dve, eaT_done, m)
                step(nc.vector.tensor_copy(ea9[:, :, 0, :, :], beside(eas[:, :, :])), ea_hi, m + 1)
                nc.vector.tensor_tensor(ea_r[:, :, :], eas[:, :, :], ea9[:, :, 0, 0, :], ALU.subtract).then_inc(ea_rest, 1)

            def split_rest(m):
                dve.wait_ge(ea_rest, m + 1)
                step(nc.vector.tensor_copy(ea9[:, :, 1, :, :], beside(ea_r[:, :, :])), ea_mid, m + 1)
                nc.vector.tensor_tensor(ea9[:, :, 2, :, :], beside(ea_r[:, :, :]), ea9[:, :, 1, :, :], ALU.subtract)\
                  .then_inc(ea_split, 1)

            split_high(0)
            split_rest(0)
            half = ST * P // 2
            with dve.Fori(0, G) as i:
                for j in range(STEPS):
                    dve.wait_ge(a_relu, ONE + STEPS * i + j + 1)
                    nc.vector.bn_stats(bn_edge[:, 2 * j, :], heT[0:C, j, 0:half])
                    nc.vector.bn_stats(bn_edge[:, 2 * j + 1, :], heT[0:C, j, half:2 * half]).then_inc(a_bn, 1)
                    if j == 2:
                        split_high(i + 1)
                    if j == 3:
                        split_rest(i + 1)
                dve.wait_ge(a_bn, STEPS * (i + 2))
                dve.sem_inc(a_turn, 1)
                step(nc.vector.bn_aggr(mv_group[:, :], bn_edge[:, :, :].rearrange("p a b -> p (a b)")), a_mv, 2 * i + 1)
                nc.vector.tensor_copy(mv_edge[:, bass.ds(i, 1), :].rearrange("p a b -> p (a b)"), mv_group[:, :]).then_inc(a_mv, 1)
            dve.wait_ge(a_mv, 2 * G)
            link(nc.vector.reduce_sum(col(MEAN), mv_edge[:, :, 0], AX.X))
            link(nc.vector.reduce_sum(col(TMP), mv_edge[:, :, 1], AX.X))
            link(nc.vector.tensor_scalar(col(MEAN), col(MEAN), 1.0 / G, None, ALU.mult))
            link(nc.vector.tensor_scalar(mv_edge[:, :, 0], mv_edge[:, :, 0], col(MEAN), None, ALU.subtract))
            link(nc.vector.tensor_tensor(mv_edge[:, :, 1], mv_edge[:, :, 0], mv_edge[:, :, 0], ALU.mult))
            link(nc.vector.reduce_sum(col(VAR), mv_edge[:, :, 1], AX.X))
            link(nc.vector.tensor_tensor(col(VAR), col(VAR), col(TMP), ALU.add))
            link(nc.vector.tensor_scalar(col(VAR), col(VAR), 1.0 / G, None, ALU.mult))
            coefficients(GEDGE, BEDGE)
            link(nc.vector.tensor_scalar(wc1[0:C, :], wc[:, :], col(SCALE), None, ALU.mult))
            nc.vector.tensor_copy(ce_lhs[:, C:C1], col(SHIFT)).then_inc(ce_ready, 1)
            dve.wait_ge(ce_done, 1)
            nc.vector.tensor_tensor(wc1[C:C1, :], ps[C:C1, 7, 0:C], bmsg_row[C:C1, :], ALU.add).then_inc(wc1_ready, 1)

            def make_onehot(s, n, j):
                dve.wait_ge(s.onehot_used, n + 1)
                nc.vector.tensor_tensor(onehot[:, j, :].rearrange("p (t w) -> p t w", w=P),
                                        iota[:, :].unsqueeze(1).to_broadcast([P, ST, P]),
                                        rel[:, bass.ds(n * ST, ST)].unsqueeze(2).to_broadcast([P, ST, P]),
                                        ALU.is_equal).then_inc(s.onehot_ready, 1)

            def copy_window(s, i):
                dve.wait_ge(s.win_in, 16 * (i + 1))
                nc.vector.tensor_copy(win[:, :], win_ld[:, :]).then_inc(s.win_ready, 1)

            def add_features(i):
                xt, ht = x_all[:, bass.ds(i * C, C)], h_all[:, bass.ds(i * C, C)]
                step(nc.vector.tensor_tensor(ht, ht, rows[:, 0, :], ALU.mult), xn_scaled, i + 1)
                step(nc.vector.tensor_tensor(xt, xt, ht, ALU.add), xn_added, i + 1)
                nc.vector.tensor_tensor(xt, xt, rows[:, 1, :], ALU.add).then_inc(xn_done, 1)

            def next_window(s, i):
                if s is L0:
                    dve.wait_ge(s.P_done, STEPS * (i + 1))
                else:
                    dve.wait_ge(s.rows_used, ONE + STEPS * (i + 1))
                copy_window(s, i + 1)

            def take_sums(k, i):
                s = L[k]
                dve.wait_ge(s.onehot_used, STEPS * (i + 2))
                dve.wait_ge(s.sums_out, 16 * (N_ZEROS + i))
                nc.vector.tensor_copy(seg_sb[:, 0:WIDTH[k]], ps[:, 6, 0:WIDTH[k]])
                if k == 0:
                    nc.vector.scalar_tensor_tensor(acc_sum[:, :], ps[:, 6, 0:C1], kept_all[:, bass.ds(i, 1)], acc_sum[:, :],
                                                   ALU.mult, ALU.add)
                nc.vector.tensor_copy(carry[:, 0:1], carry_all[:, bass.ds(i + 1, 1)]).then_inc(s.seg_out, 1)

            def add_squares(n, j):
                dve.wait_ge(msg_squared, n + 1)
                after(dve, msg_added, n)
                nc.vector.tensor_tensor(acc_sq[:, :], acc_sq[:, :], pre[:, j, :], ALU.add).then_inc(msg_added, 1)

            def layer0_group(i, first, features):
                s = L0
                for j in range(STEPS):
                    n = STEPS * i + j
                    make_onehot(s, n + 2, (j + 2) % STEPS)
                    if j == STEPS - 1:
                        next_window(s, i)
                    dve.wait_ge(s.P_done, n + 1)
                    dve.wait_ge(rows_in[j], 16 * (i + 1))
                    nc.vector.tensor_tensor(pre[:, j, :], ps[:, 2 + j % 2, 0:STC], pre[:, j, :], ALU.add).then_inc(s.rows_used, 1)
                    if not (first and j == 0):
                        m, _, slot = step_before(i, j)
                        add_squares(m, slot)
                    if j == 0 and not first:
                        take_sums(0, i - 1)
                    if j == 0:
                        split_high(G + i + 1)
                    if j == 1:
                        split_rest(G + i + 1)
                    if j == 3 and features:
                        add_features(i)

            def scale_messages(n, i, j):
                dve.wait_ge(L1.P_done, n + 1)
                dve.wait_ge(factors_in[j], 16 * (i + 1))
                nc.vector.tensor_tensor(hm[:, j, :, 0:C], ps[:, 7, 0:STC].rearrange("p (a b) -> p a b", b=C),
                                        pre[:, j, :].rearrange("p (a b) -> p a b", b=C), ALU.mult).then_inc(P_out, 1)

            def layer1_group(i, first, last):
                s = L1
                for j in range(STEPS):
                    make_onehot(s, STEPS * i + j + 2, (j + 2) % STEPS)
                    if not (first and j == 0):
                        scale_messages(*step_before(i, j))
                    if j == 1 and not first:
                        take_sums(1, i - 1)
                    if j == STEPS - 1:
                        next_window(s, i)

            def edges(k):
                s = L[k]
                copy_window(s, 0)
                nc.vector.memset(carry[:, 0:1], 0.0)
                nc.vector.memset(seg_sb[:, :], 0.0).then_inc(s.seg_out, 1)
                make_onehot(s, 0, 0)
                make_onehot(s, 1, 1)
                if k == 0:
                    dve.wait_ge(xall_in, 16 * NCH)
                    layer0_group(0, True, True)
                    with dve.Fori(1, NT) as i:
                        layer0_group(i, False, True)
                    with dve.Fori(NT, G) as i:
                        layer0_group(i, False, False)
                    add_squares(STEPS * G - 1, STEPS - 1)
                else:
                    over_groups(dve, layer1_group)
                    scale_messages(STEPS * G - 1, G - 1, STEPS - 1)
                take_sums(k, G - 1)
                dve.wait_ge(s.seg_out, G + 1)

            def norm_stats(k, c, b):
                for j in range(CH):
                    last = nc.vector.bn_stats(ln_bn[b][:, j, :], y_ch[b][:, j * C:(j + 1) * C])
                step(last, norm_bnd, NCH * k + c + 1)
                dve.sem_inc(norm_turn, 1)
                for j in range(CH):
                    last = nc.vector.bn_aggr(ln_mv[b][:, j, :], ln_bn[b][:, j, :])
                step(last, norm_agg, NCH * k + c + 1)
                nc.vector.tensor_scalar(ln_mv[b][:, :, 1], ln_mv[b][:, :, 1], EPS, None, ALU.add).then_inc(norm_eps, 1)

            def norm_scale(k, c, b):
                dve.wait_ge(norm_root, NCH * k + c + 1)
                step(nc.vector.reciprocal(ln_rs[b][:, :], ln_rs[b][:, :]), norm_inv, NCH * k + c + 1)
                nc.vector.scalar_tensor_tensor(ln_nb[b][:, :], ln_mv[b][:, :, 0], -1.0, ln_rs[b][:, :], ALU.mult, ALU.mult)\
                  .then_inc(norm_scaled, 1)

            def middle_chunk(c, i, b):
                dve.wait_ge(s_in[b], 16 * (i + 1))
                y3 = y_ch[b][:, :].rearrange("p (a b) -> p a b", b=C)
                step(nc.vector.tensor_tensor(y3, s_ch[b][:, :, 0:C], rows[:, 0, :].unsqueeze(1).to_broadcast([NP, CH, C]), ALU.mult),
                     y_scaled, c + 1)
                step(nc.vector.tensor_tensor(y_ch[b][:, :], y_ch[b][:, :], x_all[:, bass.ds(c * CHC, CHC)], ALU.add), y_added, c + 1)
                for j in range(CH):
                    last = nc.vector.scalar_tensor_tensor(y3[:, j, :], rows[:, 1, :], s_ch[b][:, j, C:C1], y3[:, j, :],
                                                          ALU.mult, ALU.add)
                step(last, y_ready, c + 1)
                norm_stats(0, c, b)
                norm_scale(0, c, b)
                if not first_chunk(c):
                    pc, _, pb = chunk_before(c, i, b)
                    split_chunk(1, pc, pb)

            def end_norm(c, i, b):
                dve.wait_ge(h1_in[b], 16 * (i + 1))
                dve.wait_ge(f_o, c + 1)
                step(nc.vector.tensor_tensor(y_ch[b][:, :], ps[0:NP, 5 + 2 * b, 0:CHC], y_ch[b][:, :], ALU.add), f_y, c + 1)
                norm_stats(1, c, b)
                norm_scale(1, c, b)

            def end_chunk(c, i, b):
                dve.wait_ge(f_z, c + 1)
                step(nc.vector.tensor_tensor(r1[b][:, :], ps[0:NP, 4 + 2 * b, 0:CHC], h_all[:, bass.ds(c * CHC, CHC)], ALU.add),
                     z_summed, c + 1)
                nc.vector.tensor_scalar(r1[b][:, :], r1[b][:, :], 0.0, None, ALU.max).then_inc(f_zr, 1)
                if not first_chunk(c):
                    end_norm(*chunk_before(c, i, b))

            edges(0)
            dve.wait_ge(msg_added, STEPS * G)
            nc.vector.tensor_copy(part_sums[:, 0, :], acc_sum[:, 0:C])
            nc.vector.reduce_sum(part_sums[:, 1, :], acc_sq[:, :].rearrange("p (a c) -> p c a", c=C), AX.X).then_inc(sums_wanted, 1)
            dve.wait_ge(node_sums, 2)
            coefficients_of_sums(ps[0:C, 7, 0:1], ps[0:C, 7, 1:2], E, GM, BM)
            dve.wait_ge(xn_done, NT)
            spread(2)
            over_chunks(dve, middle_chunk)
            split_chunk(1, LAST[0], LAST[2])
            edges(1)
            over_chunks(dve, end_chunk)
            end_norm(*LAST)


_INS = ["x", "src", "dst", "edge_attr_4", "edge_attr_96", "L0_gnn_W_node", "L0_gnn_b_node", "L0_gnn_g_node",
        "L0_gnn_beta_node", "L0_gnn_W_edge", "L0_gnn_b_edge", "L0_gnn_g_edge", "L0_gnn_beta_edge", "L0_gnn_W_msg",
        "L0_gnn_b_msg", "L0_gnn_g_msg", "L0_gnn_beta_msg", "L1_gnn_Wm1", "L1_gnn_bm1", "L1_gnn_Wm2", "L1_gnn_bm2",
        "L1_gnn_Wu1", "L1_gnn_bu1", "L1_gnn_Wu2", "L1_gnn_bu2"]


def kernel(**inputs):
    import numpy as np
    import concourse.bacc as bacc
    from concourse.bass_utils import run_bass_kernel_spmd

    nc = bacc.Bacc("TRN2", target_bir_lowering=False, num_devices=1)
    arrays, args = {}, []
    for name in _INS:
        a = np.ascontiguousarray(inputs[name])
        arrays[f"in_{name}"] = a
        args.append(nc.dram_tensor(f"in_{name}", a.shape, mybir.dt.from_np(a.dtype), kind="ExternalInput").ap())
    out = nc.dram_tensor("out_nodes", inputs["x"].shape, F32, kind="ExternalOutput").ap()
    build_gnn(nc, *args, out)
    r = run_bass_kernel_spmd(nc, [arrays], core_ids=[0])
    return r.results[0]["out_nodes"]
```

```python
import concourse.bass as bass
from concourse import mybir
from contextlib import ExitStack

F32 = mybir.dt.float32
BF16 = mybir.dt.bfloat16
I32 = mybir.dt.int32
ALU = mybir.AluOpType
ACT = mybir.ActivationFunctionType
AX = mybir.AxisListType

P = 128
BANK = 512
EPS = 1e-5


def build_gnn(nc, x, src, dst, edge4, factors, W_node, b_node, g_node, beta_node, W_edge, b_edge, g_edge,
              beta_edge, W_msg, b_msg, g_msg, beta_msg, Wm1, bm1, Wm2, bm2, Wu1, bu1, Wu2, bu2, out):
    N, C = x.shape
    E, KE = edge4.shape
    STEPS, ST = 5, 5
    TG = STEPS * ST
    GE = TG * P
    G = E // GE
    NT, CH = 100, 5
    NP = N // NT
    NCH = NT // CH
    assert G * GE == E and G % 2 == 1 and NP * NT == N and NP <= P and NCH % 2 == 0 and NT <= G
    C1 = C + 1
    STC = ST * C
    CHC = CH * C
    NR = N + P
    PARTS = 3
    RT = PARTS * PARTS * KE
    TR = P // RT
    NB = -(-TG // TR)
    RB = TR * RT

    src_v = src.rearrange("(g p t) -> g p t", p=P, t=TG)
    dst_v = dst.rearrange("(g p t) -> p g t", p=P, t=TG)
    edge4_v = edge4.rearrange("(g p t) k -> g p (t k)", p=P, t=TG)
    factors_v = factors.rearrange("(g p t) c -> g p (t c)", p=P, t=TG)
    x_v = x.rearrange("(p j) c -> p (j c)", j=NT)
    out_v = out.rearrange("(p j) c -> p (j c)", j=NT)

    def dram(name, shape, dt=F32):
        return nc.dram_tensor(name, shape, dt, kind="Internal").ap()

    srows = [dram(f"source_rows{k}", (N, C)) for k in range(2)]
    drows = [dram(f"dest_rows{k}", (NR, PARTS * C), BF16) for k in range(2)]
    sums = [dram("sums0", (NR, C1)), dram("sums1", (NR, C))]
    h1_dram = dram("h1_rows", (N, C))
    queue = dram("gathered_queue", (G, P, TG * C))
    srows_v = [t.rearrange("(p j) c -> p (j c)", j=NT) for t in srows]
    drows_v = [t[0:N, :].rearrange("(p j) c -> p (j c)", j=NT) for t in drows]
    sums_v = [t[0:N, :].rearrange("(p j) c -> p (j c)", j=NT) for t in sums]
    h1_v = h1_dram.rearrange("(p j) c -> p (j c)", j=NT)
    WIDTH = (C1, C)

    ctx = ExitStack()
    with ctx:
        def sb(name, shape, dt=F32):
            return ctx.enter_context(nc.sbuf_tensor(name, shape, dt))

        def sem(name):
            return ctx.enter_context(nc.semaphore(name))

        ident = sb("ident", [P, P])
        ident_b = sb("ident_b", [P, P], BF16)
        ones = sb("ones", [P, P])
        iota_i = sb("iota_i", [P, P], I32)
        iota = sb("iota", [P, P])
        iotap_i = sb("iotap_i", [P, 1], I32)
        iotap = sb("iotap", [P, 1])
        zeros = sb("zeros", [P, CH * C1])
        rel = sb("rel", [P, (G + 1) * TG])
        base_i = sb("base_i", [1, G], I32)
        base_f = sb("base_f", [1, G])
        base_all = sb("base_all", [P, G])
        carry_all = sb("carry_all", [P, G + 1])
        kept_all = sb("kept_all", [P, G])
        part_mask = sb("part_mask", [RB, TR, PARTS, PARTS])
        pm = sb("pm", [RB, TR, PARTS])
        we_rep = sb("we_rep", [RB, C])
        we_r = sb("we_r", [RB, C])
        we_acc = sb("we_acc", [RB, C])
        we_b = sb("we_b", [RB, PARTS, C], BF16)
        we_blk = sb("we_blk", [RB, TR, C], BF16)
        proj_w = [sb(f"proj_w{k}", [C1, 3 * C]) for k in range(2)]
        wc = sb("wc", [C, C])
        wc1 = sb("wc1", [C1, C])
        bmsg_row = sb("bmsg_row", [C1, C])
        wm2 = sb("wm2", [C1, C])
        wu1b = sb("wu1b", [C, C])
        wu2 = sb("wu2", [C1, C])
        cols = sb("cols", [C, 8])
        stat = sb("stat", [C, 16])
        ce_lhs = sb("ce_lhs", [C, C1])
        diag = sb("diag", [C, 2, C])
        rows = sb("rows", [NP, 2, C])
        bn_edge = sb("bn_edge", [C, 2, 2 * STEPS, 6])
        mv_group = sb("mv_group", [C, 2])
        mv_edge = sb("mv_edge", [C, G, 2])
        part_sums = sb("part_sums", [P, 2, C])
        acc_sum = sb("acc_sum", [P, C1])
        acc_sq = sb("acc_sq", [P, STC])

        x_all = sb("x_all", [NP, NT * C])
        h_all = sb("h_all", [NP, NT * C])
        xs = [sb(f"xs{b}", [NP, CHC]) for b in range(2)]
        xT = [sb(f"xT{b}", [C1, CH * NP]) for b in range(2)]
        u_st = [sb(f"u_st{b}", [NP, CHC]) for b in range(2)]
        v_st = [sb(f"v_st{b}", [NP, CH, PARTS, C], BF16) for b in range(2)]
        r1 = [sb(f"r1{b}", [NP, CHC]) for b in range(2)]
        s_ch = [sb(f"s_ch{b}", [NP, CH, C1]) for b in range(2)]
        h_sq = [t[:, :, :].rearrange("p a b -> p (a b)")[:, 0:CHC] for t in s_ch]
        y_ch = [sb(f"y_ch{b}", [NP, CHC]) for b in range(2)]
        ln_bn = [sb(f"ln_bn{b}", [NP, CH, 6]) for b in range(2)]
        ln_mv = [sb(f"ln_mv{b}", [NP, CH, 2]) for b in range(2)]
        ln_rs = [sb(f"ln_rs{b}", [NP, CH]) for b in range(2)]
        ln_nb = [sb(f"ln_nb{b}", [NP, CH]) for b in range(2)]

        idx = sb("idx", [P, STEPS, ST], I32)
        grows = sb("grows", [P, STEPS, STC])
        onehot = sb("onehot", [P, STEPS, ST * P])
        onehotT = sb("onehotT", [P, STEPS, ST * P], BF16)
        eas = sb("eas", [P, TG, KE])
        ea_r = sb("ea_r", [P, TG, KE])
        ea9 = sb("ea9", [P, TG, PARTS, PARTS, KE], BF16)
        eaT = sb("eaT", [RB, 2, NB * P], BF16)
        heT = sb("heT", [C1, STEPS, ST * P])
        pre = sb("pre", [P, STEPS, STC])
        hm = sb("hm", [P, STEPS, ST, C1])
        win_ld = sb("win_ld", [P, PARTS * C], BF16)
        win = sb("win", [P, PARTS * C], BF16)
        seg_sb = sb("seg_sb", [P, C1])
        carry = sb("carry", [P, P])
        relraw = onehot[:, :, :].rearrange("p s n -> p (s n)")[:, 0:G * TG].bitcast(I32)
        hsum = pre[:, :, :].rearrange("p s n -> p (s n)")[0:NP, 0:NCH * C].rearrange("p (n c) -> p n c", c=C)
        hsqsum = onehot[:, :, :].rearrange("p s n -> p (s n)")[0:NP, 0:NCH * C].rearrange("p (n c) -> p n c", c=C)

        ps = ctx.enter_context(nc.psum_tensor("ps", [P, 8, BANK], F32))
        flat = ps[:, :, :].rearrange("p b n -> p (b n)")
        flat_b = flat.bitcast(BF16)

        link_v = sem("link_v")
        wa_in = sem("wa_in")
        const_ready = sem("const_ready")
        bias_rows = sem("bias_rows")
        identb_ready = sem("identb_ready")
        zero_w, zero_in, param_in, dst_in, xall_in = (sem(n) for n in ("zero_w", "zero_in", "param_in", "dst_in", "xall_in"))
        base_cast, base_bc, rel_ready, we_ready = (sem(n) for n in ("base_cast", "base_bc", "rel_ready", "we_ready"))
        xs_in = [sem(f"xs_in{b}") for b in range(2)]
        xs_T, xT_ready, proj_done, u_ready = sem("xs_T"), sem("xT_ready"), sem("proj_done"), sem("u_ready")
        vh_ready = [sem(f"vh_ready{k}") for k in range(2)]
        r1_ready = [sem(f"r1_ready{k}") for k in range(2)]
        mid_ready = [sem(f"mid_ready{k}") for k in range(2)]
        low_ready = [sem(f"low_ready{k}") for k in range(2)]
        u_out = [sem(f"u_out{b}") for b in range(2)]
        v_out = [sem(f"v_out{b}") for b in range(2)]
        squared, chunk_summed, node_sums = sem("squared"), sem("chunk_summed"), sem("node_sums")
        root_wanted, root_ready = sem("root_wanted"), sem("root_ready")
        sums_wanted, diag_ready, rows_spread = sem("sums_wanted"), sem("diag_ready"), sem("rows_spread")
        rows_read = sem("rows_read")
        ce_ready, ce_done, wc1_ready = sem("ce_ready"), sem("ce_done"), sem("wc1_ready")
        ea_in, ea_hi, ea_rest, ea_mid, ea_split, eaT_done, eaT_sb = (sem(n) for n in (
            "ea_in", "ea_hi", "ea_rest", "ea_mid", "ea_split", "eaT_done", "eaT_sb"))
        a_he, a_relu, a_bn, a_turn, a_mv = (sem(n) for n in ("a_he", "a_relu", "a_bn", "a_turn", "a_mv"))
        xn_scaled, xn_added, xn_done = (sem(n) for n in ("xn_scaled", "xn_added", "xn_done"))

        class EdgeSems:

            def __init__(self, k):
                self.rows_used = sem(f"rows_used{k}")
                self.onehot_ready = sem(f"onehot_ready{k}")
                self.onehot_used = sem(f"onehot_used{k}")
                self.T_done = sem(f"T_done{k}")
                self.T_copied = sem(f"T_copied{k}")
                self.H_relu = sem(f"H_relu{k}")
                self.P_done = sem(f"P_done{k}")
                self.win_in = sem(f"win_in{k}")
                self.win_ready = sem(f"win_ready{k}")
                self.seg_out = sem(f"seg_out{k}")
                self.sums_out = sem(f"sums_out{k}")
                self.turn = sem(f"turn{k}")

        L0, L1 = L = (EdgeSems(0), EdgeSems(1))
        idx_in = [sem(f"idx_in{j}") for j in range(STEPS)]
        gathered = [sem(f"gathered{j}") for j in range(STEPS)]
        stored = [sem(f"stored{j}") for j in range(STEPS)]
        rows_in = [sem(f"rows_in{j}") for j in range(STEPS)]
        H_done, h_ready = sem("H_done"), sem("h_ready")
        factors_in = [sem(f"factors_in{j}") for j in range(STEPS)]
        P_out = sem("P_out")
        msg_squared, msg_added = sem("msg_squared"), sem("msg_added")
        s_in = [sem(f"s_in{b}") for b in range(2)]
        y_scaled, y_added, y_ready, z_summed = (sem(n) for n in ("y_scaled", "y_added", "y_ready", "z_summed"))
        h1_out = [sem(f"h1_out{b}") for b in range(2)]
        m_in = [sem(f"m_in{b}") for b in range(2)]
        h1_in = [sem(f"h1_in{b}") for b in range(2)]
        o_out = [sem(f"o_out{b}") for b in range(2)]
        f_T, f_mT, f_z, f_zr, f_zT, f_zT_sb, f_o, f_y = (sem("f_" + n) for n in ("T", "mT", "z", "zr", "zT", "zT_sb", "o", "y"))

        norm_bnd, norm_turn, norm_agg, norm_eps, norm_root, norm_inv, norm_scaled, norm_done = (
            sem("norm_" + n) for n in ("bnd", "turn", "agg", "eps", "root", "inv", "scaled", "done"))

        PARAMS = [(proj_w[0][0:C, 0:C], W_msg[0:C, :]), (proj_w[0][0:C, C:2 * C], W_msg[C:2 * C, :]),
                  (proj_w[0][0:C, 2 * C:3 * C], W_node), (proj_w[0][C:C1, 2 * C:3 * C], b_node.unsqueeze(0)),
                  (proj_w[1][0:C, 0:C], Wm1[0:C, :]), (proj_w[1][0:C, C:2 * C], Wm1[C:2 * C, :]),
                  (proj_w[1][0:C, 2 * C:3 * C], Wu1[0:C, :]), (proj_w[1][C:C1, C:2 * C], bm1.unsqueeze(0)),
                  (proj_w[1][C:C1, 2 * C:3 * C], bu1.unsqueeze(0)),
                  (wc[:, :], W_msg[2 * C:3 * C, :]), (bmsg_row[C:C1, :], b_msg.unsqueeze(0)),
                  (wm2[0:C, :], Wm2), (wm2[C:C1, :], bm2.unsqueeze(0)), (wu1b[:, :], Wu1[C:2 * C, :]),
                  (wu2[0:C, :], Wu2), (wu2[C:C1, :], bu2.unsqueeze(0))]
        PARAMS += [(cols[:, i:i + 1], v.unsqueeze(1)) for i, v in
                   enumerate((b_edge, g_edge, beta_edge, g_node, beta_node, g_msg, beta_msg))]
        PARAMS += [(we_rep[KE * t:KE * (t + 1), :], W_edge) for t in range(RB // KE)]
        BE, GEDGE, BEDGE, GN, BN, GM, BM = range(7)
        MEAN, SCALE, SHIFT, VAR, ROOT, TMP = range(6)
        ONE, A0 = 1, 2
        N_ZEROS = NCH + 1
        N_CONST = 9
        N_CONSTS = N_CONST + 5

        def after(eng, s, value):
            if not (isinstance(value, int) and value <= 0):
                eng.wait_ge(s, value)

        LB = G % 2
        PEEL = 2

        def over_chunks(eng, body, tail=0):
            def pair(i):
                for b in range(2):
                    body(2 * i + b, i, b)
            for i in range(PEEL):
                pair(i)
            with eng.Fori(PEEL, NCH // 2 - 1) as i:
                pair(i)
            pair(NCH // 2 - 1)
            for c in range(NCH, NCH + tail):
                body(c, c // 2, c % 2)

        def lagging(stage, lag, c, i, b):
            if not isinstance(c, int):
                stage(c - lag, i - (lag - b + 1) // 2, (b - lag) % 2)
            elif 0 <= c - lag < NCH:
                stage(c - lag, (c - lag) // 2, (c - lag) % 2)

        def chunk_before(c, i, b):
            return c - 1, (i if b else i - 1), 1 - b

        def first_chunk(c):
            return isinstance(c, int) and c == 0

        LAST = (NCH - 1, NCH // 2 - 1, 1)

        def over_pairs(eng, body, pairs):
            with eng.Fori(0, pairs) as q:
                for b in range(2):
                    body(2 * q + b, b)

        def step_before(i, j, lag=1):
            back = int(j < lag)
            return STEPS * i + j - lag, i - back, (j - lag) % STEPS

        def over_groups(eng, body):
            body(0, True, False)
            with eng.Fori(1, G - 1) as i:
                body(i, False, False)
            body(G - 1, False, True)

        def load_x(eng, c, b):
            eng.dma_start(xs[b][:, :], x_v[:, bass.ds(c * CHC, CHC)]).then_inc(xs_in[b], 16)

        def store_v(eng, k, c, i, b):
            eng.wait_ge(low_ready[k], c + 1)
            eng.dma_start(drows_v[k][:, bass.ds(c * PARTS * CHC, PARTS * CHC)],
                          v_st[b][:, :, :, :].rearrange("p a b c -> p (a b c)")).then_inc(v_out[b], 16)

        block = ctx.enter_context(nc.Block())

        @block.sync
        def _(sp):
            for b in range(2):
                load_x(sp, b, b)
            sp.dma_start(*PARAMS[0]).then_inc(wa_in, 16)
            with nc.allow_non_contiguous_dma(reason="columns of parameters and first destinations, once"):
                for to, of in PARAMS[1:]:
                    sp.dma_start(to, of).then_inc(param_in, 16)
                first = dst.rearrange("(g e) -> g e", e=GE)[:, 0:1].rearrange("g a -> a g")
                sp.dma_start(base_i[:, :], first).then_inc(dst_in, 16)

            def store_u(k, c, i, b):
                sp.wait_ge(u_ready, NCH * k + c + 1)
                sp.dma_start(srows_v[k][:, bass.ds(c * CHC, CHC)], u_st[b][:, :]).then_inc(u_out[b], 16)

            def x_chunk(c, i, b):
                if not (isinstance(c, int) and c + 2 >= NCH):
                    sp.wait_ge(xs_T, c + 1)
                    load_x(sp, c + 2, b)
                if not first_chunk(c):
                    store_u(0, *chunk_before(c, i, b))

            for j in range(STEPS):
                sp.dma_start(idx[:, j, :], src_v[0:1, :, j * ST:(j + 1) * ST].rearrange("a p t -> (a p) t"))\
                  .then_inc(idx_in[j], 16)
            over_chunks(sp, x_chunk)
            store_u(0, *LAST)
            sp.wait_ge(const_ready, 1)
            sp.dma_start(proj_w[0][C:C1, 0:2 * C], zeros[0:1, 0:2 * C]).then_inc(zero_w, 16)
            sp.dma_start(proj_w[1][C:C1, 0:C], zeros[0:1, 0:C]).then_inc(zero_w, 16)
            sp.dma_start(relraw.rearrange("p (g t) -> p g t", t=TG), dst_v).then_inc(dst_in, 16)
            for k in range(2):
                sp.dma_start(drows[k][N:NR, :], zeros[:, 0:PARTS * C // 2].bitcast(BF16)).then_inc(zero_in, 16)

            def load_indices(k, i, j):
                sp.dma_start(idx[:, j, :], src_v[bass.ds(i, 1), :, j * ST:(j + 1) * ST].rearrange("a p t -> (a p) t"))\
                  .then_inc(idx_in[j], 16)

            LAG = 2

            def enqueue(i, j, more):
                sp.wait_ge(gathered[j], 16 * ST * (i + 1))
                sp.dma_start(queue[bass.ds(i, 1), :, j * STC:(j + 1) * STC].rearrange("a p n -> (a p) n"), grows[:, j, :])\
                  .then_inc(stored[j], 16)
                if more and j >= LAG:
                    sp.wait_ge(stored[j - LAG], 16 * (i + 1))
                    load_indices(0, i + 1, j - LAG)

            def queue_group(i):
                for j in range(STEPS):
                    enqueue(i, j, True)
                for j in range(STEPS - LAG, STEPS):
                    sp.wait_ge(stored[j], 16 * (i + 1))
                    load_indices(0, i + 1, j)

            with sp.Fori(0, NCH) as i:
                queue_group(i)
                sp.dma_start(x_all[:, bass.ds(i * CHC, CHC)], x_v[:, bass.ds(i * CHC, CHC)]).then_inc(xall_in, 16)
                for k in range(2):
                    n = CH * WIDTH[k]
                    sp.dma_start(sums_v[k][:, bass.ds(i * n, n)], zeros[0:NP, 0:n]).then_inc(L[k].sums_out, 16)
            for k in range(2):
                sp.dma_start(sums[k][N:NR, :], zeros[:, 0:WIDTH[k]]).then_inc(L[k].sums_out, 16)
            with sp.Fori(NCH, G - 1) as i:
                queue_group(i)
            for j in range(STEPS):
                enqueue(G - 1, j, False)

            def load_sums(c, b):
                sp.dma_start(s_ch[b][:, :, :].rearrange("p a b -> p (a b)"), sums_v[0][:, bass.ds(c * CH * C1, CH * C1)])\
                  .then_inc(s_in[b], 16)

            def next_sums(c, i, b):
                if not (isinstance(c, int) and c + 2 >= NCH):
                    sp.wait_ge(y_ready, c + 1)
                    load_sums(c + 2, b)

            def store_h1(c, i, b):
                sp.wait_ge(norm_done, c + 1)
                sp.dma_start(h1_v[:, bass.ds(c * CHC, CHC)], xs[b][:, :]).then_inc(h1_out[b], 16)

            def middle_chunk(*at):
                lagging(next_sums, 0, *at)
                lagging(lambda *a: store_u(1, *a), 2, *at)
                lagging(store_h1, 0, *at)
                lagging(lambda *a: store_v(sp, 1, *a), 3, *at)

            sp.wait_ge(L0.sums_out, 16 * (N_ZEROS + G))
            for b in range(2):
                load_sums(b, b)
            over_chunks(sp, middle_chunk, 3)

            def first_of(i):
                return sp.value_load(dst[bass.ds(i * GE, 1)].unsqueeze(0), min_val=0, max_val=N - 1)

            def load_window(first):
                sp.dma_start(win_ld[:, :], drows[1][bass.ds(first, P), :]).then_inc(L1.win_in, 16)

            def load_factors(i, j):
                sp.dma_start(pre[:, j, :], factors_v[bass.ds(i, 1), :, j * STC:(j + 1) * STC].rearrange("a p n -> (a p) n"))\
                  .then_inc(factors_in[j], 16)

            def store_sums(i):
                first = first_of(i)
                sp.wait_ge(L1.seg_out, i + 2)
                sp.wait_ge(L1.sums_out, 16 * (N_ZEROS + i))
                sp.dma_start(sums[1][bass.ds(first, P), :], seg_sb[:, 0:C]).then_inc(L1.sums_out, 16)

            for j in range(STEPS):
                load_indices(1, 0, j)
                load_factors(0, j)
            first = first_of(0)
            for b in range(2):
                sp.wait_ge(v_out[b], 16 * NCH)
            sp.wait_ge(zero_in, 32)
            load_window(first)
            def refill(i, store):
                first = first_of(i)
                sp.wait_ge(L1.win_ready, i)
                load_window(first)
                for j in range(STEPS):
                    sp.wait_ge(L1.rows_used, ONE + STEPS * (i - 1) + j + 1)
                    load_indices(1, i, j)
                    if j:
                        sp.wait_ge(P_out, ONE + STEPS * (i - 1) + j)
                        load_factors(i, j - 1)
                    if j == 3 and store:
                        store_sums(i - 2)
                sp.wait_ge(P_out, ONE + STEPS * i)
                load_factors(i, STEPS - 1)

            refill(1, False)
            with sp.Fori(2, G) as i:
                refill(i, True)
            first = first_of(0)
            sp.wait_ge(L1.win_ready, G)
            load_window(first)
            store_sums(G - 2)
            store_sums(G - 1)

            def load_m(c, b):
                sp.dma_start(xs[b][:, :], sums_v[1][:, bass.ds(c * CHC, CHC)]).then_inc(m_in[b], 16)

            def load_h1(c, b):
                sp.dma_start(y_ch[b][:, :], h1_v[:, bass.ds(c * CHC, CHC)]).then_inc(h1_in[b], 16)

            def store_out(c, i, b):
                sp.wait_ge(norm_done, NCH + c + 1)
                sp.dma_start(out_v[:, bass.ds(c * CHC, CHC)], u_st[b][:, :]).then_inc(o_out[b], 16)

            def next_m(c, i, b):
                if not (isinstance(c, int) and c + 2 >= NCH):
                    sp.wait_ge(f_T, c + 1)
                    load_m(c + 2, b)

            def finish_chunk(c, i, b):
                store_out(c, i, b)
                if not (isinstance(c, int) and c + 2 >= NCH):
                    load_h1(c + 2, b)

            def last_chunk(*at):
                lagging(next_m, 0, *at)
                lagging(finish_chunk, 2, *at)

            for b in range(2):
                sp.wait_ge(h1_out[b], 16 * (NCH // 2))
                load_h1(b, b)
            sp.wait_ge(L1.sums_out, 16 * (N_ZEROS + G))
            for b in range(2):
                load_m(b, b)
            over_chunks(sp, last_chunk, 2)
            for b in range(2):
                sp.wait_ge(o_out[b], 16 * (NCH // 2))

        @block.gpsimd
        def _(pool):
            pool.memset(zeros[:, :], 0.0).then_inc(const_ready, 1)
            pool.memset(ones[:, :], 1.0).then_inc(const_ready, 1)
            pool.iota(iota_i[:, :], pattern=[[1, P]], base=0, channel_multiplier=0).then_inc(const_ready, 1)
            pool.iota(iotap_i[:, :], pattern=[[0, 1]], base=0, channel_multiplier=1).then_inc(const_ready, 1)
            pool.memset(ident[:, :], 0.0).then_inc(const_ready, 1)
            pool.memset(part_mask[:, :, :, :], 1.0).then_inc(const_ready, 1)
            pool.memset(hm[:, :, :, C:C1], 1.0).then_inc(const_ready, 1)
            pool.memset(rel[:, G * TG:], 0.0).then_inc(const_ready, 1)
            pool.memset(ce_lhs[:, :], 0.0).then_inc(const_ready, 1)
            pool.wait_ge(const_ready, N_CONST)
            pool.affine_select(out=ident[:, :], in_=ident[:, :], compare_op=ALU.not_equal, fill=1.0, base=0,
                               pattern=[[-1, P]], channel_multiplier=1).then_inc(const_ready, 1)
            row_of = [[RT, TR], [KE, PARTS], [PARTS * KE, PARTS]]
            pool.affine_select(out=part_mask[:, :, :, :], in_=part_mask[:, :, :, :], compare_op=ALU.is_ge, fill=0.0, base=0,
                               pattern=[[-s, n] for s, n in row_of], channel_multiplier=1).then_inc(const_ready, 1)
            pool.wait_ge(const_ready, N_CONST + 2)
            pool.affine_select(out=part_mask[:, :, :, :], in_=part_mask[:, :, :, :], compare_op=ALU.is_ge, fill=0.0,
                               base=KE - 1, pattern=row_of, channel_multiplier=-1).then_inc(const_ready, 1)
            pool.memset(carry[:, :], 0.0).then_inc(const_ready, 1)
            pool.memset(carry_all[:, 0:1], 0.0).then_inc(const_ready, 1)
            pool.wait_ge(const_ready, N_CONSTS)

            for k in range(2):
                for b in range(2):
                    pool.wait_ge(u_out[b], 16 * (NCH // 2) * (k + 1))
                with pool.Fori(0, G) as i:
                    pool.wait_ge(idx_in[0], 16 * (k * G + 1) + 16 * i)
                    pool.sem_inc(L[k].turn, 1)
                    for j in range(STEPS):
                        if j:
                            pool.wait_ge(u_out[1], 16 * (NCH // 2) * (k + 1))
                            pool.wait_ge(idx_in[j], 16 * (k * G + 1) + 16 * i)
                        for t in range(ST):
                            pool.indirect_dma_start(
                                out=grows[:, j, t * C:(t + 1) * C], out_offset=None, in_=srows[k],
                                in_offset=bass.IndirectOffsetOnAxis(ap=idx[:, j, t:t + 1], axis=0)).then_inc(gathered[j], 16)

        @block.tensor
        def _(pe):
            def in_bank(bank, t, rows_=C, width=P):
                return flat[0:rows_, bank * BANK + t * P:bank * BANK + t * P + width]

            pe.wait_ge(const_ready, N_CONSTS)
            pe.wait_ge(wa_in, 16)
            pe.wait_ge(bias_rows, 1)

            def transpose_chunk(r, c, i, b):
                if r < 2:
                    pe.wait_ge(xs_in[b], 16 * (NCH // 2 * r + 1) + 16 * i)
                else:
                    pe.wait_ge(norm_done, c + 1)
                after(pe, xT_ready, NCH * r + c)
                for j in range(CH):
                    last = nc.tensor.transpose(in_bank(0, j, C, NP), xs[b][:, j * C:(j + 1) * C], ident[0:NP, 0:NP])
                last.then_inc(xs_T, 1)

            def project_chunk(r, c, i, b):
                k = r // 2
                pe.wait_ge(xT_ready, NCH * r + c + 1)
                if r != 1:
                    after(pe, u_ready, NCH * k + c - 1)
                if r > 0:
                    after(pe, r1_ready[k], c - 1)
                    after(pe, vh_ready[k], c - 1)
                rows_ = C if r == 0 else C1
                for j in range(CH):
                    for m in ((0,), (1, 2), (0, 1, 2))[r]:
                        last = nc.tensor.matmul(ps[0:NP, 2 + 3 * b + m, j * C:(j + 1) * C], xT[b][0:rows_, j * NP:(j + 1) * NP],
                                                proj_w[k][0:rows_, m * C:(m + 1) * C], start=True, stop=True)
                last.then_inc(proj_done, 1)

            def project(r):
                def body(c, i, b):
                    if r == 2 and not first_chunk(c):
                        project_chunk(r, *chunk_before(c, i, b))
                    transpose_chunk(r, c, i, b)
                    if r < 2 and not first_chunk(c):
                        project_chunk(r, *chunk_before(c, i, b))
                over_chunks(pe, body)
                project_chunk(r, *LAST)

            project(0)
            pe.wait_ge(base_cast, 1)
            pe.wait_ge(u_ready, NCH)
            nc.tensor.matmul(ps[:, 7, 0:G], ones[0:1, 0:P], base_f[:, :], start=True, stop=True).then_inc(base_bc, 1)
            pe.wait_ge(param_in, 16 * (len(PARAMS) - 1))
            pe.wait_ge(zero_w, 32)
            pe.wait_ge(rel_ready, 1)
            project(1)

            def sum_partitions(nth, n):
                pe.wait_ge(sums_wanted, nth)
                for m in range(2):
                    last = nc.tensor.matmul(ps[0:C, 7, m:m + 1], part_sums[0:n, m, :], ones[0:n, 0:1], start=True, stop=True)
                last.then_inc(node_sums, 1)

            sum_partitions(1, NP)

            def spread_rows():
                for m in range(2):
                    last = nc.tensor.matmul(ps[0:NP, 7, m * C:(m + 1) * C], ones[0:C, 0:NP], diag[:, m, :], start=True, stop=True)
                last.then_inc(rows_spread, 1)

            pe.wait_ge(diag_ready, 1)
            spread_rows()

            def attributes_T(m):
                pe.wait_ge(ea_split, m + 1)
                flat_ea = ea9[:, :, :, :, :].rearrange("p t a b k -> p (t a b k)")
                for q in range(NB):
                    width = min(RB, (TG - q * TR) * RT)
                    last = nc.tensor.transpose(flat_b[0:width, q * P:(q + 1) * P], flat_ea[:, q * RB:q * RB + width], ident_b[:, :])
                last.then_inc(eaT_done, 1)

            def edge_hidden(j, bank, b):
                for t in range(ST):
                    q, r = divmod(j * ST + t, TR)
                    rows_ = min(RB, (TG - q * TR) * RT)
                    last = nc.tensor.matmul(in_bank(bank, t), we_blk[0:rows_, r, :], eaT[0:rows_, b, q * P:(q + 1) * P],
                                            start=True, stop=True)
                return last

            pe.wait_ge(we_ready, 1)
            pe.wait_ge(identb_ready, 1)
            attributes_T(0)

            def statistics_group(m, b):
                pe.wait_ge(eaT_sb, m + 1)
                for j in range(STEPS):
                    pe.wait_ge(a_relu, A0 + STEPS * m + j - 1)
                    edge_hidden(j, 2 + 2 * ((b + j) % 2), b).then_inc(a_he, 1)
                    if j == 2:
                        attributes_T(m + 1)

            over_pairs(pe, statistics_group, G // 2)
            statistics_group(G - 1, 0)

            pe.wait_ge(ce_ready, 1)
            nc.tensor.matmul(ps[0:C1, 7, 0:C], ce_lhs[:, :], wc[:, :], start=True, stop=True).then_inc(ce_done, 1)

            def onehot_T(s, n, j, bank):
                pe.wait_ge(s.onehot_ready, n + 1)
                after(pe, s.T_copied, n)
                high = onehot[:, j, :].bitcast(BF16).rearrange("p (n h) -> p n h", h=2)[:, :, 1]
                for t in range(ST):
                    at = 2 * bank * BANK + t * P
                    last = nc.tensor.transpose(flat_b[:, at:at + P], high[:, t * P:(t + 1) * P], ident_b[:, :])
                last.then_inc(s.T_done, 1)

            def sum_step(s, k, j):
                if j == 0:
                    nc.tensor.matmul(ps[:, 6, 0:WIDTH[k]], carry[:, :], seg_sb[:, 0:WIDTH[k]], start=True, stop=False)
                for t in range(ST):
                    last = nc.tensor.matmul(ps[:, 6, 0:WIDTH[k]], onehot[:, j, t * P:(t + 1) * P], hm[:, j, t, 0:WIDTH[k]],
                                            start=False, stop=(j == STEPS - 1 and t == ST - 1))
                last.then_inc(s.onehot_used, 1)

            s = L0

            def H0(n, j):
                after(pe, s.H_relu, n)
                edge_hidden(j, 4, LB).then_inc(H_done, 1)

            def P0(n, j):
                pe.wait_ge(s.H_relu, n + 1)
                pe.wait_ge(s.T_copied, n + 1)
                pe.wait_ge(s.rows_used, ONE + n if j == 0 else ONE + n - 1)
                for t in range(ST):
                    nc.tensor.matmul(ps[:, 2 + j % 2, t * C:(t + 1) * C], heT[:, j, t * P:(t + 1) * P], wc1[:, :],
                                     start=(t == 0), stop=False)
                for t in range(ST):
                    for m in range(PARTS):
                        last = nc.tensor.matmul(ps[:, 2 + j % 2, t * C:(t + 1) * C], onehotT[:, j, t * P:(t + 1) * P],
                                                win[:, m * C:(m + 1) * C], start=False,
                                                stop=(t == ST - 1 and m == PARTS - 1))
                last.then_inc(s.P_done, 1)

            def S0(n, j):
                pe.wait_ge(h_ready, n + 1)
                sum_step(s, 0, j)

            pe.sem_inc(s.onehot_used, STEPS)
            pe.wait_ge(wc1_ready, 1)
            pe.wait_ge(eaT_sb, G + 1)
            onehot_T(s, 0, 0, 7)
            H0(0, 0)

            def layer0_group(i, first, last):
                for j in range(STEPS):
                    n = STEPS * i + j
                    onehot_T(s, n + 1, (j + 1) % STEPS, 7)
                    if j == STEPS - 1:
                        pe.wait_ge(eaT_sb, G + i + 2)
                    H0(n + 1, (j + 1) % STEPS)
                    if j == 0:
                        pe.wait_ge(s.win_ready, i + 1)
                    P0(n, j)
                    if j == 1:
                        pe.wait_ge(s.seg_out, i + 1)
                    if not (first and j == 0):
                        m, _, slot = step_before(i, j)
                        S0(m, slot)
                    if j == STEPS - 3:
                        attributes_T(G + i + 1)

            over_groups(pe, layer0_group)
            S0(STEPS * G - 1, STEPS - 1)

            sum_partitions(2, P)
            pe.wait_ge(diag_ready, 2)
            spread_rows()
            pe.wait_ge(rows_read, 2)
            project(2)

            s = L1

            def X1(n, i, j):
                pe.wait_ge(s.T_copied, n + 1)
                pe.wait_ge(s.H_relu, ONE + n if j == 0 else ONE + n - 1)
                pe.wait_ge(gathered[j], 16 * ST * (G + 1) + 16 * ST * i)
                for t in range(ST):
                    o = in_bank(2 + 2 * (j % 2), t)
                    for m in range(PARTS):
                        nc.tensor.matmul(o, win[:, m * C:(m + 1) * C], onehotT[:, j, t * P:(t + 1) * P],
                                         start=(m == 0), stop=False)
                    last = nc.tensor.matmul(o, grows[:, j, t * C:(t + 1) * C], ident[:, :], start=False, stop=True)
                last.then_inc(s.rows_used, 1)

            def E1(n, j):
                pe.wait_ge(s.H_relu, ONE + n + 1)
                pe.wait_ge(P_out, ONE + n)
                for t in range(ST):
                    last = nc.tensor.matmul(ps[:, 7, t * C:(t + 1) * C], heT[:, j, t * P:(t + 1) * P], wm2[:, :],
                                            start=True, stop=True)
                last.then_inc(s.P_done, 1)

            def S1(n, j):
                pe.wait_ge(P_out, ONE + n + 1)
                sum_step(s, 1, j)

            pe.sem_inc(s.onehot_used, STEPS)
            pe.sem_inc(s.rows_used, ONE)
            pe.wait_ge(low_ready[1], NCH)
            pe.wait_ge(vh_ready[1], NCH)
            onehot_T(s, 0, 0, 0)

            def layer1_group(i, first, last):
                for j in range(STEPS):
                    n = STEPS * i + j
                    onehot_T(s, n + 1, (j + 1) % STEPS, 0)
                    if j == 0:
                        pe.wait_ge(s.win_ready, i + 1)
                    X1(n, i, j)
                    if not (first and j == 0):
                        m, _, slot = step_before(i, j)
                        E1(m, slot)
                    if j == 2:
                        pe.wait_ge(s.seg_out, i + 1)
                    if not (first and j < 2):
                        m, _, slot = step_before(i, j, 2)
                        S1(m, slot)

            over_groups(pe, layer1_group)
            n = STEPS * G - 1
            E1(n, STEPS - 1)
            S1(n - 1, STEPS - 2)
            S1(n, STEPS - 1)

            pe.wait_ge(s.T_copied, STEPS * G + 1)
            pe.wait_ge(s.seg_out, G + 1)

            def sums_T(c, i, b):
                pe.wait_ge(m_in[b], 16 * (i + 1))
                after(pe, f_mT, c)
                for j in range(CH):
                    last = nc.tensor.transpose(in_bank(0, j, C, NP), xs[b][:, j * C:(j + 1) * C], ident[0:NP, 0:NP])
                last.then_inc(f_T, 1)

            def hidden_T(c, i, b):
                pe.wait_ge(f_zr, c + 1)
                after(pe, f_zT_sb, c)
                for j in range(CH):
                    last = nc.tensor.transpose(in_bank(2, j, C, NP), r1[b][:, j * C:(j + 1) * C], ident[0:NP, 0:NP])
                last.then_inc(f_zT, 1)

            def hidden(c, i, b):
                pe.wait_ge(f_mT, c + 1)
                after(pe, f_zr, c - 1)
                for j in range(CH):
                    last = nc.tensor.matmul(ps[0:NP, 4 + 2 * b, j * C:(j + 1) * C], xT[b][0:C, j * NP:(j + 1) * NP], wu1b[:, :],
                                            start=True, stop=True)
                last.then_inc(f_z, 1)

            def update(c, i, b):
                pe.wait_ge(f_zT_sb, c + 1)
                after(pe, f_y, c - 1)
                for j in range(CH):
                    last = nc.tensor.matmul(ps[0:NP, 5 + 2 * b, j * C:(j + 1) * C], xT[b][:, j * NP:(j + 1) * NP], wu2[:, :],
                                            start=True, stop=True)
                last.then_inc(f_o, 1)

            def end_chunk(c, i, b):
                sums_T(c, i, b)
                if not first_chunk(c):
                    hidden_T(*chunk_before(c, i, b))
                hidden(c, i, b)
                if not first_chunk(c):
                    update(*chunk_before(c, i, b))

            over_chunks(pe, end_chunk)
            hidden_T(*LAST)
            update(*LAST)

        @block.scalar
        def _(act):
            def of_nodes(b):
                return xT[b][0:C, :].rearrange("p (j n) -> p j n", j=CH)

            def from_bank(bank):
                return flat[0:C, bank * BANK:bank * BANK + CH * P].rearrange("p (j n) -> p j n", j=CH)[:, :, 0:NP]

            act.sem_inc(a_relu, A0)
            act.sem_inc(L1.H_relu, ONE)
            def copy_T(r, c, b):
                act.wait_ge(xs_T, NCH * r + c + 1)
                nc.scalar.copy(of_nodes(b), from_bank(0)).then_inc(xT_ready, 1)

            def unload_u(k, b):
                nc.scalar.copy(u_st[b][:, :], ps[0:NP, 2 + 3 * b, 0:CHC]).then_inc(u_ready, 1)

            def unload_vh(k, c, i, b):
                nc.scalar.copy(v_st[b][:, :, 0, :], ps[0:NP, 3 + 3 * b, 0:CHC].rearrange("p (a b) -> p a b", b=C))
                third = h_all[:, bass.ds(c * CHC, CHC)]
                if k == 0:
                    nc.scalar.activation(third, ps[0:NP, 4 + 3 * b, 0:CHC], ACT.Relu).then_inc(vh_ready[k], 1)
                else:
                    nc.scalar.copy(third, ps[0:NP, 4 + 3 * b, 0:CHC]).then_inc(vh_ready[k], 1)

            def middle_part(k, c, i, b):
                if k == 0:
                    act.wait_ge(vh_ready[k], c + 1)
                act.wait_ge(r1_ready[k], c + 1)
                nc.scalar.copy(v_st[b][:, :, 1, :], r1[b][:, :].rearrange("p (a b) -> p a b", b=C)).then_inc(mid_ready[k], 1)
                if k == 0:
                    nc.scalar.activation(h_sq[b], h_all[:, bass.ds(c * CHC, CHC)], ACT.Square).then_inc(squared, 1)

            def unload_chunk(r, c, i, b):
                act.wait_ge(proj_done, NCH * r + c + 1)
                if r == 0:
                    after(act, u_out[b], 16 * i)
                    unload_u(0, b)
                elif r == 1:
                    after(act, v_out[b], 16 * i)
                    unload_vh(0, c, i, b)
                    middle_part(0, c, i, b)
                else:
                    act.wait_ge(u_out[b], 16 * (NCH // 2) + 16 * i)
                    act.wait_ge(v_out[b], 16 * (NCH // 2) + 16 * i)
                    unload_u(1, b)
                    unload_vh(1, c, i, b)

            for r in range(2):
                def x_chunk(c, i, b):
                    copy_T(r, c, b)
                    if r == 1 and not (isinstance(c, int) and c + 2 >= NCH):
                        load_x(act, c + 2, b)
                    if not first_chunk(c):
                        before = chunk_before(c, i, b)
                        unload_chunk(r, *before)
                        if r == 1:
                            store_v(act, 0, *before)

                if r == 1:
                    for b in range(2):
                        load_x(act, b, b)
                over_chunks(act, x_chunk)
                unload_chunk(r, *LAST)
                if r == 1:
                    store_v(act, 0, *LAST)
                if r == 0:
                    act.wait_ge(dst_in, 32)
                    nc.scalar.copy(base_f[:, :], base_i[:, :]).then_inc(base_cast, 1)
                    nc.scalar.copy(rel[:, 0:G * TG], relraw).then_inc(base_cast, 1)
                    act.wait_ge(const_ready, N_CONSTS)
                    nc.scalar.copy(ident_b[:, :], ident[:, :]).then_inc(identb_ready, 1)

            def coefficient_root(n):
                act.wait_ge(root_wanted, n)
                nc.scalar.activation(stat[:, ROOT:ROOT + 1], stat[:, VAR:VAR + 1], ACT.Sqrt).then_inc(root_ready, 1)

            def load_attributes(i):
                act.dma_start(eas[:, :, :].rearrange("p t k -> p (t k)"), edge4_v[bass.ds(i, 1), :, :].rearrange("a p n -> (a p) n"))\
                   .then_inc(ea_in, 16)

            def copy_attributes_T(m, b):
                act.wait_ge(eaT_done, m + 1)
                whole = (NB - 1) * P
                nc.scalar.copy(eaT[:, b, 0:whole], flat_b[0:RB, 0:whole])
                rest = (TG - (NB - 1) * TR) * RT
                nc.scalar.copy(eaT[0:rest, b, whole:], flat_b[0:rest, whole:whole + P]).then_inc(eaT_sb, 1)

            def hidden_relu(j, bank):
                return nc.scalar.activation(heT[0:C, j, :], flat[0:C, bank * BANK:bank * BANK + ST * P], ACT.Relu,
                                            bias=cols[:, BE:BE + 1])

            load_attributes(0)
            coefficient_root(1)
            act.wait_ge(ea_split, 1)
            load_attributes(1)
            copy_attributes_T(0, 0)

            def statistics_group(m, b, next_group):
                for j in range(STEPS):
                    n = STEPS * m + j
                    act.wait_ge(a_he, n + 1)
                    act.wait_ge(a_bn, n + 1)
                    hidden_relu(j, 2 + 2 * ((b + j) % 2)).then_inc(a_relu, 1)
                    if j == 1 and next_group is not None:
                        act.wait_ge(ea_split, m + 2)
                        load_attributes(next_group)
                    if j == 2:
                        copy_attributes_T(m + 1, 1 - b)

            over_pairs(act, lambda m, b: statistics_group(m, b, m + 2), G // 2 - 1)
            statistics_group(G - 3, 0, G - 1)
            statistics_group(G - 2, 1, 0)
            statistics_group(G - 1, 0, None)
            coefficient_root(2)

            def copy_onehot_T(s, n, j, bank):
                act.wait_ge(s.T_done, n + 1)
                nc.scalar.copy(onehotT[:, j, :], flat_b[:, 2 * bank * BANK:2 * bank * BANK + ST * P]).then_inc(s.T_copied, 1)

            s = L0

            def first_of(i):
                return act.value_load(dst[bass.ds(i * GE, 1)].unsqueeze(0), min_val=0, max_val=N - 1)

            def load_window(first):
                act.dma_start(win_ld[:, :], drows[0][bass.ds(first, P), :]).then_inc(s.win_in, 16)

            def dequeue(i, j):
                act.wait_ge(stored[j], 16 * (i + 1))
                act.dma_start(pre[:, j, :], queue[bass.ds(i, 1), :, j * STC:(j + 1) * STC].rearrange("a p n -> (a p) n"))\
                   .then_inc(rows_in[j], 16)

            def HE(n, j):
                act.wait_ge(H_done, n + 1)
                hidden_relu(j, 4).then_inc(s.H_relu, 1)

            def store_sums(i):
                first = first_of(i)
                act.wait_ge(s.sums_out, 16 * (N_ZEROS + i))
                act.wait_ge(s.seg_out, i + 2)
                act.dma_start(sums[0][bass.ds(first, P), :], seg_sb[:, :]).then_inc(s.sums_out, 16)

            first = first_of(0)
            for b in range(2):
                act.wait_ge(v_out[b], 16 * (NCH // 2))
            act.wait_ge(zero_in, 32)
            load_window(first)
            act.wait_ge(chunk_summed, NCH)
            AHEAD = 3
            for j in range(AHEAD):
                dequeue(0, j)
            copy_onehot_T(s, 0, 0, 7)
            HE(0, 0)

            def message_relu(n, j):
                act.wait_ge(s.rows_used, ONE + n + 1)
                nc.scalar.activation(hm[:, j, :, 0:C], pre[:, j, :].rearrange("p (a b) -> p a b", b=C), ACT.Relu)\
                  .then_inc(h_ready, 1)

            def message_square(n, j):
                act.wait_ge(h_ready, n + 1)
                nc.scalar.activation(pre[:, j, :].rearrange("p (a b) -> p a b", b=C), hm[:, j, :, 0:C], ACT.Square)\
                  .then_inc(msg_squared, 1)

            def layer0_group(i, first, last):
                act.wait_ge(ea_split, G + i + 1)
                load_attributes(0 if last else i + 1)
                start = first_of(0 if last else i + 1)
                act.wait_ge(s.win_ready, i + 1)
                load_window(start)
                for j in range(STEPS):
                    n = STEPS * i + j
                    m, _, slot = step_before(i, j)
                    before = not (first and j == 0)
                    if before:
                        message_relu(m, slot)
                    copy_onehot_T(s, n + 1, (j + 1) % STEPS, 7)
                    HE(n + 1, (j + 1) % STEPS)
                    if before:
                        message_square(m, slot)
                    if j == STEPS - 2:
                        copy_attributes_T(G + i + 1, LB)
                    if not (last and j + AHEAD >= STEPS):
                        after(act, msg_added, n - 1)
                        dequeue(i + (j + AHEAD) // STEPS, (j + AHEAD) % STEPS)
                    if j == 2 and not first:
                        store_sums(i - 1)

            over_groups(act, layer0_group)
            message_relu(STEPS * G - 1, STEPS - 1)
            message_square(STEPS * G - 1, STEPS - 1)
            store_sums(G - 1)
            coefficient_root(3)

            def take_root(k, c, b):
                act.wait_ge(norm_eps, NCH * k + c + 1)
                nc.scalar.activation(ln_rs[b][:, :], ln_mv[b][:, :, 1], ACT.Sqrt).then_inc(norm_root, 1)

            def norm_apply(k, c, i, b, to, stored):
                after(act, stored[b], 16 * i)
                act.wait_ge(norm_scaled, NCH * k + c + 1)
                for j in range(CH):
                    last = nc.scalar.activation(to[b][:, j * C:(j + 1) * C], y_ch[b][:, j * C:(j + 1) * C], ACT.Identity,
                                                bias=ln_nb[b][:, j:j + 1], scale=ln_rs[b][:, j:j + 1])
                last.then_inc(norm_done, 1)

            def middle_chunk(*at):
                lagging(lambda c, i, b: take_root(0, c, b), 0, *at)
                lagging(lambda c, i, b: copy_T(2, c, b), 1, *at)
                lagging(lambda *a: unload_chunk(2, *a), 2, *at)
                lagging(lambda *a: norm_apply(0, *a, xs, h1_out), 0, *at)
                lagging(lambda *a: middle_part(1, *a), 2, *at)

            over_chunks(act, middle_chunk, 2)

            s = L1
            copy_onehot_T(s, 0, 0, 0)
            with act.Fori(0, G) as i:
                for j in range(STEPS):
                    n = STEPS * i + j
                    copy_onehot_T(s, n + 1, (j + 1) % STEPS, 0)
                    act.wait_ge(s.rows_used, ONE + n + 1)
                    at = (2 + 2 * (j % 2)) * BANK
                    nc.scalar.activation(heT[0:C, j, :], flat[0:C, at:at + ST * P], ACT.Relu).then_inc(s.H_relu, 1)

            def copy_sums_T(c, i, b):
                act.wait_ge(f_T, c + 1)
                nc.scalar.copy(of_nodes(b), from_bank(0)).then_inc(f_mT, 1)

            def copy_hidden_T(c, i, b):
                act.wait_ge(f_zT, c + 1)
                nc.scalar.copy(of_nodes(b), from_bank(2)).then_inc(f_zT_sb, 1)

            def end_chunk(*at):
                lagging(copy_sums_T, 0, *at)
                lagging(lambda c, i, b: take_root(1, c, b), 2, *at)
                lagging(copy_hidden_T, 1, *at)
                lagging(lambda *a: norm_apply(1, *a, u_st, o_out), 2, *at)

            over_chunks(act, end_chunk, 2)

        @block.vector
        def _(dve):
            chain = [0]

            def link(ins):
                chain[0] += 1
                ins.then_inc(link_v, 1)
                dve.wait_ge(link_v, chain[0])

            def step(ins, s, value):
                ins.then_inc(s, 1)
                dve.wait_ge(s, value)

            dve.sem_inc(a_bn, STEPS)
            dve.sem_inc(L0.rows_used, ONE)
            dve.sem_inc(P_out, ONE)

            for b in range(2):
                nc.vector.memset(xT[b][C:C1, :], 1.0)
            nc.vector.memset(heT[C:C1, :, :], 1.0).then_inc(bias_rows, 1)

            def col(i):
                return stat[:, i:i + 1]

            dve.wait_ge(const_ready, N_CONSTS)
            nc.vector.tensor_copy(iota[:, :], iota_i[:, :])
            nc.vector.tensor_copy(iotap[:, :], iotap_i[:, :])
            dve.wait_ge(base_bc, 1)
            link(nc.vector.tensor_copy(base_all[:, :], ps[:, 7, 0:G]))
            dve.wait_ge(base_cast, 2)
            r3 = rel[:, 0:G * TG].rearrange("p (g t) -> p g t", t=TG)
            nc.vector.tensor_tensor(r3, r3, base_all[:, :].unsqueeze(2).to_broadcast([P, G, TG]), ALU.subtract).then_inc(rel_ready, 1)
            link(nc.vector.tensor_tensor(carry_all[:, 1:G], base_all[:, 1:G], base_all[:, 0:G - 1], ALU.subtract))
            nc.vector.memset(carry_all[:, G:G + 1], 0.0)
            link(nc.vector.tensor_scalar(carry_all[:, 1:G], carry_all[:, 1:G], iotap[:, :], None, ALU.is_equal))
            nc.vector.tensor_scalar(kept_all[:, :], carry_all[:, 1:G + 1], -1.0, 1.0, ALU.mult, ALU.add)

            dve.wait_ge(param_in, 16 * (len(PARAMS) - 1))
            link(nc.vector.reduce_sum(pm[:, :, :].rearrange("p r b -> p (r b)"),
                                      part_mask[:, :, :, :].rearrange("p r b a -> p (r b) a"), AX.X))
            link(nc.vector.tensor_copy(we_b[:, 0, :], we_rep[:, :]))
            link(nc.vector.tensor_tensor(we_r[:, :], we_rep[:, :], we_b[:, 0, :], ALU.subtract))
            link(nc.vector.tensor_copy(we_b[:, 1, :], we_r[:, :]))
            link(nc.vector.tensor_tensor(we_b[:, 2, :], we_r[:, :], we_b[:, 1, :], ALU.subtract))
            for r in range(TR):
                link(nc.vector.tensor_scalar(we_acc[:, :], we_b[:, 0, :], pm[:, r, 0:1], None, ALU.mult))
                link(nc.vector.scalar_tensor_tensor(we_acc[:, :], we_b[:, 1, :], pm[:, r, 1:2], we_acc[:, :], ALU.mult, ALU.add))
                link(nc.vector.scalar_tensor_tensor(we_blk[:, r, :], we_b[:, 2, :], pm[:, r, 2:3], we_acc[:, :], ALU.mult, ALU.add))
            nc.vector.memset(acc_sum[:, :], 0.0)
            nc.vector.memset(acc_sq[:, :], 0.0).then_inc(we_ready, 1)

            def rest_of_rows(k, c, i, b):
                dve.wait_ge(vh_ready[k], c + 1)
                nc.vector.tensor_tensor(r1[b][:, :].rearrange("p (a b) -> p a b", b=C),
                                        ps[0:NP, 3 + 3 * b, 0:CHC].rearrange("p (a b) -> p a b", b=C), v_st[b][:, :, 0, :],
                                        ALU.subtract).then_inc(r1_ready[k], 1)

            def low_part(k, c, i, b):
                dve.wait_ge(mid_ready[k], c + 1)
                nc.vector.tensor_tensor(v_st[b][:, :, 2, :], r1[b][:, :].rearrange("p (a b) -> p a b", b=C), v_st[b][:, :, 1, :],
                                        ALU.subtract).then_inc(low_ready[k], 1)

            def x_chunk(c, i, b):
                rest_of_rows(0, c, i, b)
                nc.vector.reduce_sum(hsum[:, bass.ds(c, 1), :].rearrange("p a c -> p (a c)"),
                                     h_all[:, bass.ds(c * CHC, CHC)].rearrange("p (a c) -> p c a", c=C), AX.X)
                low_part(0, c, i, b)
                dve.wait_ge(squared, c + 1)
                nc.vector.reduce_sum(hsqsum[:, bass.ds(c, 1), :].rearrange("p a c -> p (a c)"),
                                     h_sq[b].rearrange("p (a c) -> p c a", c=C), AX.X).then_inc(chunk_summed, 1)

            over_chunks(dve, x_chunk)
            roots = [0]

            def coefficients(gamma, beta):
                nc.vector.tensor_scalar(col(VAR), col(VAR), 0.0, EPS, ALU.max, ALU.add).then_inc(root_wanted, 1)
                roots[0] += 1
                dve.wait_ge(root_ready, roots[0])
                link(nc.vector.reciprocal(col(TMP), col(ROOT)))
                link(nc.vector.tensor_tensor(col(SCALE), col(TMP), cols[:, gamma:gamma + 1], ALU.mult))
                link(nc.vector.tensor_tensor(col(TMP), col(SCALE), col(MEAN), ALU.mult))
                link(nc.vector.tensor_tensor(col(SHIFT), cols[:, beta:beta + 1], col(TMP), ALU.subtract))

            def coefficients_of_sums(total, squares, count, gamma, beta):
                link(nc.vector.tensor_scalar(col(MEAN), total, 1.0 / count, None, ALU.mult))
                link(nc.vector.tensor_scalar(col(VAR), squares, 1.0 / count, None, ALU.mult))
                link(nc.vector.tensor_tensor(col(TMP), col(MEAN), col(MEAN), ALU.mult))
                link(nc.vector.tensor_tensor(col(VAR), col(VAR), col(TMP), ALU.subtract))
                coefficients(gamma, beta)

            def spread(nth):
                nc.vector.tensor_scalar(diag[:, 0, :], ident[0:C, 0:C], col(SCALE), None, ALU.mult)
                nc.vector.tensor_scalar(diag[:, 1, :], ident[0:C, 0:C], col(SHIFT), None, ALU.mult).then_inc(diag_ready, 1)
                dve.wait_ge(rows_spread, nth)
                step(nc.vector.tensor_copy(rows[:, :, :].rearrange("p a b -> p (a b)"), ps[0:NP, 7, 0:2 * C]), rows_read, nth)

            dve.wait_ge(chunk_summed, NCH)
            link(nc.vector.reduce_sum(part_sums[0:NP, 0, :], hsum.rearrange("p n c -> p c n"), AX.X))
            nc.vector.reduce_sum(part_sums[0:NP, 1, :], hsqsum.rearrange("p n c -> p c n"), AX.X).then_inc(sums_wanted, 1)
            dve.wait_ge(node_sums, 1)
            coefficients_of_sums(ps[0:C, 7, 0:1], ps[0:C, 7, 1:2], N, GN, BN)
            spread(1)

            def beside(a):
                return a.unsqueeze(2).to_broadcast([P, TG, PARTS, KE])

            def split_high(m):
                dve.wait_ge(ea_in, 16 * (m + 1))
                after(dve, eaT_done, m)
                step(nc.vector.tensor_copy(ea9[:, :, 0, :, :], beside(eas[:, :, :])), ea_hi, m + 1)
                nc.vector.tensor_tensor(ea_r[:, :, :], eas[:, :, :], ea9[:, :, 0, 0, :], ALU.subtract).then_inc(ea_rest, 1)

            def split_rest(m):
                dve.wait_ge(ea_rest, m + 1)
                step(nc.vector.tensor_copy(ea9[:, :, 1, :, :], beside(ea_r[:, :, :])), ea_mid, m + 1)
                nc.vector.tensor_tensor(ea9[:, :, 2, :, :], beside(ea_r[:, :, :]), ea9[:, :, 1, :, :], ALU.subtract)\
                  .then_inc(ea_split, 1)

            for m in range(2):
                split_high(m)
                split_rest(m)
            half = ST * P // 2

            def aggregate(m, b):
                dve.wait_ge(a_bn, STEPS * (m + 2))
                dve.sem_inc(a_turn, 1)
                step(nc.vector.bn_aggr(mv_group[:, :], bn_edge[:, b, :, :].rearrange("p a b -> p (a b)")), a_mv, 2 * m + 1)
                nc.vector.tensor_copy(mv_edge[:, bass.ds(m, 1), :].rearrange("p a b -> p (a b)"), mv_group[:, :]).then_inc(a_mv, 1)

            def statistics_group(m, b, first=False, last=False):
                for j in range(STEPS):
                    dve.wait_ge(a_relu, A0 + STEPS * m + j + 1)
                    nc.vector.bn_stats(bn_edge[:, b, 2 * j, :], heT[0:C, j, 0:half])
                    nc.vector.bn_stats(bn_edge[:, b, 2 * j + 1, :], heT[0:C, j, half:2 * half]).then_inc(a_bn, 1)
                    if j == 1 and not first:
                        aggregate(m - 1, 1 - b)
                    if j == 3 and not last:
                        split_high(m + 2)
                    if j == 4 and not last:
                        split_rest(m + 2)

            statistics_group(0, 0, True)
            statistics_group(1, 1)
            with dve.Fori(1, G // 2) as q:
                for b in range(2):
                    statistics_group(2 * q + b, b)
            statistics_group(G - 1, 0, last=True)
            aggregate(G - 1, 0)
            dve.wait_ge(a_mv, 2 * G)
            link(nc.vector.reduce_sum(col(MEAN), mv_edge[:, :, 0], AX.X))
            link(nc.vector.reduce_sum(col(TMP), mv_edge[:, :, 1], AX.X))
            link(nc.vector.tensor_scalar(col(MEAN), col(MEAN), 1.0 / G, None, ALU.mult))
            link(nc.vector.tensor_scalar(mv_edge[:, :, 0], mv_edge[:, :, 0], col(MEAN), None, ALU.subtract))
            link(nc.vector.tensor_tensor(mv_edge[:, :, 1], mv_edge[:, :, 0], mv_edge[:, :, 0], ALU.mult))
            link(nc.vector.reduce_sum(col(VAR), mv_edge[:, :, 1], AX.X))
            link(nc.vector.tensor_tensor(col(VAR), col(VAR), col(TMP), ALU.add))
            link(nc.vector.tensor_scalar(col(VAR), col(VAR), 1.0 / G, None, ALU.mult))
            coefficients(GEDGE, BEDGE)
            link(nc.vector.tensor_scalar(wc1[0:C, :], wc[:, :], col(SCALE), None, ALU.mult))
            nc.vector.tensor_copy(ce_lhs[:, C:C1], col(SHIFT)).then_inc(ce_ready, 1)
            dve.wait_ge(ce_done, 1)
            nc.vector.tensor_tensor(wc1[C:C1, :], ps[C:C1, 7, 0:C], bmsg_row[C:C1, :], ALU.add).then_inc(wc1_ready, 1)

            def make_onehot(s, n, j):
                dve.wait_ge(s.onehot_used, n + 1)
                nc.vector.tensor_tensor(onehot[:, j, :].rearrange("p (t w) -> p t w", w=P),
                                        iota[:, :].unsqueeze(1).to_broadcast([P, ST, P]),
                                        rel[:, bass.ds(n * ST, ST)].unsqueeze(2).to_broadcast([P, ST, P]),
                                        ALU.is_equal).then_inc(s.onehot_ready, 1)

            def copy_window(s, i):
                dve.wait_ge(s.win_in, 16 * (i + 1))
                nc.vector.tensor_copy(win[:, :], win_ld[:, :]).then_inc(s.win_ready, 1)

            def add_features(i):
                xt, ht = x_all[:, bass.ds(i * C, C)], h_all[:, bass.ds(i * C, C)]
                step(nc.vector.tensor_tensor(ht, ht, rows[:, 0, :], ALU.mult), xn_scaled, i + 1)
                step(nc.vector.tensor_tensor(xt, xt, ht, ALU.add), xn_added, i + 1)
                nc.vector.tensor_tensor(xt, xt, rows[:, 1, :], ALU.add).then_inc(xn_done, 1)

            def next_window(s, i):
                if s is L0:
                    dve.wait_ge(s.P_done, STEPS * (i + 1))
                else:
                    dve.wait_ge(s.rows_used, ONE + STEPS * (i + 1))
                copy_window(s, i + 1)

            def take_sums(k, i):
                s = L[k]
                dve.wait_ge(s.onehot_used, STEPS * (i + 2))
                dve.wait_ge(s.sums_out, 16 * (N_ZEROS + i))
                nc.vector.tensor_copy(seg_sb[:, 0:WIDTH[k]], ps[:, 6, 0:WIDTH[k]])
                if k == 0:
                    nc.vector.scalar_tensor_tensor(acc_sum[:, :], ps[:, 6, 0:C1], kept_all[:, bass.ds(i, 1)], acc_sum[:, :],
                                                   ALU.mult, ALU.add)
                nc.vector.tensor_copy(carry[:, 0:1], carry_all[:, bass.ds(i + 1, 1)]).then_inc(s.seg_out, 1)

            def add_squares(n, j):
                dve.wait_ge(msg_squared, n + 1)
                after(dve, msg_added, n)
                nc.vector.tensor_tensor(acc_sq[:, :], acc_sq[:, :], pre[:, j, :], ALU.add).then_inc(msg_added, 1)

            def layer0_group(i, first, features):
                s = L0
                for j in range(STEPS):
                    n = STEPS * i + j
                    make_onehot(s, n + 2, (j + 2) % STEPS)
                    if j == STEPS - 1:
                        next_window(s, i)
                    dve.wait_ge(s.P_done, n + 1)
                    dve.wait_ge(rows_in[j], 16 * (i + 1))
                    nc.vector.tensor_tensor(pre[:, j, :], ps[:, 2 + j % 2, 0:STC], pre[:, j, :], ALU.add).then_inc(s.rows_used, 1)
                    if not (first and j == 0):
                        m, _, slot = step_before(i, j)
                        add_squares(m, slot)
                    if j == 0 and not first:
                        take_sums(0, i - 1)
                    if j == 0:
                        split_high(G + i + 1)
                    if j == 1:
                        split_rest(G + i + 1)
                    if j == 3 and features:
                        add_features(i)

            def scale_messages(n, i, j):
                dve.wait_ge(L1.P_done, n + 1)
                dve.wait_ge(factors_in[j], 16 * (i + 1))
                nc.vector.tensor_tensor(hm[:, j, :, 0:C], ps[:, 7, 0:STC].rearrange("p (a b) -> p a b", b=C),
                                        pre[:, j, :].rearrange("p (a b) -> p a b", b=C), ALU.mult).then_inc(P_out, 1)

            def layer1_group(i, first, last):
                s = L1
                for j in range(STEPS):
                    make_onehot(s, STEPS * i + j + 2, (j + 2) % STEPS)
                    if not (first and j == 0):
                        scale_messages(*step_before(i, j))
                    if j == 1 and not first:
                        take_sums(1, i - 1)
                    if j == STEPS - 1:
                        next_window(s, i)

            def edges(k):
                s = L[k]
                copy_window(s, 0)
                nc.vector.memset(carry[:, 0:1], 0.0)
                nc.vector.memset(seg_sb[:, :], 0.0).then_inc(s.seg_out, 1)
                make_onehot(s, 0, 0)
                make_onehot(s, 1, 1)
                if k == 0:
                    dve.wait_ge(xall_in, 16 * NCH)
                    layer0_group(0, True, True)
                    with dve.Fori(1, NT) as i:
                        layer0_group(i, False, True)
                    with dve.Fori(NT, G) as i:
                        layer0_group(i, False, False)
                    add_squares(STEPS * G - 1, STEPS - 1)
                else:
                    over_groups(dve, layer1_group)
                    scale_messages(STEPS * G - 1, G - 1, STEPS - 1)
                take_sums(k, G - 1)
                dve.wait_ge(s.seg_out, G + 1)

            def norm_stats(k, c, b):
                for j in range(CH):
                    last = nc.vector.bn_stats(ln_bn[b][:, j, :], y_ch[b][:, j * C:(j + 1) * C])
                step(last, norm_bnd, NCH * k + c + 1)
                dve.sem_inc(norm_turn, 1)
                for j in range(CH):
                    last = nc.vector.bn_aggr(ln_mv[b][:, j, :], ln_bn[b][:, j, :])
                step(last, norm_agg, NCH * k + c + 1)
                nc.vector.tensor_scalar(ln_mv[b][:, :, 1], ln_mv[b][:, :, 1], EPS, None, ALU.add).then_inc(norm_eps, 1)

            def norm_scale(k, c, b):
                dve.wait_ge(norm_root, NCH * k + c + 1)
                step(nc.vector.reciprocal(ln_rs[b][:, :], ln_rs[b][:, :]), norm_inv, NCH * k + c + 1)
                nc.vector.scalar_tensor_tensor(ln_nb[b][:, :], ln_mv[b][:, :, 0], -1.0, ln_rs[b][:, :], ALU.mult, ALU.mult)\
                  .then_inc(norm_scaled, 1)

            def message_sums(c, i, b):
                dve.wait_ge(s_in[b], 16 * (i + 1))
                y3 = y_ch[b][:, :].rearrange("p (a b) -> p a b", b=C)
                step(nc.vector.tensor_tensor(y3, s_ch[b][:, :, 0:C], rows[:, 0, :].unsqueeze(1).to_broadcast([NP, CH, C]), ALU.mult),
                     y_scaled, c + 1)
                step(nc.vector.tensor_tensor(y_ch[b][:, :], y_ch[b][:, :], x_all[:, bass.ds(c * CHC, CHC)], ALU.add), y_added, c + 1)
                for j in range(CH):
                    last = nc.vector.scalar_tensor_tensor(y3[:, j, :], rows[:, 1, :], s_ch[b][:, j, C:C1], y3[:, j, :],
                                                          ALU.mult, ALU.add)
                step(last, y_ready, c + 1)

            def middle_chunk(*at):
                lagging(message_sums, 0, *at)
                lagging(lambda *a: low_part(1, *a), 3, *at)
                lagging(lambda c, i, b: norm_stats(0, c, b), 0, *at)
                lagging(lambda *a: rest_of_rows(1, *a), 2, *at)
                lagging(lambda c, i, b: norm_scale(0, c, b), 0, *at)

            def hidden_sum(c, i, b):
                dve.wait_ge(f_z, c + 1)
                nc.vector.tensor_tensor(r1[b][:, :], ps[0:NP, 4 + 2 * b, 0:CHC], h_all[:, bass.ds(c * CHC, CHC)], ALU.add)\
                  .then_inc(z_summed, 1)

            def node_relu(c, i, b):
                dve.wait_ge(z_summed, c + 1)
                nc.vector.tensor_scalar(r1[b][:, :], r1[b][:, :], 0.0, None, ALU.max).then_inc(f_zr, 1)

            def add_h1(c, i, b):
                dve.wait_ge(h1_in[b], 16 * (i + 1))
                dve.wait_ge(f_o, c + 1)
                step(nc.vector.tensor_tensor(y_ch[b][:, :], ps[0:NP, 5 + 2 * b, 0:CHC], y_ch[b][:, :], ALU.add), f_y, c + 1)
                norm_stats(1, c, b)

            def end_chunk(*at):
                lagging(hidden_sum, 0, *at)
                lagging(lambda c, i, b: norm_scale(1, c, b), 2, *at)
                lagging(node_relu, 0, *at)
                lagging(add_h1, 1, *at)

            edges(0)
            dve.wait_ge(msg_added, STEPS * G)
            nc.vector.tensor_copy(part_sums[:, 0, :], acc_sum[:, 0:C])
            nc.vector.reduce_sum(part_sums[:, 1, :], acc_sq[:, :].rearrange("p (a c) -> p c a", c=C), AX.X).then_inc(sums_wanted, 1)
            dve.wait_ge(node_sums, 2)
            coefficients_of_sums(ps[0:C, 7, 0:1], ps[0:C, 7, 1:2], E, GM, BM)
            dve.wait_ge(xn_done, NT)
            spread(2)
            over_chunks(dve, middle_chunk, 3)
            edges(1)
            over_chunks(dve, end_chunk, 2)


_INS = ["x", "src", "dst", "edge_attr_4", "edge_attr_96", "L0_gnn_W_node", "L0_gnn_b_node", "L0_gnn_g_node",
        "L0_gnn_beta_node", "L0_gnn_W_edge", "L0_gnn_b_edge", "L0_gnn_g_edge", "L0_gnn_beta_edge", "L0_gnn_W_msg",
        "L0_gnn_b_msg", "L0_gnn_g_msg", "L0_gnn_beta_msg", "L1_gnn_Wm1", "L1_gnn_bm1", "L1_gnn_Wm2", "L1_gnn_bm2",
        "L1_gnn_Wu1", "L1_gnn_bu1", "L1_gnn_Wu2", "L1_gnn_bu2"]


def kernel(**inputs):
    import numpy as np
    import concourse.bacc as bacc
    from concourse.bass_utils import run_bass_kernel_spmd

    nc = bacc.Bacc("TRN2", target_bir_lowering=False, num_devices=1)
    arrays, args = {}, []
    for name in _INS:
        a = np.ascontiguousarray(inputs[name])
        arrays[f"in_{name}"] = a
        args.append(nc.dram_tensor(f"in_{name}", a.shape, mybir.dt.from_np(a.dtype), kind="ExternalInput").ap())
    out = nc.dram_tensor("out_nodes", inputs["x"].shape, F32, kind="ExternalOutput").ap()
    build_gnn(nc, *args, out)
    r = run_bass_kernel_spmd(nc, [arrays], core_ids=[0])
    return r.results[0]["out_nodes"]
```
